# Optimizing a Trainium2 kernel written in Bass

```python
import numpy as np
import jax
import jax.numpy as jnp

def _softmax(x, axis=-1):
    return jax.nn.softmax(x, axis=axis)

def _gelu(x):
    return jax.nn.gelu(x, approximate=True)

def _silu(x):
    return jax.nn.silu(x)

def _sigmoid(x):
    return jax.nn.sigmoid(x)

def _layernorm(x, axis=-1, eps=1e-05):
    m = jnp.mean(x, axis=axis, keepdims=True)
    v = jnp.var(x, axis=axis, keepdims=True)
    return (x - m) / jnp.sqrt(v + eps)

def _scatter_add(tgt, idx, src, axis=0):
    return tgt.at[idx].add(src)

def _segment_sum(src, seg, n):
    return jax.ops.segment_sum(src, seg, n)
kernel_name = 'mk_macaron_d2_jaxref_r4_ae8806'

def setup_inputs(seed: int=0):
    np.random.seed(seed)
    _w = jnp.asarray

    def _L0_attn_setup():
        import jax, jax.numpy as jnp
        import numpy as np
        DIM = 256
        HEADS = 16
        DIM_HEAD = 64
        SOFTCLAMP = 50.0

        def _rmsnorm(x, w):
            eps = jnp.finfo(x.dtype).eps
            var = jnp.mean(jnp.square(x), axis=-1, keepdims=True)
            return x * jax.lax.rsqrt(var + eps) * w

        def _head_rmsnorm(x, gamma):
            norm = jnp.linalg.norm(x, axis=-1, keepdims=True)
            normed = x / jnp.maximum(norm, 1e-12)
            scale = (gamma + 1.0) * DIM_HEAD ** 0.5
            return normed * scale[None, :, None, :]
        key = jax.random.key(seed)
        ks = jax.random.split(key, 7)
        b, n = (4, 512)
        di = HEADS * DIM_HEAD
        s = 0.02
        return {'tokens': jax.random.normal(ks[0], (b, n, DIM), dtype=jnp.float32), 'norm_w': jnp.ones((DIM,), dtype=jnp.float32), 'Wq': jax.random.normal(ks[1], (DIM, di), dtype=jnp.float32) * s, 'Wkv': jax.random.normal(ks[2], (DIM, 2 * di), dtype=jnp.float32) * s, 'Wo': jax.random.normal(ks[3], (di, DIM), dtype=jnp.float32) * s, 'q_gamma': jnp.zeros((HEADS, DIM_HEAD), dtype=jnp.float32), 'k_gamma': jnp.zeros((HEADS, DIM_HEAD), dtype=jnp.float32)}
    _L0_attn_in = _L0_attn_setup()

    def _L0_ffn_setup():
        import jax, jax.numpy as jnp
        import numpy as np
        CAP_FACTOR = 1.5
        key = jax.random.key(seed)
        ks = jax.random.split(key, 6)
        E, S, D, M = (48, 4, 256, 256)
        K = D // S
        x = jax.random.normal(ks[0], (4, 1024, D), dtype=jnp.float32)
        Wr = jax.random.normal(ks[1], (E, D), dtype=jnp.float32) * 0.02
        W1 = jax.random.normal(ks[2], (E, S, D, M), dtype=jnp.float32) * (1.0 / np.sqrt(D))
        b1 = jnp.zeros((E, S, M), dtype=jnp.float32)
        W2 = jax.random.normal(ks[3], (E, S, M, K), dtype=jnp.float32) * (1.0 / np.sqrt(M))
        b2 = jnp.zeros((E, S, K), dtype=jnp.float32)
        return {'x': x, 'Wr': Wr, 'W1': W1, 'b1': b1, 'W2': W2, 'b2': b2}
    _L0_ffn_in = _L0_ffn_setup()

    def _L1_attn_setup():
        import jax, jax.numpy as jnp
        import numpy as np
        import math
        from jax import lax
        EPS = 1e-06

        def _layernorm(x, scale, bias):
            mu = jnp.mean(x, axis=-1, keepdims=True)
            var = jnp.var(x, axis=-1, keepdims=True)
            return (x - mu) * lax.rsqrt(var + EPS) * scale + bias

        def _rmsnorm(x, scale):
            ms = jnp.mean(x * x, axis=-1, keepdims=True)
            return x * lax.rsqrt(ms + EPS) * scale

        def _apply_rope(x, phi):
            half = x.shape[-1] // 2
            x_r, x_i = (x[..., :half], x[..., half:])
            c, s = (jnp.cos(phi), jnp.sin(phi))
            return jnp.concatenate([x_r * c - x_i * s, x_r * s + x_i * c], axis=-1)

        def _ssd_trapezoidal_scan(x_heads, B_ssm, C_ssm, dt, A, lam):
            a = jnp.exp(A[None, None, :] * dt)
            Bb, L, H, P = x_heads.shape
            N = B_ssm.shape[-1]
            xs = (jnp.moveaxis(x_heads, 1, 0), jnp.moveaxis(B_ssm, 1, 0), jnp.moveaxis(C_ssm, 1, 0), jnp.moveaxis(a, 1, 0), jnp.moveaxis(dt, 1, 0), jnp.moveaxis(lam, 1, 0))
            h0 = jnp.zeros((Bb, H, P, N), x_heads.dtype)

            def step(carry, inp):
                h, prev_Bx = carry
                x_t, B_t, C_t, a_t, dt_t, lam_t = inp
                Bx = jnp.einsum('bhp,bn->bhpn', x_t, B_t)
                ae = a_t[:, :, None, None]
                dte = dt_t[:, :, None, None]
                le = lam_t[:, :, None, None]
                h = ae * h + dte * (le * Bx + (1.0 - le) * ae * prev_Bx)
                y = jnp.einsum('bhpn,bn->bhp', h, C_t)
                return ((h, Bx), y)
            _, ys = lax.scan(step, (h0, jnp.zeros_like(h0)), xs)
            return jnp.moveaxis(ys, 0, 1)
        D_MODEL, D_STATE, N_HEADS, EXPAND = (256, 64, 16, 2)
        D_INNER = D_MODEL * EXPAND
        HEAD_DIM = D_INNER // N_HEADS
        PROJ = D_INNER + D_INNER + D_STATE + D_STATE + N_HEADS + N_HEADS
        key = jax.random.key(seed)
        ks = jax.random.split(key, 6)
        u = jax.random.normal(ks[0], (4, 1024, D_MODEL), dtype=jnp.float32)
        in_proj_w = jax.random.normal(ks[1], (D_MODEL, PROJ), dtype=jnp.float32) * D_MODEL ** (-0.5)
        A_log = jnp.log(jnp.arange(1, N_HEADS + 1, dtype=jnp.float32))
        uu = jax.random.uniform(ks[2], (N_HEADS,), dtype=jnp.float32, minval=math.log(0.001), maxval=math.log(0.1))
        dt_vals = jnp.clip(jnp.exp(uu), 0.0001)
        dt_bias = dt_vals + jnp.log(-jnp.expm1(-dt_vals))
        theta_w = jax.random.normal(ks[3], (D_MODEL, D_STATE // 2), dtype=jnp.float32) * 0.01
        out_proj_w = jax.random.normal(ks[4], (D_INNER, D_MODEL), dtype=jnp.float32) * D_INNER ** (-0.5)
        return {'u': u, 'norm_scale': jnp.ones((D_MODEL,), jnp.float32), 'norm_bias': jnp.zeros((D_MODEL,), jnp.float32), 'in_proj_w': in_proj_w, 'A_log': A_log, 'dt_bias': dt_bias, 'bcB_scale': jnp.ones((D_STATE,), jnp.float32), 'bcC_scale': jnp.ones((D_STATE,), jnp.float32), 'B_bias': jnp.zeros((D_STATE,), jnp.float32), 'C_bias': jnp.zeros((D_STATE,), jnp.float32), 'theta_w': theta_w, 'D': jnp.ones((N_HEADS,), jnp.float32), 'out_proj_w': out_proj_w}
    _L1_attn_in = _L1_attn_setup()

    def _L1_ffn_setup():
        import jax, jax.numpy as jnp
        import numpy as np
        DIM = 256

        def _reference_tuple_inner(x, W_r, W_k, W_v, mu_r, mu_k):
            B, T, C = x.shape
            x_prev = jnp.concatenate([jnp.zeros((B, 1, C), x.dtype), x[:, :-1, :]], axis=1)
            xr = mu_r * x + (1.0 - mu_r) * x_prev
            xk = mu_k * x + (1.0 - mu_k) * x_prev
            r = jax.nn.sigmoid(jnp.einsum('btc,dc->btd', xr, W_r))
            k = jnp.einsum('btc,dc->btd', xk, W_k)
            k_act = jnp.square(jax.nn.relu(k))
            out = r * jnp.einsum('btc,dc->btd', k_act, W_v)
            new_state = x[:, -1, :]
            return (out, new_state)
        key = jax.random.key(seed)
        ks = jax.random.split(key, 6)
        B, T, C = (8, 512, DIM)
        x = jax.random.normal(ks[0], (B, T, C), dtype=jnp.float32)
        s = 1.0 / np.sqrt(C)
        W_r = jax.random.uniform(ks[1], (C, C), jnp.float32, -s, s)
        W_k = jax.random.uniform(ks[2], (C, C), jnp.float32, -s, s)
        W_v = jax.random.uniform(ks[3], (C, C), jnp.float32, -s, s)
        mu_r = jax.random.uniform(ks[4], (C,), jnp.float32)
        mu_k = jax.random.uniform(ks[5], (C,), jnp.float32)
        return {'x': x, 'W_r': W_r, 'W_k': W_k, 'W_v': W_v, 'mu_r': mu_r, 'mu_k': mu_k}
    _L1_ffn_in = _L1_ffn_setup()
    _d = {'L0_attn_tokens': _L0_attn_in['tokens'], 'L0_attn_norm_w': _L0_attn_in['norm_w'], 'L0_attn_Wq': _L0_attn_in['Wq'], 'L0_attn_Wkv': _L0_attn_in['Wkv'], 'L0_attn_Wo': _L0_attn_in['Wo'], 'L0_attn_q_gamma': _L0_attn_in['q_gamma'], 'L0_attn_k_gamma': _L0_attn_in['k_gamma'], 'L0_ffn_Wr': _L0_ffn_in['Wr'], 'L0_ffn_W1': _L0_ffn_in['W1'], 'L0_ffn_b1': _L0_ffn_in['b1'], 'L0_ffn_W2': _L0_ffn_in['W2'], 'L0_ffn_b2': _L0_ffn_in['b2'], 'L1_attn_norm_scale': _L1_attn_in['norm_scale'], 'L1_attn_norm_bias': _L1_attn_in['norm_bias'], 'L1_attn_in_proj_w': _L1_attn_in['in_proj_w'], 'L1_attn_A_log': _L1_attn_in['A_log'], 'L1_attn_dt_bias': _L1_attn_in['dt_bias'], 'L1_attn_bcB_scale': _L1_attn_in['bcB_scale'], 'L1_attn_bcC_scale': _L1_attn_in['bcC_scale'], 'L1_attn_B_bias': _L1_attn_in['B_bias'], 'L1_attn_C_bias': _L1_attn_in['C_bias'], 'L1_attn_theta_w': _L1_attn_in['theta_w'], 'L1_attn_D': _L1_attn_in['D'], 'L1_attn_out_proj_w': _L1_attn_in['out_proj_w'], 'L1_ffn_W_r': _L1_ffn_in['W_r'], 'L1_ffn_W_k': _L1_ffn_in['W_k'], 'L1_ffn_W_v': _L1_ffn_in['W_v'], 'L1_ffn_mu_r': _L1_ffn_in['mu_r'], 'L1_ffn_mu_k': _L1_ffn_in['mu_k']}
    _x0 = _d['L0_attn_tokens']
    _d['L0_attn_tokens'] = jax.random.normal(jax.random.fold_in(jax.random.key(seed), 1), (8, 512, 256), dtype=_x0.dtype)
    del _x0
    return _d

def reference(L0_attn_tokens, L0_attn_norm_w, L0_attn_Wq, L0_attn_Wkv, L0_attn_Wo, L0_attn_q_gamma, L0_attn_k_gamma, L0_ffn_Wr, L0_ffn_W1, L0_ffn_b1, L0_ffn_W2, L0_ffn_b2, L1_attn_norm_scale, L1_attn_norm_bias, L1_attn_in_proj_w, L1_attn_A_log, L1_attn_dt_bias, L1_attn_bcB_scale, L1_attn_bcC_scale, L1_attn_B_bias, L1_attn_C_bias, L1_attn_theta_w, L1_attn_D, L1_attn_out_proj_w, L1_ffn_W_r, L1_ffn_W_k, L1_ffn_W_v, L1_ffn_mu_r, L1_ffn_mu_k):

    def _L0_attn_ref(tokens, norm_w, Wq, Wkv, Wo, q_gamma, k_gamma):
        import jax, jax.numpy as jnp
        import numpy as np
        DIM = 256
        HEADS = 16
        DIM_HEAD = 64
        SOFTCLAMP = 50.0

        def _rmsnorm(x, w):
            eps = jnp.finfo(x.dtype).eps
            var = jnp.mean(jnp.square(x), axis=-1, keepdims=True)
            return x * jax.lax.rsqrt(var + eps) * w

        def _head_rmsnorm(x, gamma):
            norm = jnp.linalg.norm(x, axis=-1, keepdims=True)
            normed = x / jnp.maximum(norm, 1e-12)
            scale = (gamma + 1.0) * DIM_HEAD ** 0.5
            return normed * scale[None, :, None, :]
        b, n, _ = tokens.shape
        x = _rmsnorm(tokens, norm_w)
        q = x @ Wq
        kv = x @ Wkv
        k, v = jnp.split(kv, 2, axis=-1)
        split = lambda t: t.reshape(b, n, HEADS, DIM_HEAD).transpose(0, 2, 1, 3)
        q, k, v = (split(q), split(k), split(v))
        q = _head_rmsnorm(q, q_gamma)
        k = _head_rmsnorm(k, k_gamma)
        sim = jnp.einsum('bhid,bhjd->bhij', q, k)
        sim = jnp.tanh(sim / SOFTCLAMP) * SOFTCLAMP
        sim = sim * DIM_HEAD ** (-0.5)
        attn = jax.nn.softmax(sim, axis=-1)
        out = jnp.einsum('bhij,bhjd->bhid', attn, v)
        out = out.transpose(0, 2, 1, 3).reshape(b, n, HEADS * DIM_HEAD)
        return out @ Wo

    def _L0_ffn_ref(x, Wr, W1, b1, W2, b2):
        import jax, jax.numpy as jnp
        import numpy as np
        CAP_FACTOR = 1.5
        orig_shape = x.shape
        D = x.shape[-1]
        E = Wr.shape[0]
        xf = x.reshape(-1, D)
        T = xf.shape[0]
        cap = int(CAP_FACTOR * T / E)
        logits = xf @ Wr.T
        vals, idx = jax.lax.top_k(logits.T, cap)
        w = jax.nn.softmax(vals, axis=-1)
        xg = xf[idx]
        h = jax.nn.gelu(jnp.einsum('ecd,esdm->ecsm', xg, W1) + b1[:, None], approximate=False)
        y = jnp.einsum('ecsm,esmk->ecsk', h, W2) + b2[:, None]
        y = y.reshape(E, cap, D) * w[..., None]
        out = jnp.zeros_like(xf).at[idx.reshape(-1)].add(y.reshape(-1, D))
        return out.reshape(orig_shape)

    def _L1_attn_ref(u, norm_scale, norm_bias, in_proj_w, A_log, dt_bias, bcB_scale, bcC_scale, B_bias, C_bias, theta_w, D, out_proj_w):
        import jax, jax.numpy as jnp
        import numpy as np
        import math
        from jax import lax
        EPS = 1e-06

        def _layernorm(x, scale, bias):
            mu = jnp.mean(x, axis=-1, keepdims=True)
            var = jnp.var(x, axis=-1, keepdims=True)
            return (x - mu) * lax.rsqrt(var + EPS) * scale + bias

        def _rmsnorm(x, scale):
            ms = jnp.mean(x * x, axis=-1, keepdims=True)
            return x * lax.rsqrt(ms + EPS) * scale

        def _apply_rope(x, phi):
            half = x.shape[-1] // 2
            x_r, x_i = (x[..., :half], x[..., half:])
            c, s = (jnp.cos(phi), jnp.sin(phi))
            return jnp.concatenate([x_r * c - x_i * s, x_r * s + x_i * c], axis=-1)

        def _ssd_trapezoidal_scan(x_heads, B_ssm, C_ssm, dt, A, lam):
            a = jnp.exp(A[None, None, :] * dt)
            Bb, L, H, P = x_heads.shape
            N = B_ssm.shape[-1]
            xs = (jnp.moveaxis(x_heads, 1, 0), jnp.moveaxis(B_ssm, 1, 0), jnp.moveaxis(C_ssm, 1, 0), jnp.moveaxis(a, 1, 0), jnp.moveaxis(dt, 1, 0), jnp.moveaxis(lam, 1, 0))
            h0 = jnp.zeros((Bb, H, P, N), x_heads.dtype)

            def step(carry, inp):
                h, prev_Bx = carry
                x_t, B_t, C_t, a_t, dt_t, lam_t = inp
                Bx = jnp.einsum('bhp,bn->bhpn', x_t, B_t)
                ae = a_t[:, :, None, None]
                dte = dt_t[:, :, None, None]
                le = lam_t[:, :, None, None]
                h = ae * h + dte * (le * Bx + (1.0 - le) * ae * prev_Bx)
                y = jnp.einsum('bhpn,bn->bhp', h, C_t)
                return ((h, Bx), y)
            _, ys = lax.scan(step, (h0, jnp.zeros_like(h0)), xs)
            return jnp.moveaxis(ys, 0, 1)
        D_MODEL, D_STATE, N_HEADS, EXPAND = (256, 64, 16, 2)
        D_INNER = D_MODEL * EXPAND
        HEAD_DIM = D_INNER // N_HEADS
        PROJ = D_INNER + D_INNER + D_STATE + D_STATE + N_HEADS + N_HEADS
        residual = u
        x_in = _layernorm(u, norm_scale, norm_bias)
        proj = x_in @ in_proj_w
        i = 0
        x = proj[..., i:i + D_INNER]
        i += D_INNER
        z = proj[..., i:i + D_INNER]
        i += D_INNER
        B_raw = proj[..., i:i + D_STATE]
        i += D_STATE
        C_raw = proj[..., i:i + D_STATE]
        i += D_STATE
        dt_raw = proj[..., i:i + N_HEADS]
        i += N_HEADS
        lam_raw = proj[..., i:i + N_HEADS]
        A = -jnp.exp(A_log)
        dt = jax.nn.softplus(dt_raw + dt_bias)
        lam = jax.nn.sigmoid(lam_raw)
        B_ssm = _rmsnorm(B_raw, bcB_scale) + B_bias
        C_ssm = _rmsnorm(C_raw, bcC_scale) + C_bias
        theta = u @ theta_w
        dt_scalar = jnp.mean(dt, axis=-1, keepdims=True)
        phi = jnp.cumsum(dt_scalar.astype(jnp.float32) * theta.astype(jnp.float32), axis=1).astype(B_ssm.dtype)
        B_ssm = _apply_rope(B_ssm, phi)
        C_ssm = _apply_rope(C_ssm, phi)
        x = jax.nn.silu(x)
        x_heads = x.reshape(*x.shape[:-1], N_HEADS, HEAD_DIM)
        y_heads = _ssd_trapezoidal_scan(x_heads, B_ssm, C_ssm, dt, A, lam)
        y_heads = y_heads + x_heads * D[None, None, :, None]
        y = y_heads.reshape(*y_heads.shape[:-2], D_INNER) * jax.nn.silu(z)
        y = y @ out_proj_w
        return y + residual

    def _L1_ffn_ref(x, W_r, W_k, W_v, mu_r, mu_k):
        import jax, jax.numpy as jnp
        import numpy as np
        DIM = 256

        def _reference_tuple_inner(x, W_r, W_k, W_v, mu_r, mu_k):
            B, T, C = x.shape
            x_prev = jnp.concatenate([jnp.zeros((B, 1, C), x.dtype), x[:, :-1, :]], axis=1)
            xr = mu_r * x + (1.0 - mu_r) * x_prev
            xk = mu_k * x + (1.0 - mu_k) * x_prev
            r = jax.nn.sigmoid(jnp.einsum('btc,dc->btd', xr, W_r))
            k = jnp.einsum('btc,dc->btd', xk, W_k)
            k_act = jnp.square(jax.nn.relu(k))
            out = r * jnp.einsum('btc,dc->btd', k_act, W_v)
            new_state = x[:, -1, :]
            return (out, new_state)
        return _reference_tuple_inner(x, W_r, W_k, W_v, mu_r, mu_k)[0]
    x = L0_attn_tokens
    x = x + 0.5 * _L0_ffn_ref(_layernorm(x, axis=-1), L0_ffn_Wr, L0_ffn_W1, L0_ffn_b1, L0_ffn_W2, L0_ffn_b2)
    x = x + _L0_attn_ref(_layernorm(x, axis=-1), L0_attn_norm_w, L0_attn_Wq, L0_attn_Wkv, L0_attn_Wo, L0_attn_q_gamma, L0_attn_k_gamma)
    x = x + 0.5 * _L0_ffn_ref(_layernorm(x, axis=-1), L0_ffn_Wr, L0_ffn_W1, L0_ffn_b1, L0_ffn_W2, L0_ffn_b2)
    x = x + 0.5 * _L1_ffn_ref(_layernorm(x, axis=-1), L1_ffn_W_r, L1_ffn_W_k, L1_ffn_W_v, L1_ffn_mu_r, L1_ffn_mu_k)
    x = x + _L1_attn_ref(_layernorm(x, axis=-1), L1_attn_norm_scale, L1_attn_norm_bias, L1_attn_in_proj_w, L1_attn_A_log, L1_attn_dt_bias, L1_attn_bcB_scale, L1_attn_bcC_scale, L1_attn_B_bias, L1_attn_C_bias, L1_attn_theta_w, L1_attn_D, L1_attn_out_proj_w)
    x = x + 0.5 * _L1_ffn_ref(_layernorm(x, axis=-1), L1_ffn_W_r, L1_ffn_W_k, L1_ffn_W_v, L1_ffn_mu_r, L1_ffn_mu_k)
    return x

_drawn_inputs = setup_inputs


def setup_inputs(seed=0):
    import zlib

    import numpy as np

    out = dict(_drawn_inputs(seed))
    spreads = {'L0_attn_norm_w': (1.0, 0.6),
     'L0_attn_q_gamma': (0.0, 0.8),
     'L0_attn_k_gamma': (0.0, 0.8),
     'L0_ffn_b1': (0.0, 2.0),
     'L0_ffn_b2': (0.0, 0.8),
     'L1_attn_norm_scale': (1.0, 0.2),
     'L1_attn_norm_bias': (0.0, 0.1),
     'L1_attn_bcB_scale': (1.0, 0.2),
     'L1_attn_bcC_scale': (1.0, 0.2),
     'L1_attn_B_bias': (0.0, 0.302),
     'L1_attn_C_bias': (0.0, 0.411),
     'L1_attn_D': (1.0, 0.2)}
    factors = {'L0_attn_Wq': 3.033,
     'L0_attn_Wkv': 2.669,
     'L0_attn_Wo': 2.71,
     'L1_attn_theta_w': 8.0,
     'L1_ffn_W_r': 4.216,
     'L1_ffn_mu_r': 8.0}
    for name, (base, spread) in spreads.items():
        noise = np.random.default_rng([zlib.crc32(name.encode()), seed]).standard_normal(out[name].shape)
        drawn = base * np.exp(spread * noise) if base else spread * noise
        out[name] = jnp.asarray(drawn.astype(out[name].dtype))
    for name, factor in factors.items():
        out[name] = (out[name] * factor).astype(out[name].dtype)
    return out
```

```python
from contextlib import ExitStack

import concourse.bass as bass
from concourse import mybir

F32 = mybir.dt.float32
BF16 = mybir.dt.bfloat16
U32 = mybir.dt.uint32
ALU = mybir.AluOpType
ACT = mybir.ActivationFunctionType
AX = mybir.AxisListType

P = 128
D = 256
KC = D // P
SEQ = 512
BATCH = 8
TOKENS = BATCH * SEQ
GT = SEQ // P
GROUPS = TOKENS // SEQ
LN_EPS = 1e-5


def wait_at(eng, sem, count, ready):
    if isinstance(count, int):
        eng.wait_ge(sem, count)
        return
    value = eng.snap(eng.to_reg(count))
    eng.wait_ge(ready, 1)
    eng.wait_ge(sem, value)


def ahead(i, u, k=1):
    return i + (u + k) // 2, (u + k) % 2


class Space:

    def __init__(self, nc, ctx, prefix):
        self.nc, self.ctx, self.prefix, self.counts = nc, ctx, prefix, []

    def sb(self, name, shape, dtype=F32):
        return self.ctx.enter_context(self.nc.sbuf_tensor(f"{self.prefix}_{name}", shape, dtype))

    def ps(self, name, shape, dtype=F32):
        return self.ctx.enter_context(self.nc.psum_tensor(f"{self.prefix}_{name}", shape, dtype))

    def sem(self, name):
        count = self.ctx.enter_context(self.nc.semaphore(f"{self.prefix}_{name}"))
        self.counts.append(count)
        return count

    def clear(self):
        numbers = sorted(c.num for c in self.counts)
        start = 0
        for k in range(1, len(numbers) + 1):
            if k == len(numbers) or numbers[k] != numbers[k - 1] + 1:
                self.nc.gpsimd.sem_clear(range(numbers[start], numbers[k - 1] + 1))
                start = k
        self.nc.all_engine_barrier()

    def sems(self, name, n):
        return [self.sem(f"{name}{k}") for k in range(n)]


class Constants:

    def __init__(self, nc, ctx):
        s = Space(nc, ctx, "const")
        self.ident = s.sb("ident", [P, P])
        self.ones = s.sb("ones", [P, P])
        self.flip = s.sb("flip", [P, P])
        self.first = s.sb("first", [P, P])
        self.last = s.sb("last", [P, P])
        self.tri = s.sb("tri", [P, P])
        self.shift = s.sb("shift", [P, P])
        self.wrap = s.sb("wrap", [P, P])
        self.ident_b = s.sb("ident_b", [P, P], BF16)
        self.never = s.sb("never", [P, P], BF16)
        self.minus_half = s.sb("minus_half", [P, 64])
        self.half_offset = s.sb("half_offset", [P, 1])
        self.ready = s.sem("ready")
        made = s.sem("made")
        with nc.Block() as block:

            @block.gpsimd
            def _(pool):
                pool.memset(self.minus_half[:], -0.5)
                pool.memset(self.ones[:], 1.0).then_inc(made, 1)
                pool.memset(self.half_offset[:], float(TOKENS // 2)).then_inc(made, 1)
                pool.wait_ge(made, 2)
                pool.affine_select(out=self.half_offset[:], in_=self.half_offset[:], pattern=[[0, 1]],
                                   compare_op=ALU.is_ge, fill=0.0, base=-64, channel_multiplier=1)
                for out, pattern, base, cm in (
                    (self.ident, [[-1, P]], 0, 1),
                    (self.flip, [[1, P]], -(P - 1), 1),
                    (self.first, [[0, P]], 0, 1),
                    (self.last, [[0, P]], -(P - 1), 1),
                ):
                    pool.affine_select(out=out[:], in_=self.ones[:], pattern=pattern, compare_op=ALU.is_equal,
                                       fill=0.0, base=base, channel_multiplier=cm)
                pool.affine_select(out=self.tri[:], in_=self.ones[:], pattern=[[1, P]], compare_op=ALU.is_ge,
                                   fill=0.0, base=0, channel_multiplier=-1)
                pool.affine_select(out=self.shift[:], in_=self.ones[:], pattern=[[-1, P]], compare_op=ALU.is_equal,
                                   fill=0.0, base=-1, channel_multiplier=1)
                pool.affine_select(out=self.ident_b[:], in_=self.ones[:], pattern=[[-1, P]], compare_op=ALU.is_equal,
                                   fill=0.0, base=0, channel_multiplier=1)
                pool.memset(self.never[:], 0.0).then_inc(made, 1)
                pool.memset(self.wrap[:], 0.0).then_inc(made, 1)
                pool.wait_ge(made, 4)
                pool.affine_select(out=self.never[:], in_=self.never[:], pattern=[[1, P]], compare_op=ALU.is_ge,
                                   fill=-1e30, base=0, channel_multiplier=-1)
                pool.affine_select(out=self.wrap[:], in_=self.wrap[:], pattern=[[-1, P]], compare_op=ALU.not_equal,
                                   fill=1.0, base=P - 1, channel_multiplier=1)
                pool.drain().then_inc(self.ready, 1)


class Norm:

    def __init__(self, s, x, banks=2, lead=0, unroll=2, turned=None, eps2=None):
        self.x = x
        self.unroll, self.eps2 = unroll, eps2
        self.lead, self.banks = lead, banks
        self.xn = s.sb("xn", [P, unroll, GT, D])
        self.stats = s.sb("stats", [P, unroll, GT, 6])
        self.moments = s.sb("moments", [P, unroll, GT, 2])
        self.var = s.sb("var", [P, unroll, GT])
        self.rstd = s.sb("rstd", [P, unroll, GT])
        self.xT = s.sb("xT", [P, unroll, KC, lead + SEQ])
        self.turned = s.ps("turned", [P, banks, KC, SEQ]) if turned is None else turned
        if eps2 is not None:
            self.eps2_tile = s.sb("eps2_tile", [P, GT])
            self.work = s.sb("work", [P, unroll, 3, GT])
            self.eps2_set = s.sem("eps2_set")
            self.norm2_step = s.sem("norm2_step")
        self.x_landed = s.sems("x_landed", 2)
        self.stats_ready = s.sem("stats_ready")
        self.moments_ready = s.sem("moments_ready")
        self.var_ready = s.sem("var_ready")
        self.rstd_ready = s.sem("rstd_ready")
        self.xn_ready = s.sem("xn_ready")
        self.xn_free = s.sem("xn_free")
        self.xn_stored = None
        self.turned_ready = s.sem("turned_ready")
        self.xT_ready = s.sem("xT_ready")
        self.xT_free = s.sem("xT_free")

    def load(self, sp, ready, x_dram, i, u, group):
        sp.dma_start(self.x[:, bass.ds(group, 1)].rearrange("p g t d -> p (g t) d"),
                     x_dram[bass.ds(group * SEQ, SEQ), :].rearrange("(t p) d -> p t d", p=P)
                     ).then_inc(self.x_landed[u], 16)

    def moments_of(self, dve, ready, i, u, group, loaded=True):
        n1 = self.unroll * i + (u + 1)
        if loaded:
            wait_at(dve, self.x_landed[u], 16 * i + 16, ready)
        x = self.x[:, bass.ds(group, 1)].rearrange("p g t d -> p (g t) d")
        for t in range(GT):
            last = dve.bn_stats(self.stats[:, u, t, :], x[:, t, :])
        last.then_inc(self.stats_ready, 1)
        wait_at(dve, self.stats_ready, n1, ready)
        for t in range(GT):
            last = dve.bn_aggr(self.moments[:, u, t, :], self.stats[:, u, t, :])
        last.then_inc(self.moments_ready, 1)
        wait_at(dve, self.moments_ready, n1, ready)
        dve.tensor_scalar(self.var[:, u, :], self.moments[:, u, :, 1], LN_EPS, None, ALU.add
                          ).then_inc(self.var_ready, 1)

    def root(self, pool, ready, const, i, u):
        n = self.unroll * i + u
        wait_at(pool, self.var_ready, n + 1, ready)
        half = const.minus_half[:, 0:GT]
        if self.eps2 is None:
            pool.tensor_tensor(self.rstd[:, u, :], self.var[:, u, :], half, ALU.pow).then_inc(self.rstd_ready, 1)
            return
        root, ms, fac = (self.work[:, u, k, :] for k in range(3))
        pool.tensor_tensor(root, self.var[:, u, :], half, ALU.pow).then_inc(self.norm2_step, 1)
        wait_at(pool, self.norm2_step, 5 * n + 1, ready)
        pool.tensor_tensor(ms, root, root, ALU.mult).then_inc(self.norm2_step, 1)
        wait_at(pool, self.norm2_step, 5 * n + 2, ready)
        pool.tensor_tensor(ms, ms, self.moments[:, u, :, 1], ALU.mult).then_inc(self.norm2_step, 1)
        wait_at(pool, self.norm2_step, 5 * n + 3, ready)
        pool.tensor_tensor(ms, ms, self.eps2_tile[:], ALU.add).then_inc(self.norm2_step, 1)
        wait_at(pool, self.norm2_step, 5 * n + 4, ready)
        pool.tensor_tensor(fac, ms, half, ALU.pow).then_inc(self.norm2_step, 1)
        wait_at(pool, self.norm2_step, 5 * n + 5, ready)
        pool.tensor_tensor(self.rstd[:, u, :], root, fac, ALU.mult).then_inc(self.rstd_ready, 1)

    def normalise(self, dve, ready, i, u, group):
        n1 = self.unroll * i + (u + 1)
        wait_at(dve, self.rstd_ready, n1, ready)
        wait_at(dve, self.xn_free, n1, ready)
        if self.xn_stored is not None:
            wait_at(dve, self.xn_stored, n1, ready)
        x = self.x[:, bass.ds(group, 1)].rearrange("p g t d -> p (g t) d")
        for t in range(GT):
            last = dve.tensor_scalar(self.xn[:, u, t, :], x[:, t, :], self.moments[:, u, t, 0:1],
                                     self.rstd[:, u, t:t + 1], ALU.subtract, ALU.mult)
        last.then_inc(self.xn_ready, 1)

    def turn(self, pe, ready, const, i, u):
        n1 = self.unroll * i + (u + 1)
        wait_at(pe, self.xn_ready, n1, ready)
        wait_at(pe, self.xT_ready, n1, ready)
        for c in range(KC):
            for t in range(GT):
                last = pe.transpose(self.turned[:, u % self.banks, c, t * P:(t + 1) * P],
                                    self.xn[:, u, t, c * P:(c + 1) * P], const.ident[:])
        last.then_inc(self.turned_ready, 1)

    def keep(self, act, ready, i, u, count=True):
        n1 = self.unroll * i + (u + 1)
        wait_at(act, self.turned_ready, n1, ready)
        act.sem_inc(self.xn_free, 1)
        wait_at(act, self.xT_free, n1, ready)
        copy = act.activation(self.xT[:, u, :, self.lead:], self.turned[:, u % self.banks], ACT.Copy)
        if count:
            copy.then_inc(self.xT_ready, 1)

    def kept(self, eng, ready, i, u):
        wait_at(eng, self.xT_ready, self.unroll * i + (u + 1 + self.banks), ready)


EXPERTS = 48
SLOTS = 4
HID = 256
HC = SLOTS * HID // P
YK = D // SLOTS
CAP = int(1.5 * TOKENS / EXPERTS)
EU = 4
HALF = TOKENS // 2
ROUNDS = CAP // 8


def moe_stage(nc, lasting, const, name, load, x_all, x_dram, acc_dram, xn_dram, wr_dram, w1_dram, b1_dram, w2_dram, b2_dram):
    with ExitStack() as ctx:
        s = Space(nc, ctx, name)
        ready = const.ready
        with ExitStack() as rctx:
            r = Space(nc, rctx, name + "_router")
            keep_vals = s.sb("sel_w", [P, EXPERTS])
            index = s.sb("index", [P, EXPERTS], U32)
            norm = Norm(r, x_all)
            wr = r.sb("wr", [P, KC, 64])
            logits = r.sb("logits", [P, HALF])
            vals = r.sb("vals", [P, CAP])
            idx = r.sb("idx", [P, CAP], U32)
            idxf = r.sb("idxf", [P, CAP])
            both = r.sb("both", [P, 2, P])
            swapped = r.sb("swapped", [P, 2, EXPERTS])
            take = r.sb("take", [P, EXPERTS])
            best = r.sb("best", [P, EXPERTS])
            diff = r.sb("diff", [P, EXPERTS])
            token = r.sb("token", [P, EXPERTS])
            top = r.sb("top", [P, 2, EXPERTS])
            peak = r.sb("peak", [P, EXPERTS])
            expo = r.sb("expo", [P, EXPERTS])
            total = r.sb("total", [P, EXPERTS])
            plog = r.ps("plog", [P, 2, SEQ])
            small = r.ps("small", [P, 512])
            small2 = r.ps("small2", [P, 512])
            wr_zero, wr_landed = r.sem("wr_zero"), r.sem("wr_landed")
            norm.xn_stored = r.sem("xn_stored")
            xn_store = lasting.sems(name + "_xn_store", 2)
            acc_set = r.sem("acc_set")
            logits_psum = r.sem("logits_psum")
            logits_kept = r.sem("logits_kept")
            chain = r.sem("topk_chain")
            pe_small, exp_ready = r.sem("pe_small"), r.sem("exp_ready")
            xn_out = xn_dram.rearrange("(g t p) d -> g p t d", t=GT, p=P)

            with nc.Block() as block:

                @block.sync
                def _(sp):
                    sp.wait_ge(wr_zero, 1)
                    sp.dma_start(wr[:, :, 0:EXPERTS], wr_dram).then_inc(wr_landed, 16)
                    if load:
                        sp.dma_start(acc_dram.rearrange("(a p) d -> p a d", p=P),
                                     x_dram.rearrange("(a p) d -> p a d", p=P)).then_inc(acc_set, 16)
                    if not load:
                        return
                    with sp.Fori(0, GROUPS // 2) as i:
                        for u in range(2):
                            norm.load(sp, ready, x_dram, i, u, i + u * (GROUPS // 2))
                        for u in range(2):
                            wait_at(sp, norm.x_landed[u], 16 * i + 16, ready)
                    sp.wait_ge(acc_set, 16)

                @block.vector
                def _(dve):
                    dve.memset(wr[:], 0.0).then_inc(wr_zero, 1)
                    with dve.Fori(0, GROUPS // 2) as i:
                        for u in range(2):
                            norm.moments_of(dve, ready, i, u, i + u * (GROUPS // 2), load)
                            norm.normalise(dve, ready, i, u, i + u * (GROUPS // 2))
                    steps = 0

                    def link(ins):
                        nonlocal steps
                        steps += 1
                        ins.then_inc(chain, 1)
                        dve.wait_ge(chain, steps)

                    dve.wait_ge(logits_kept, GROUPS + 2)
                    for k in range(ROUNDS):
                        eight = vals[:, 8 * k:8 * k + 8]
                        link(dve.max(eight, logits[:]))
                        link(dve.max_index(idx[:, 8 * k:8 * k + 8], eight, logits[:]))
                        if k < ROUNDS - 1:
                            link(dve.match_replace(logits[:], eight, logits[:], -3.4e38))
                    link(dve.tensor_copy(idxf[:], idx[:]))
                    link(dve.tensor_scalar(idxf[:], idxf[:], const.half_offset[:, 0:1], None, ALU.add))
                    dve.wait_ge(pe_small, 1)
                    link(dve.tensor_copy(both[:], small[:, 0:2 * P].rearrange("p (a b) -> p a b", a=2)))
                    dve.wait_ge(pe_small, 2)
                    link(dve.tensor_copy(swapped[:], small2[:, 0:2 * EXPERTS].rearrange("p (a b) -> p a b", a=2)))
                    link(dve.tensor_tensor(take[:], both[:, 0, 0:EXPERTS], swapped[:, 0, :], ALU.is_ge))
                    link(dve.tensor_tensor(best[:], both[:, 0, 0:EXPERTS], swapped[:, 0, :], ALU.max))
                    link(dve.tensor_tensor(diff[:], both[:, 1, 0:EXPERTS], swapped[:, 1, :], ALU.subtract))
                    link(dve.tensor_tensor(diff[:], diff[:], take[:], ALU.mult))
                    link(dve.tensor_tensor(token[:], diff[:], swapped[:, 1, :], ALU.add))
                    link(dve.tensor_copy(index[:], token[:]))
                    dve.wait_ge(pe_small, 3)
                    link(dve.tensor_copy(top[:], small[:, 256:256 + 2 * EXPERTS].rearrange("p (a b) -> p a b", a=2)))
                    link(dve.tensor_tensor(peak[:], top[:, 0, :], top[:, 1, :], ALU.max))
                    link(dve.tensor_tensor(best[:], best[:], peak[:], ALU.subtract))
                    dve.wait_ge(pe_small, 4)
                    link(dve.reciprocal(total[:], small2[:, 256:256 + EXPERTS]))
                    link(dve.scalar_tensor_tensor(out=keep_vals[:], in0=expo[:], scalar=0.5, in1=total[:],
                                                  op0=ALU.mult, op1=ALU.mult))

                @block.gpsimd
                def _(pool):
                    pool.sem_inc(norm.xn_stored, 2)
                    with pool.Fori(0, GROUPS // 2) as i:
                        for u in range(2):
                            norm.root(pool, ready, const, i, u)
                            wait_at(pool, norm.xn_ready, 2 * i + (u + 1), ready)
                            pool.dma_start(xn_out[bass.ds(i + u * (GROUPS // 2), 1)].rearrange("g p t d -> p (g t) d"),
                                           norm.xn[:, u]).then_inc(xn_store[u], 16)
                            wait_at(pool, xn_store[u], 16 * i + 16, ready)
                            pool.sem_inc(norm.xn_stored, 1)

                @block.tensor
                def _(pe):
                    pe.wait_ge(wr_landed, 16)
                    with pe.Fori(0, GROUPS // 2) as i:
                        for u in range(2):
                            norm.turn(pe, ready, const, i, u)
                            norm.kept(pe, ready, i, u)
                            wait_at(pe, logits_kept, 2 * i + (u + 1), ready)
                            for c in range(KC):
                                last = pe.matmul(plog[64 * u:64 * u + 64, u, :], wr[:, c, :], norm.xT[:, u, c, :],
                                                 start=(c == 0), stop=(c == KC - 1))
                            last.then_inc(logits_psum, 1)
                    pe.wait_ge(chain, 3 * ROUNDS + 1)
                    pe.transpose(small[:, 0:P], vals[:], const.ident[:])
                    pe.transpose(small[:, P:2 * P], idxf[:], const.ident[:]).then_inc(pe_small, 1)
                    pe.wait_ge(chain, 3 * ROUNDS + 2)
                    for a in range(2):
                        last = pe.matmul(small2[:, a * EXPERTS:(a + 1) * EXPERTS], const.flip[:],
                                         both[:, a, 64:64 + EXPERTS], start=True, stop=True)
                    last.then_inc(pe_small, 1)
                    pe.wait_ge(chain, 3 * ROUNDS + 9)
                    for a, row in enumerate((const.first, const.last)):
                        last = pe.matmul(small[:, 256 + a * EXPERTS:256 + (a + 1) * EXPERTS], row[:], best[:],
                                         start=True, stop=True)
                    last.then_inc(pe_small, 1)
                    pe.wait_ge(exp_ready, 1)
                    pe.matmul(small2[:, 256:256 + EXPERTS], const.ones[:], expo[:], start=True, stop=True
                              ).then_inc(pe_small, 1)

                @block.scalar
                def _(act):
                    act.sem_inc(norm.xT_free, 2)
                    act.sem_inc(norm.xn_free, 2)
                    act.sem_inc(norm.xT_ready, norm.banks)
                    act.sem_inc(logits_kept, 2)
                    with act.Fori(0, GROUPS // 2) as i:
                        for u in range(2):
                            norm.keep(act, ready, i, u)
                            wait_at(act, logits_psum, 2 * i + (u + 1), ready)
                            act.sem_inc(norm.xT_free, 1)
                            rows = slice(64 * u, 64 * u + 64)
                            act.activation(logits[rows, bass.ds(i * SEQ, SEQ)], plog[rows, u, :], ACT.Copy
                                           ).then_inc(logits_kept, 1)
                    act.wait_ge(chain, 3 * ROUNDS + 12)
                    act.activation(expo[:], best[:], ACT.Exp).then_inc(exp_ready, 1)
            r.clear()

        w1 = s.sb("w1", [P, EU, KC, SLOTS * HID])
        w2 = s.sb("w2", [P, EU, HC, YK])
        b2 = s.sb("b2", [1, EU, D])
        b1 = s.sb("b1", [P, EXPERTS, HC])
        slot = s.sb("slot", [P, EU], U32)
        xg = s.sb("xg", [P, EU, D])
        xgT = s.sb("xgT", [P, 2, KC, P])
        hb = s.sb("hb", [P, 2, HC, P])
        h = s.sb("h", [P, 2, HC, P])
        y = s.sb("y", [P, EU, D])
        pT = s.ps("pT", [P, 2, 512])
        pH = s.ps("pH", [P, 2, HC, P])
        pY = s.ps("pY", [P, 2, 512])
        b1_landed = s.sem("b1_landed")
        w_landed = s.sems("w_landed", EU)
        gathered = lasting.sems(name + "_gathered", EU)
        scattered = lasting.sem(name + "_scattered")
        slot_ready, gT_psum, gT_ready = s.sem("slot_ready"), s.sem("gT_psum"), s.sem("gT_ready")
        h_psum, h_ready, y_psum = s.sem("h_psum"), s.sem("h_ready"), s.sem("y_psum")
        h_biased = s.sem("h_biased")
        y_ready = s.sem("y_ready")
        w_free = s.sem("w_free")

        def count(i, u, extra=1):
            return EU * i + (u + extra)

        with nc.Block() as block:

            @block.sync
            def _(sp):
                sp.dma_start(b1[:], b1_dram).then_inc(b1_landed, 16)
                with sp.Fori(0, EXPERTS // EU) as i:
                    for u in range(EU):
                        wait_at(sp, w_free, count(i, u), ready)
                        e = EU * i + u
                        sp.dma_start(w1[:, u], w1_dram[bass.ds(e, 1)].rearrange("e p c n -> p (e c) n")
                                     ).then_inc(w_landed[u], 16)
                        sp.dma_start(w2[:, u], w2_dram[bass.ds(e, 1)].rearrange("e p c n -> p (e c) n")
                                     ).then_inc(w_landed[u], 16)
                        sp.dma_start(b2[:, u], b2_dram[bass.ds(e, 1), :]).then_inc(w_landed[u], 16)

            @block.gpsimd
            def _(pool):
                for u in range(EU):
                    pool.tensor_copy(slot[:, u:u + 1], index[:, u:u + 1]).then_inc(slot_ready, 1)
                    pool.wait_ge(slot_ready, u + 1)
                    pool.indirect_dma_start(xg[:, u, :], None, xn_dram, bass.IndirectOffsetOnAxis(slot[:, u:u + 1], 0)
                                            ).then_inc(gathered[u], 16)
                with pool.Fori(0, EXPERTS // EU - 1) as i:
                    for u in range(EU):
                        wait_at(pool, y_ready, count(i, u, 3), ready)
                        pool.indirect_dma_start(acc_dram, bass.IndirectOffsetOnAxis(slot[:, u:u + 1], 0), y[:, u, :],
                                                None, compute_op=ALU.add).then_inc(scattered, 16)
                        wait_at(pool, scattered, 16 * count(i, u), ready)
                        pool.tensor_copy(slot[:, u:u + 1], index[:, bass.ds(count(i, u, EU), 1)]
                                         ).then_inc(slot_ready, 1)
                        wait_at(pool, slot_ready, count(i, u, 1 + EU), ready)
                        pool.indirect_dma_start(xg[:, u, :], None, xn_dram,
                                                bass.IndirectOffsetOnAxis(slot[:, u:u + 1], 0)
                                                ).then_inc(gathered[u], 16)
                for e in range(EXPERTS - EU, EXPERTS):
                    pool.wait_ge(y_ready, e + 3)
                    u = e % EU
                    pool.indirect_dma_start(acc_dram, bass.IndirectOffsetOnAxis(slot[:, u:u + 1], 0), y[:, u, :],
                                            None, compute_op=ALU.add).then_inc(scattered, 16)
                    pool.wait_ge(scattered, 16 * (e + 1))

            @block.tensor
            def _(pe):
                with pe.Fori(0, EXPERTS // EU) as i:
                    for u in range(EU):
                        v = u % 2
                        wait_at(pe, gathered[u], 16 * i + 16, ready)
                        for c in range(KC):
                            last = pe.transpose(pT[:, v, c * P:(c + 1) * P], xg[:, u, c * P:(c + 1) * P],
                                                const.ident[:])
                        last.then_inc(gT_psum, 1)
                        wait_at(pe, w_landed[u], 48 * i + 48, ready)
                        wait_at(pe, gT_ready, count(i, u), ready)
                        wait_at(pe, h_biased, count(i, u), ready)
                        for j in range(HC):
                            for c in range(KC):
                                last = pe.matmul(pH[:, v, j, :], w1[:, u, c, j * P:(j + 1) * P], xgT[:, v, c, :],
                                                 start=(c == 0), stop=(c == KC - 1))
                        last.then_inc(h_psum, 1)
                        wait_at(pe, h_ready, count(i, u), ready)
                        wait_at(pe, y_ready, count(i, u), ready)
                        pe.matmul(pY[:, v, 0:D], const.ones[0:1, :], b2[:, u, :], start=True, stop=False,
                                  skip_group_check=True)
                        for j in range(HC):
                            q = j * P // HID
                            last = pe.matmul(pY[:, v, q * YK:(q + 1) * YK], h[:, v, j, :], w2[:, u, j, :],
                                             start=False, stop=(j == HC - 1), skip_group_check=True)
                        last.then_inc(y_psum, 1)

            @block.scalar
            def _(act):
                with act.Fori(0, EXPERTS // EU) as i:
                    for u in range(EU):
                        v = u % 2
                        wait_at(act, gT_psum, count(i, u), ready)
                        act.activation(xgT[:, v], pT[:, v, 0:D].rearrange("p (c n) -> p c n", c=KC), ACT.Copy
                                       ).then_inc(gT_ready, 1)
                        wait_at(act, h_biased, count(i, u, 3), ready)
                        act.activation(h[:, v], hb[:, v], ACT.Gelu).then_inc(h_ready, 1)

            @block.vector
            def _(dve):
                dve.wait_ge(b1_landed, 16)
                dve.sem_inc(h_biased, 2)
                dve.sem_inc(y_ready, 2)
                dve.sem_inc(w_free, EU)
                with dve.Fori(0, EXPERTS // EU) as i:
                    for u in range(EU):
                        v = u % 2
                        e = EU * i + u
                        wait_at(dve, h_psum, count(i, u), ready)
                        bias = b1[:, bass.ds(e, 1), :].rearrange("p e j -> p (e j)").unsqueeze(2).to_broadcast([P, HC, P])
                        dve.tensor_tensor(hb[:, v], pH[:, v], bias, ALU.add).then_inc(h_biased, 1)
                        wait_at(dve, y_psum, count(i, u), ready)
                        dve.sem_inc(w_free, 1)
                        dve.tensor_scalar(y[:, u, :], pY[:, v, 0:D], keep_vals[:, bass.ds(e, 1)], None, ALU.mult
                                          ).then_inc(y_ready, 1)
        s.clear()


HEADS = 16
DH = 64
DI = HEADS * DH
PAIRS = HEADS // 2
CLAMP = 50.0
RMS_EPS = 1.1920929e-07
QW = 512
CHUNKS = 3 * DI // QW
HV = QW // DH


def attention_stage(nc, const, x_all, x_dram, out_dram, wqkv_dram, wo_dram, nw_dram, gamma_dram):
    QKV_USE = 1
    TURN_USE = QKV_USE + GT * CHUNKS // 2
    WO_USE = TURN_USE + PAIRS
    MISC = WO_USE + GT // 2
    with ExitStack() as ctx:
        s = Space(nc, ctx, "attn")
        ready = const.ready
        misc = s.ps("misc", [P, 2, 512])
        norm = Norm(s, x_all, banks=1, unroll=1, turned=misc[:].unsqueeze(1), eps2=RMS_EPS)
        w = s.sb("w", [P, KC, 3 * DI])
        wo = s.sb("wo", [P, PAIRS, D])
        nw = s.sb("nw", [P, KC])
        gamma = s.sb("gamma", [P, 2, PAIRS])
        scale = s.sb("scale", [P, PAIRS])
        qk = s.sb("qk", [P, GT, 2, HEADS, DH])
        sq = s.sb("sq", [P, 2 * HEADS, DH])
        ss = s.sb("ss", [P, GT, 2 * HEADS])
        rn = s.sb("rn", [P, GT, 2 * HEADS])
        va = s.sb("va", [P, GT, PAIRS, 3, DH])
        qT = s.sb("qT", [P, 2, SEQ])
        kT = s.sb("kT", [P, 2, SEQ])
        th = s.sb("th", [P, 2, GT, SEQ])
        pr = s.sb("pr", [P, 2, GT, SEQ])
        rec = s.sb("rec", [P, SEQ])
        oT = s.sb("oT", [P, PAIRS, SEQ])
        pS = s.ps("pS", [P, 2, 2, SEQ])
        pO = s.ps("pO", [P, 2, SEQ])
        w_landed, setup = s.sem("w_landed"), s.sem("setup")
        misc_ready = s.sems("misc_ready", 2)
        misc_free = s.sems("misc_free", 2)
        sq_ready = s.sem("sq_ready")
        sum_ready = s.sem("sum_ready")
        ss_ready, rn_ready, qk_ready, v_ready = s.sem("ss_ready"), s.sem("rn_ready"), s.sem("qk_ready"), s.sem("v_ready")
        score_ready = s.sem("score_ready")
        tanh_ready = s.sem("tanh_ready")
        exp_ready = s.sem("exp_ready")
        pv_ready = s.sem("pv_ready")
        rec_ready = s.sem("rec_ready")
        o_ready = s.sem("o_ready")
        out_ready, stored = s.sem("out_ready"), s.sem("stored")

        def chunk_use(t, j):
            return j % 2, QKV_USE + (CHUNKS * t + j) // 2

        def wait_ready(eng, n, bank, use):
            wait_at(eng, misc_ready[bank], MISC * n + (use + 1), ready)

        with nc.Block() as block:

            @block.sync
            def _(sp):
                sp.dma_start(w[:], wqkv_dram).then_inc(w_landed, 16)
                sp.dma_start(wo[:], wo_dram).then_inc(w_landed, 16)
                sp.dma_start(nw[:], nw_dram).then_inc(w_landed, 16)
                sp.dma_start(gamma[:], gamma_dram).then_inc(w_landed, 16)
                with sp.Fori(0, GROUPS) as i:
                    norm.load(sp, ready, x_dram, i, 0, i)
                    wait_at(sp, norm.x_landed[0], 16 * i + 16, ready)
                with sp.Fori(0, GROUPS) as n:
                    wait_at(sp, out_ready, n * GT + GT, ready)
                    sp.dma_start(out_dram[bass.ds(n * SEQ, SEQ), :].rearrange("(t p) d -> p t d", p=P),
                                 x_all[:, bass.ds(n, 1)].rearrange("p g t d -> p (g t) d")).then_inc(stored, 16)
                    wait_at(sp, stored, 16 * n + 16, ready)

            @block.vector
            def _(dve):
                def project(n):
                    for t in range(GT):
                        wait_at(dve, sq_ready, GT * n + (t + 1), ready)
                        dve.tensor_reduce(ss[:, t, :], sq[:], AX.X, ALU.add).then_inc(sum_ready, 1)
                        wait_at(dve, sum_ready, GT * n + (t + 2), ready)
                        dve.tensor_scalar(ss[:, t, :], ss[:, t, :], 1e-24, None, ALU.max).then_inc(ss_ready, 1)
                        if t:
                            unit(n, t - 1)
                    unit(n, GT - 1)

                def unit(n, t):
                    wait_at(dve, rn_ready, GT * n + (t + 1), ready)
                    rows = qk[:, t].rearrange("p a h d -> p (a h) d")
                    dve.tensor_tensor(rows, rows, rn[:, t, :].unsqueeze(2).to_broadcast([P, 2 * HEADS, DH]), ALU.mult
                                      ).then_inc(qk_ready, 1)

                def turn_pair(n, p):
                    wait_ready(dve, n, 0, TURN_USE + p)
                    dve.tensor_scalar(qT[:, p % 2, :], misc[:, 0, :], scale[:, p:p + 1], None, ALU.mult
                                      ).then_inc(misc_free[0], 1)
                    wait_ready(dve, n, 1, TURN_USE + p)
                    dve.tensor_copy(kT[:, p % 2, :], misc[:, 1, :]).then_inc(misc_free[1], 1)

                def head(n, h):
                    v = h % 2
                    own, other = slice(DH * v, DH * v + DH), slice(DH * (1 - v), DH * (1 - v) + DH)
                    wait_at(dve, pv_ready, HEADS * n + (h + 3), ready)
                    dve.reciprocal(rec[own, :], pO[other, v, :]).then_inc(rec_ready, 1)
                    wait_at(dve, rec_ready, HEADS * n + (h + 1), ready)
                    dve.tensor_tensor(oT[own, h // 2, :], pO[own, v, :], rec[own, :], ALU.mult).then_inc(o_ready, 1)

                def batch(n, more):
                    project(n)
                    turn_pair(n, 0)
                    if more:
                        norm.moments_of(dve, ready, n + 1, 0, n + 1)
                    for h in range(HEADS):
                        if h:
                            head(n, h - 1)
                        if h % 2 == 0 and h // 2 + 1 < PAIRS:
                            turn_pair(n, h // 2 + 1)
                        if h == 2 and more:
                            norm.normalise(dve, ready, n + 1, 0, n + 1)
                    head(n, HEADS - 1)
                    for t in range(GT):
                        wait_ready(dve, n, t % 2, WO_USE + t // 2)
                        x = x_all[:, bass.ds(n, 1), t, :].rearrange("p g d -> p (g d)")
                        dve.tensor_tensor(x, x, misc[:, t % 2, 0:D], ALU.add).then_inc(misc_free[t % 2], 1)
                    dve.drain().then_inc(out_ready, GT)

                dve.sem_inc(misc_free[0], 1)
                dve.sem_inc(misc_free[1], 1)
                dve.sem_inc(sum_ready, 1)
                dve.sem_inc(o_ready, 2)
                dve.wait_ge(w_landed, 64)
                for c in range(KC):
                    dve.tensor_scalar(w[:, c, :], w[:, c, :], nw[:, c:c + 1], None, ALU.mult).then_inc(setup, 1)
                dve.memset(va[:, :, :, 1, :], 1.0).then_inc(setup, 1)
                dve.tensor_scalar(gamma[:], gamma[:], 1.0, None, ALU.add).then_inc(setup, 1)
                dve.wait_ge(setup, 4)
                dve.scalar_tensor_tensor(out=scale[:], in0=gamma[:, 0, :], scalar=DH / CLAMP, in1=gamma[:, 1, :],
                                         op0=ALU.mult, op1=ALU.mult).then_inc(setup, 1)
                dve.wait_ge(setup, 5)
                norm.moments_of(dve, ready, 0, 0, 0)
                norm.normalise(dve, ready, 0, 0, 0)
                with dve.Fori(0, GROUPS - 1) as n:
                    batch(n, True)
                batch(GROUPS - 1, False)

            @block.gpsimd
            def _(pool):
                def batch(n, more):
                    for t in range(GT):
                        wait_at(pool, ss_ready, GT * n + (t + 1), ready)
                        pool.tensor_tensor(rn[:, t, :], ss[:, t, :], const.minus_half[:, 0:2 * HEADS], ALU.pow
                                           ).then_inc(rn_ready, 1)
                    if more:
                        norm.root(pool, ready, const, n + 1, 0)

                pool.memset(norm.eps2_tile[:], RMS_EPS).then_inc(norm.eps2_set, 1)
                pool.wait_ge(norm.eps2_set, 1)
                norm.root(pool, ready, const, 0, 0)
                with pool.Fori(0, GROUPS - 1) as n:
                    batch(n, True)
                batch(GROUPS - 1, False)

            @block.scalar
            def _(act):
                act.sem_inc(norm.xT_free, 1)
                act.sem_inc(norm.xn_free, 1)
                act.sem_inc(norm.xT_ready, norm.banks)
                act.sem_inc(tanh_ready, 2)
                with act.Fori(0, GROUPS) as n:
                    norm.keep(act, ready, n, 0)
                    norm.kept(act, ready, n, 0)
                    act.sem_inc(misc_free[0], 1)
                    act.sem_inc(misc_free[1], 1)
                    for t in range(GT):
                        for j in range(CHUNKS):
                            bank, use = chunk_use(t, j)
                            wait_ready(act, n, bank, use)
                            if j < 4:
                                heads = slice((j % 2) * HV, (j % 2 + 1) * HV)
                                act.activation(qk[:, t, j // 2, heads, :],
                                               misc[:, bank, :].rearrange("p (h d) -> p h d", h=HV),
                                               ACT.Copy).then_inc(misc_free[bank], 1)
                            else:
                                pairs = slice((j - 4) * HV // 2, (j - 3) * HV // 2)
                                act.activation(va[:, t, pairs, 0:3:2, :],
                                               misc[:, bank, :].rearrange("p (q a d) -> p q a d", a=2, d=DH),
                                               ACT.Copy).then_inc(misc_free[bank], 1)
                        for bank in range(2):
                            wait_at(act, misc_free[bank], MISC * n + (chunk_use(t, 2)[1] + 2), ready)
                        wait_at(act, sum_ready, GT * n + (t + 1), ready)
                        act.activation(sq[:], qk[:, t].rearrange("p a h d -> p (a h) d"), ACT.Square
                                       ).then_inc(sq_ready, 1)
                    act.drain().then_inc(v_ready, 1)
                    act.sem_inc(norm.xT_free, 1)
                    for h in range(HEADS):
                        v = h % 2
                        for a in range(2):
                            wait_at(act, score_ready, 2 * HEADS * n + (2 * h + a + 1), ready)
                            act.activation(th[:, v, 2 * a:2 * a + 2, :], pS[:, a], ACT.Tanh).then_inc(tanh_ready, 1)
                        wait_at(act, tanh_ready, 2 * HEADS * n + (2 * h + 4), ready)
                        wait_at(act, pv_ready, HEADS * n + (h + 1), ready)
                        act.activation(pr[:, v], th[:, v], ACT.Exp, scale=CLAMP * DH ** -0.5).then_inc(exp_ready, 1)

            @block.tensor
            def _(pe):
                def wait_free(n, bank, use):
                    wait_at(pe, misc_free[bank], MISC * n + (use + 1), ready)

                def turn_pair(n, p):
                    for a in range(2):
                        wait_free(n, a, TURN_USE + p)
                        for t in range(GT):
                            last = pe.transpose(misc[:, a, t * P:(t + 1) * P],
                                                qk[:, t, a, 2 * p:2 * p + 2, :].rearrange("p h d -> p (h d)"),
                                                const.ident[:])
                        last.then_inc(misc_ready[a], 1)

                def scores(n, h):
                    if h % 2 == 0:
                        for a in range(2):
                            wait_at(pe, misc_free[a], MISC * n + (TURN_USE + h // 2 + 2), ready)
                    rows = slice(DH * (h % 2), DH * (h % 2) + DH)
                    for a in range(2):
                        wait_at(pe, tanh_ready, 2 * HEADS * n + (2 * h + a + 1), ready)
                        for b in range(2):
                            j = 2 * a + b
                            last = pe.matmul(pS[:, a, b, :], kT[rows, (h // 2) % 2, j * P:(j + 1) * P],
                                             qT[rows, (h // 2) % 2, :], start=True, stop=True)
                        last.then_inc(score_ready, 1)

                def values(n, h):
                    wait_at(pe, exp_ready, HEADS * n + (h + 1), ready)
                    wait_at(pe, o_ready, HEADS * n + (h + 1), ready)
                    v = h % 2
                    for j in range(GT):
                        last = pe.matmul(pO[:, v, :], va[:, j, h // 2, v:v + 2, :].rearrange("p a d -> p (a d)"),
                                         pr[:, v, j, :], start=(j == 0), stop=(j == GT - 1))
                    last.then_inc(pv_ready, 1)

                pe.sem_inc(pv_ready, 2)
                pe.wait_ge(setup, 5)
                with pe.Fori(0, GROUPS) as n:
                    wait_free(n, 0, 0)
                    wait_free(n, 1, 0)
                    norm.turn(pe, ready, const, n, 0)
                    norm.kept(pe, ready, n, 0)
                    pe.sem_inc(misc_ready[0], 1)
                    pe.sem_inc(misc_ready[1], 1)
                    for t in range(GT):
                        for j in range(CHUNKS):
                            bank, use = chunk_use(t, j)
                            wait_free(n, bank, use)
                            for c in range(KC):
                                last = pe.matmul(misc[:, bank, :], norm.xT[:, 0, c, t * P:(t + 1) * P],
                                                 w[:, c, j * QW:(j + 1) * QW], start=(c == 0), stop=(c == KC - 1))
                            last.then_inc(misc_ready[bank], 1)
                    wait_at(pe, qk_ready, GT * n + GT, ready)
                    wait_at(pe, v_ready, n + 1, ready)
                    turn_pair(n, 0)
                    for h in range(HEADS):
                        scores(n, h)
                        if h:
                            values(n, h - 1)
                        if h % 2 == 0 and h // 2 + 1 < PAIRS:
                            turn_pair(n, h // 2 + 1)
                    values(n, HEADS - 1)
                    wait_at(pe, o_ready, HEADS * n + (HEADS + 2), ready)
                    for t in range(GT):
                        wait_free(n, t % 2, WO_USE + t // 2)
                        for p in range(PAIRS):
                            last = pe.matmul(misc[:, t % 2, 0:D], oT[:, p, t * P:(t + 1) * P], wo[:, p, :],
                                             start=(p == 0), stop=(p == PAIRS - 1))
                        last.then_inc(misc_ready[t % 2], 1)
        s.clear()


def rwkv_stage(nc, const, name, load, x_all, x_dram, out_dram, wr_dram, wk_dram, wv_dram, mu_dram):
    with ExitStack() as ctx:
        s = Space(nc, ctx, name)
        ready = const.ready
        norm = Norm(s, x_all, banks=1, lead=1)
        wr, wk, wv = s.sb("wr", [P, KC, D]), s.sb("wk", [P, KC, D]), s.sb("wv", [P, KC, D])
        mu = s.sb("mu", [P, 2, KC])
        step_back = s.sb("step_back", [P, KC, SEQ])
        mixed = s.sb("mixed", [P, 2, 2, KC, SEQ])
        relu = s.sb("relu", [P, KC, SEQ])
        act2 = s.sb("act2", [P, KC, SEQ])
        gate = s.sb("gate", [P, GT, D])
        prod = s.sb("prod", [P, GT, D])
        pk = s.ps("pk", [P, KC, SEQ])
        pr = s.ps("pr", [P, GT, D])
        pv = s.ps("pv", [P, GT, D])
        w_landed = s.sem("w_landed")
        lead_clear = s.sem("lead_clear")
        step_ready, mixed_ready = s.sem("step_ready"), s.sem("mixed_ready")
        pk_ready, relu_ready, act2_ready = s.sem("pk_ready"), s.sem("relu_ready"), s.sem("act2_ready")
        pr_ready, gate_ready, pv_ready = s.sem("pr_ready"), s.sem("gate_ready"), s.sem("pv_ready")
        prod_ready = s.sem("prod_ready")
        out_ready = s.sem("out_ready")
        stored = s.sems("stored", 2)
        last_i = GROUPS // 2 - 1

        with nc.Block() as block:

            @block.sync
            def _(sp):
                sp.dma_start(wr[:], wr_dram).then_inc(w_landed, 16)
                sp.dma_start(wk[:], wk_dram).then_inc(w_landed, 16)
                sp.dma_start(wv[:], wv_dram).then_inc(w_landed, 16)
                sp.dma_start(mu[:], mu_dram).then_inc(w_landed, 16)
                if load:
                    with sp.Fori(0, GROUPS // 2) as i:
                        for u in range(2):
                            norm.load(sp, ready, x_dram, i, u, 2 * i + u)
                        for u in range(2):
                            wait_at(sp, norm.x_landed[u], 16 * i + 16, ready)
                if out_dram is not None:
                    with sp.Fori(0, GROUPS // 2) as i:
                        for u in range(2):
                            wait_at(sp, out_ready, 2 * i + (u + 1), ready)
                            sp.dma_start(out_dram[bass.ds((2 * i + u) * SEQ, SEQ), :].rearrange("(t p) d -> p t d", p=P),
                                         x_all[:, bass.ds(2 * i + u, 1)].rearrange("p g t d -> p (g t) d")
                                         ).then_inc(stored[u], 16)
                        for u in range(2):
                            wait_at(sp, stored[u], 16 * i + 16, ready)

            @block.vector
            def _(dve):
                def first(i, u):
                    norm.moments_of(dve, ready, i, u, 2 * i + u, load)
                    norm.normalise(dve, ready, i, u, 2 * i + u)

                def mix(i, u):
                    n1 = 2 * i + (u + 1)
                    norm.kept(dve, ready, i, u)
                    now, before = norm.xT[:, u, :, 1:], norm.xT[:, u, :, 0:SEQ]
                    dve.tensor_tensor(step_back[:], now, before, ALU.subtract).then_inc(step_ready, 1)
                    wait_at(dve, step_ready, n1, ready)
                    for r in range(2):
                        for c in range(KC):
                            last = dve.scalar_tensor_tensor(out=mixed[:, u, r, c, :], in0=step_back[:, c, :],
                                                            scalar=mu[:, r, c:c + 1], in1=before[:, c, :],
                                                            op0=ALU.mult, op1=ALU.add)
                    last.then_inc(mixed_ready, 1)

                def main(i, u):
                    n1 = 2 * i + (u + 1)
                    mix(i, u)
                    wait_at(dve, relu_ready, n1, ready)
                    dve.tensor_tensor(act2[:], pk[:], relu[:], ALU.mult).then_inc(act2_ready, 1)
                    wait_at(dve, gate_ready, n1, ready)
                    wait_at(dve, pv_ready, n1, ready)
                    dve.tensor_tensor(prod[:], pv[:], gate[:], ALU.mult).then_inc(prod_ready, 1)
                    wait_at(dve, prod_ready, n1 + 1, ready)
                    x = x_all[:, bass.ds(2 * i + u, 1)].rearrange("p g t d -> p (g t d)")
                    dve.scalar_tensor_tensor(out=x, in0=prod[:].rearrange("p t d -> p (t d)"), scalar=0.5, in1=x,
                                             op0=ALU.mult, op1=ALU.add).then_inc(out_ready, 1)

                dve.memset(norm.xT[:, :, :, 0:1], 0.0).then_inc(lead_clear, 1)
                dve.sem_inc(prod_ready, 1)
                dve.wait_ge(w_landed, 64)
                dve.wait_ge(lead_clear, 1)
                first(0, 0)
                with dve.Fori(0, last_i) as i:
                    for u in range(2):
                        first(*ahead(i, u))
                        main(i, u)
                first(last_i, 1)
                main(last_i, 0)
                main(last_i, 1)

            @block.gpsimd
            def _(pool):
                with pool.Fori(0, GROUPS // 2) as i:
                    for u in range(2):
                        norm.root(pool, ready, const, i, u)

            @block.scalar
            def _(act):
                def main(i, u):
                    n1 = 2 * i + (u + 1)
                    wait_at(act, mixed_ready, n1, ready)
                    act.sem_inc(norm.xT_free, 1)
                    wait_at(act, pk_ready, n1, ready)
                    act.activation(relu[:], pk[:], ACT.Relu).then_inc(relu_ready, 1)
                    wait_at(act, pr_ready, n1, ready)
                    act.activation(gate[:], pr[:], ACT.Sigmoid).then_inc(gate_ready, 1)

                act.sem_inc(norm.xT_free, 2)
                act.sem_inc(norm.xn_free, 2)
                act.sem_inc(norm.xT_ready, norm.banks)
                act.wait_ge(lead_clear, 1)
                norm.keep(act, ready, 0, 0)
                with act.Fori(0, last_i) as i:
                    for u in range(2):
                        norm.keep(act, ready, *ahead(i, u))
                        main(i, u)
                norm.keep(act, ready, last_i, 1)
                main(last_i, 0)
                main(last_i, 1)

            @block.tensor
            def _(pe):
                def main(i, u):
                    n1 = 2 * i + (u + 1)
                    wait_at(pe, mixed_ready, n1, ready)
                    for m in range(KC):
                        for c in range(KC):
                            last = pe.matmul(pk[:, m, :], wk[:, c, m * P:(m + 1) * P], mixed[:, u, 1, c, :],
                                             start=(c == 0), stop=(c == KC - 1))
                    last.then_inc(pk_ready, 1)
                    wait_at(pe, prod_ready, n1, ready)
                    for t in range(GT):
                        for c in range(KC):
                            last = pe.matmul(pr[:, t, :], mixed[:, u, 0, c, t * P:(t + 1) * P], wr[:, c, :],
                                             start=(c == 0), stop=(c == KC - 1))
                    last.then_inc(pr_ready, 1)
                    wait_at(pe, act2_ready, n1, ready)
                    for t in range(GT):
                        for c in range(KC):
                            last = pe.matmul(pv[:, t, :], act2[:, c, t * P:(t + 1) * P], wv[:, c, :],
                                             start=(c == 0), stop=(c == KC - 1))
                    last.then_inc(pv_ready, 1)

                pe.wait_ge(w_landed, 64)
                norm.turn(pe, ready, const, 0, 0)
                with pe.Fori(0, last_i) as i:
                    for u in range(2):
                        norm.turn(pe, ready, const, *ahead(i, u))
                        main(i, u)
                norm.turn(pe, ready, const, last_i, 1)
                main(last_i, 0)
                main(last_i, 1)
        s.clear()


MH = 16
HP = 32
MI = MH * HP
NS = 64
TILES = TOKENS // P
CH = SEQ // P
PC = 2 * NS + 2 * MH
TH = NS // 2
RMS2_EPS = 1e-6
TWO_PI = 6.283185307179586
PI = 3.1415925
HALF_PI = TWO_PI / 4
ROUND = 12582912.0


def mamba_stage(nc, const, x_all, gz_dram, w_dram, theta_dram, wout_dram, norm_dram, rows_dram):
    with ExitStack() as ctx:
        s = Space(nc, ctx, "mamba")
        ready = const.ready
        xs = s.sb("xs", [P, TILES, MI])
        bc = s.sb("bc", [P, TILES, 2 * NS])
        cum = s.sb("cum", [P, TILES, MH])
        la = s.sb("la", [P, TILES, MH])
        weight = s.sb("weight", [P, TILES, MH])
        to_end = s.sb("to_end", [P, TILES, MH])
        grown = s.sb("grown", [P, TILES, MH])
        across = s.sb("across", [P, TILES, MH])
        skip = s.sb("skip", [P, TILES, MH])
        mean1 = s.sb("mean1", [P, TILES])
        root1 = s.sb("root1", [P, TILES])
        rows = s.sb("rows", [P, 4 * NS + 3 * MH])
        rows_landed = s.sem("rows_landed")

        rctx = ctx.enter_context(ExitStack())
        raw = Space(nc, rctx, "mamba_raw").sb("raw", [P, TILES, PC + TH])
        unscale = Space(nc, rctx, "mamba_un").sb("unscale", [P, TILES])
        with ExitStack() as pctx:
            r = Space(nc, pctx, "mamba_proj")
            norm = Norm(r, x_all, banks=1, eps2=RMS2_EPS)
            w = r.sb("w", [P, KC, 2 * MI + PC])
            theta_w = r.sb("theta_w", [P, KC, TH])
            nrm = r.sb("nrm", [P, 2, KC])
            xi = r.sb("xi", [P, 2, KC, SEQ])
            sg = r.sb("sg", [P, 2, 2, MI])
            gz = r.sb("gz", [P, 2, 2, MI])
            pxz = r.ps("pxz", [P, 2, 2, MI])
            pbc = r.ps("pbc", [P, 2, 512])
            w_landed = r.sem("w_landed")
            xi_ready = r.sem("xi_ready")
            xz_psum, bc_psum = r.sem("xz_psum"), r.sem("bc_psum")
            sg_ready = r.sem("sg_ready")
            silu_ready = r.sem("silu_ready")
            raw_ready = r.sem("raw_ready")
            gz_stored = r.sems("gz_stored", 2)
            unscale_ready = r.sem("unscale_ready")
            gz_out = gz_dram.rearrange("(g t p) d -> g p t d", t=GT, p=P)
            last_i = GROUPS // 2 - 1

            with nc.Block() as block:

                @block.sync
                def _(sp):
                    sp.dma_start(w[:], w_dram).then_inc(w_landed, 16)
                    sp.dma_start(theta_w[:], theta_dram).then_inc(w_landed, 16)
                    sp.dma_start(nrm[:], norm_dram).then_inc(w_landed, 16)
                    sp.dma_start(rows[:], rows_dram.rearrange("(o n) -> o n", o=1).to_broadcast([P, 4 * NS + 3 * MH])
                                 ).then_inc(rows_landed, 16)
                    with sp.Fori(0, GROUPS) as n:
                        for b in range(2):
                            wait_at(sp, silu_ready, 2 * GT * n + (4 * b + 8), ready)
                            sp.dma_start(gz_out[bass.ds(n, 1), :, 2 * b:2 * b + 2].rearrange("g p t d -> p (g t) d"), gz[:, b]
                                         ).then_inc(gz_stored[b], 16)
                    for b in range(2):
                        sp.wait_ge(gz_stored[b], 16 * GROUPS)

                @block.vector
                def _(dve):
                    def first(i, u):
                        norm.moments_of(dve, ready, i, u, 2 * i + u, False)
                        norm.normalise(dve, ready, i, u, 2 * i + u)
                        tiles = bass.ds(GT * (2 * i + u), GT)
                        dve.tensor_copy(mean1[:, tiles], norm.moments[:, u, :, 0])
                        dve.tensor_copy(root1[:, tiles], norm.work[:, u, 0, :])

                    def main(i, u, before):
                        n = 2 * i + u
                        for t in range(GT):
                            tile = GT * n + t
                            v = t % 2
                            if before and v == 0:
                                wait_at(dve, gz_stored[t // 2], 16 * n, ready)
                            for a in range(2):
                                wait_at(dve, sg_ready, 2 * tile + (a + 1), ready)
                                out = gz[:, t // 2, v, :] if a else xs[:, bass.ds(tile, 1), :].rearrange("p o d -> p (o d)")
                                dve.tensor_tensor(out, pxz[:, v, a, :], sg[:, v, a, :], ALU.mult
                                                  ).then_inc(silu_ready, 1)

                    dve.sem_inc(silu_ready, 4)
                    first(0, 0)
                    first(0, 1)
                    main(0, 0, False)
                    first(1, 0)
                    main(0, 1, True)
                    with dve.Fori(1, last_i) as i:
                        for u in range(2):
                            first(*ahead(i, u))
                            main(i, u, True)
                    first(last_i, 1)
                    main(last_i, 0, True)
                    main(last_i, 1, True)

                @block.gpsimd
                def _(pool):
                    pool.memset(norm.eps2_tile[:], RMS2_EPS).then_inc(norm.eps2_set, 1)
                    pool.wait_ge(norm.eps2_set, 1)
                    with pool.Fori(0, GROUPS // 2) as i:
                        for u in range(2):
                            norm.root(pool, ready, const, i, u)
                            pool.tensor_tensor(unscale[:, bass.ds(GT * (2 * i + u), GT)], norm.work[:, u, 1, :],
                                               norm.work[:, u, 2, :], ALU.mult).then_inc(unscale_ready, 1)

                @block.scalar
                def _(act):
                    def first(i, u):
                        norm.keep(act, ready, i, u, count=False)
                        for c in range(KC):
                            last = act.activation(xi[:, u, c, :], norm.turned[:, 0, c, :], ACT.Identity,
                                                  scale=nrm[:, 0, c:c + 1], bias=nrm[:, 1, c:c + 1])
                        last.then_inc(norm.xT_ready, 1)

                    def main(i, u):
                        n = 2 * i + u
                        for t in range(GT):
                            tile = GT * n + t
                            v = t % 2
                            for a in range(2):
                                wait_at(act, xz_psum, 2 * tile + (a + 1), ready)
                                wait_at(act, silu_ready, 2 * tile + (a + 1), ready)
                                act.activation(sg[:, v, a, :], pxz[:, v, a, :], ACT.Sigmoid).then_inc(sg_ready, 1)
                            wait_at(act, bc_psum, tile + 1, ready)
                            act.activation(raw[:, bass.ds(tile, 1), :].rearrange("p o d -> p (o d)"),
                                           pbc[:, v, 0:PC + TH], ACT.Copy).then_inc(raw_ready, 1)
                        act.sem_inc(norm.xT_free, 1)

                    act.sem_inc(norm.xT_free, 2)
                    act.sem_inc(norm.xn_free, 2)
                    act.sem_inc(norm.xT_ready, 1)
                    act.sem_inc(raw_ready, 2)
                    act.wait_ge(w_landed, 48)
                    first(0, 0)
                    with act.Fori(0, last_i) as i:
                        for u in range(2):
                            first(*ahead(i, u))
                            main(i, u)
                    first(last_i, 1)
                    main(last_i, 0)
                    main(last_i, 1)

                @block.tensor
                def _(pe):
                    def main(i, u):
                        n = 2 * i + u
                        norm.kept(pe, ready, i, u)
                        for t in range(GT):
                            tile = GT * n + t
                            v = t % 2
                            tokens = slice(t * P, (t + 1) * P)
                            for a in range(2):
                                wait_at(pe, silu_ready, 2 * tile + (a + 1), ready)
                                for c in range(KC):
                                    last = pe.matmul(pxz[:, v, a, :], xi[:, u, c, tokens], w[:, c, a * MI:(a + 1) * MI],
                                                     start=(c == 0), stop=(c == KC - 1))
                                last.then_inc(xz_psum, 1)
                            wait_at(pe, raw_ready, tile + 1, ready)
                            for c in range(KC):
                                pe.matmul(pbc[:, v, 0:PC], xi[:, u, c, tokens], w[:, c, 2 * MI:],
                                          start=(c == 0), stop=(c == KC - 1))
                            for c in range(KC):
                                last = pe.matmul(pbc[:, v, PC:PC + TH], norm.xT[:, u, c, tokens], theta_w[:, c, :],
                                                 start=(c == 0), stop=(c == KC - 1))
                            last.then_inc(bc_psum, 1)

                    pe.wait_ge(w_landed, 48)
                    norm.turn(pe, ready, const, 0, 0)
                    with pe.Fori(0, last_i) as i:
                        for u in range(2):
                            main_first = ahead(i, u)
                            norm.kept(pe, ready, i, u)
                            norm.turn(pe, ready, const, *main_first)
                            main(i, u)
                    norm.kept(pe, ready, last_i, 0)
                    norm.turn(pe, ready, const, last_i, 1)
                    main(last_i, 0)
                    main(last_i, 1)
            r.clear()

        with ExitStack() as ectx:
            r = Space(nc, ectx, "mamba_each")
            tri = const.tri
            v = r.sb("v", [P, TILES, TH])
            vp = r.sb("vp", [P, BATCH, CH, TH])
            e = r.sb("e", [P, TILES, MH])
            q = r.sb("q", [P, TILES, MH])
            f = r.sb("f", [P, TILES, MH])
            dt = r.sb("dt", [P, TILES, MH])
            lam = r.sb("lam", [P, TILES, MH])
            w2 = r.sb("w2", [P, TILES, MH])
            ends = r.sb("ends", [P, TILES, MH])
            neg_a = r.sb("neg_a", [P, MH])
            tmean = r.sb("tmean", [P, TILES])
            phi = r.sb("phi", [P, TILES, 2, TH])
            turns = r.sb("turns", [P, TILES, 2, TH])
            ms = r.sb("ms", [P, TILES, 2])
            rms = r.sb("rms", [P, TILES, 2])
            big = r.sb("big", [P, TILES, 2, TH])
            big2 = turns
            gd = r.sb("gd", [P, TILES])
            pphi = r.ps("pphi", [P, 2, 512])
            pcum = r.ps("pcum", [P, 512])
            pend = r.ps("pend", [P, 512])
            pshift = r.ps("pshift", [P, 512])
            chain = r.sem("chain")
            a_ready, neg_ready, lam_ready, sin_ready = r.sem("a_ready"), r.sem("neg_ready"), r.sem("lam_ready"), r.sem("sin_ready")
            v_ready, sums_ready, gr_ready = r.sem("v_ready"), r.sem("sums_ready"), r.sem("gr_ready")
            abs_ready, angle_ready, cum_ready = r.sem("abs_ready"), r.sem("angle_ready"), r.sem("cum_ready")
            ms_ready, rms_ready = r.sem("ms_ready"), r.sem("rms_ready")
            dt_bias, a_log, d_row = (rows[:, 4 * NS + k * MH:4 * NS + (k + 1) * MH] for k in range(3))

            def over_tiles(row, n):
                return row.unsqueeze(1).to_broadcast([P, TILES, n])

            with nc.Block() as block:

                @block.scalar
                def _(act):
                    act.wait_ge(rows_landed, 16)
                    act.activation(neg_a[:], a_log, ACT.Exp).then_inc(a_ready, 1)
                    act.wait_ge(abs_ready, 1)
                    act.activation(e[:], e[:], ACT.Exp, scale=-1.0).then_inc(neg_ready, 1)
                    act.activation(lam[:], raw[:, :, 2 * NS + MH:PC], ACT.Sigmoid).then_inc(lam_ready, 1)
                    act.wait_ge(angle_ready, 1)
                    act.activation(phi[:], phi[:], ACT.Sin).then_inc(sin_ready, 1)
                    act.wait_ge(cum_ready, 1)
                    act.activation(grown[:], cum[:], ACT.Exp).then_inc(gr_ready, 1)
                    act.activation(to_end[:], to_end[:], ACT.Exp).then_inc(gr_ready, 1)
                    act.activation(across[:], ends[:], ACT.Exp).then_inc(gr_ready, 1)

                @block.gpsimd
                def _(pool):
                    pool.wait_ge(ms_ready, 1)
                    pool.tensor_tensor(rms[:], ms[:], const.minus_half[:].rearrange("p (a b) -> p a b", b=2), ALU.pow
                                       ).then_inc(rms_ready, 1)

                @block.tensor
                def _(pe):
                    pe.wait_ge(v_ready, 1)
                    flat_v, flat_vp = v[:].rearrange("p t d -> p (t d)"), vp[:].rearrange("p b t d -> p (b t d)")
                    flat_la, flat_w2 = la[:].rearrange("p t d -> p (t d)"), w2[:].rearrange("p t d -> p (t d)")
                    for k in range(2):
                        part = slice(512 * k, 512 * k + 512)
                        pe.matmul(pphi[:, k, :], const.tri[:], flat_v[:, part], start=True, stop=False)
                        pe.matmul(pphi[:, k, :], const.ones[:], flat_vp[:, part], start=False, stop=True)
                    pe.matmul(pcum[:], const.tri[:], flat_la, start=True, stop=True)
                    pe.matmul(pend[:], const.ones[:], flat_la, start=True, stop=True)
                    pe.matmul(pshift[:], const.shift[:], flat_w2, start=True, stop=False)
                    w2_next = w2[:].rearrange("p (b t) h -> p b t h", t=CH)[:, :, 1:CH, :]
                    shift_out = pshift[:].rearrange("p (b t h) -> p b t h", t=CH, h=MH)[:, :, 0:CH - 1, :]
                    pe.matmul(shift_out, const.wrap[:], w2_next, start=False, stop=True).then_inc(sums_ready, 1)

                @block.vector
                def _(dve):
                    steps = 0

                    def link(ins, also=None):
                        nonlocal steps
                        if also is not None:
                            ins.then_inc(also, 1)
                            dve.wait_ge(also, 1)
                            return
                        steps += 1
                        ins.then_inc(chain, 1)
                        dve.wait_ge(chain, steps)

                    tt, ts, stt = dve.tensor_tensor, dve.tensor_scalar, dve.scalar_tensor_tensor
                    dve.wait_ge(rows_landed, 16)
                    link(tt(dt[:], raw[:, :, 2 * NS:2 * NS + MH], over_tiles(dt_bias, MH), ALU.add))
                    link(ts(q[:], dt[:], -1.0, None, ALU.mult))
                    link(tt(e[:], dt[:], q[:], ALU.max), abs_ready)
                    link(ts(dt[:], dt[:], 0.0, None, ALU.max))
                    bcr = raw[:, :, 0:2 * NS]
                    halves = bcr.rearrange("p t (a d) -> p t a d", a=2)
                    link(tt(bc[:], bcr, bcr, ALU.mult))
                    link(dve.tensor_reduce(ms[:], bc[:].rearrange("p t (a d) -> p t a d", a=2), AX.X, ALU.add))
                    link(ts(ms[:], ms[:], 1.0 / NS, RMS2_EPS, ALU.mult, ALU.add), ms_ready)
                    dve.wait_ge(neg_ready, 1)
                    link(ts(f[:], e[:], 2.0, None, ALU.add))
                    link(dve.reciprocal(f[:], f[:]))
                    link(tt(e[:], e[:], f[:], ALU.mult))
                    link(tt(q[:], e[:], e[:], ALU.mult))
                    link(ts(f[:], q[:], 1.0 / 17, None, ALU.mult))
                    for k in range(15, 1, -2):
                        link(stt(out=f[:], in0=f[:], scalar=1.0 / k, in1=q[:], op0=ALU.add, op1=ALU.mult))
                    link(stt(out=f[:], in0=f[:], scalar=1.0, in1=e[:], op0=ALU.add, op1=ALU.mult))
                    link(stt(out=dt[:], in0=f[:], scalar=2.0, in1=dt[:], op0=ALU.mult, op1=ALU.add))
                    dve.wait_ge(a_ready, 1)
                    link(ts(neg_a[:], neg_a[:], -1.0, None, ALU.mult))
                    link(tt(la[:], dt[:], over_tiles(neg_a[:], MH), ALU.mult))
                    link(dve.tensor_reduce(tmean[:], dt[:], AX.X, ALU.add))
                    link(stt(out=tmean[:], in0=tmean[:], scalar=1.0 / MH, in1=unscale[:], op0=ALU.mult, op1=ALU.mult))
                    link(tt(v[:], raw[:, :, PC:], tmean[:].unsqueeze(2).to_broadcast([P, TILES, TH]), ALU.mult))
                    v4 = v[:].rearrange("p (b t) d -> p b t d", t=CH)
                    link(dve.memset(vp[:, :, 0, :], 0.0))
                    for t in range(1, CH):
                        link(tt(vp[:, :, t, :], vp[:, :, t - 1, :], v4[:, :, t - 1, :], ALU.add))
                    dve.wait_ge(lam_ready, 1)
                    link(tt(weight[:], dt[:], lam[:], ALU.mult))
                    link(tt(w2[:], dt[:], weight[:], ALU.subtract), v_ready)
                    dve.wait_ge(rms_ready, 1)
                    bc4 = bc[:].rearrange("p t (a d) -> p t a d", a=2)
                    link(tt(bc4, halves, rms[:].unsqueeze(3).to_broadcast([P, TILES, 2, NS]), ALU.mult))
                    link(tt(bc[:], bc[:], over_tiles(rows[:, 0:2 * NS], 2 * NS), ALU.mult))
                    link(tt(bc[:], bc[:], over_tiles(rows[:, 2 * NS:4 * NS], 2 * NS), ALU.add))
                    dve.wait_ge(sums_ready, 1)
                    phase = pphi[:].rearrange("p a (t d) -> p (a t) d", d=TH)
                    link(dve.tensor_copy(phi[:, :, 0, :], phase))
                    link(ts(phi[:, :, 1, :], phi[:, :, 0, :], HALF_PI, None, ALU.add))
                    link(ts(turns[:], phi[:], 1.0 / TWO_PI, ROUND, ALU.mult, ALU.add))
                    link(ts(turns[:], turns[:], ROUND, None, ALU.subtract))
                    for part in (6.28125, 0.0019340515136718750, TWO_PI - 6.28125 - 0.0019340515136718750):
                        link(stt(out=phi[:], in0=turns[:], scalar=-part, in1=phi[:], op0=ALU.mult, op1=ALU.add))
                    link(ts(phi[:], phi[:], PI, -PI, ALU.min, ALU.max), angle_ready)
                    link(dve.tensor_copy(cum[:], pcum[:].rearrange("p (t h) -> p t h", h=MH)))
                    link(dve.tensor_copy(ends[:], pend[:].rearrange("p (t h) -> p t h", h=MH)))
                    link(tt(to_end[:], ends[:], cum[:], ALU.subtract), cum_ready)
                    nxt = pshift[:].rearrange("p (t h) -> p t h", h=MH)
                    link(dve.tensor_copy(w2[:], nxt))
                    link(tt(weight[:], weight[:], w2[:], ALU.add))
                    dve.wait_ge(sin_ready, 1)
                    sine = phi[:, :, 0, :].unsqueeze(2).to_broadcast([P, TILES, 2, TH])
                    cosine = phi[:, :, 1, :].unsqueeze(2).to_broadcast([P, TILES, 2, TH])
                    re, im = bc4[:, :, :, 0:TH], bc4[:, :, :, TH:NS]
                    link(tt(big[:], im, sine, ALU.mult))
                    link(tt(big2[:], re, sine, ALU.mult))
                    link(tt(re, re, cosine, ALU.mult))
                    link(tt(im, im, cosine, ALU.mult))
                    link(tt(re, re, big[:], ALU.subtract))
                    link(tt(im, im, big2[:], ALU.add))
                    dot = big[:].rearrange("p t a d -> p t (a d)")
                    link(tt(dot, bc[:, :, 0:NS], bc[:, :, NS:2 * NS], ALU.mult))
                    link(dve.tensor_reduce(gd[:], dot, AX.X, ALU.add))
                    link(tt(w2[:], w2[:], gd[:].unsqueeze(2).to_broadcast([P, TILES, MH]), ALU.mult))
                    link(tt(skip[:], over_tiles(d_row, MH), w2[:], ALU.subtract))
                    dve.wait_ge(gr_ready, 3)
                    link(tt(to_end[:], to_end[:], weight[:], ALU.mult))
            r.clear()
        rctx.close()

        with ExitStack() as sctx:
            r = Space(nc, sctx, "mamba_scan")
            wout = r.sb("wout", [P, CH, D])
            zg = r.sb("zg", [P, 2, 2, MI])
            bcs = r.sb("bcs", [P, CH, 2 * NS])
            bcT = r.sb("bcT", [NS, CH, 2, P])
            steps_la = r.sb("steps_la", [P, 2, MH, P])
            decay = r.sb("decay", [P, MH, P])
            mat = r.sb("mat", [P, MH, P])
            gsb = r.sb("gsb", [P, 2, P])
            xw = r.sb("xw", [P, 2, MH, HP])
            xe = r.sb("xe", [P, 2, MH, HP])
            xd = r.sb("xd", [P, 2, MH, HP])
            state = r.sb("state", [NS, MH, HP])
            y = r.sb("y", [P, 2, MH, HP])
            yT = r.sb("yT", [P, MI // P, P])
            un = r.sb("un", [P, D])
            p_la = r.ps("p_la", [P, MH, P])
            p_y = r.ps("p_y", [P, 512])
            p_in = r.ps("p_in", [P, 512])
            p_st = r.ps("p_st", [P, 512])
            p_m = r.ps("p_m", [P, 512])
            wout_landed = r.sem("wout_landed")
            zg_landed = r.sems("zg_landed", 2)
            names = ("bcs_ready", "bcT_psum", "bcT_ready", "la_ready", "xw_ready", "xe_ready", "xd_ready", "sum_psum", "diff_ready",
                     "exp_ready", "g_psum", "g_ready", "mat_ready", "in_psum", "st_psum", "state_ready", "scaled_ready",
                     "intra_psum", "added_ready", "skip_ready", "y_ready", "yT_psum", "yT_ready", "out_psum", "un_ready",
                     "half_ready", "out_ready", "grown_ready", "zg_free0", "zg_free1")
            q = {k: r.sem(k) for k in names}

            with nc.Block() as block:

                @block.sync
                def _(sp):
                    zg_in = gz_dram.rearrange("(g t p) d -> g p t d", t=CH, p=P)
                    sp.dma_start(wout[:], wout_dram).then_inc(wout_landed, 16)
                    with sp.Fori(0, BATCH) as n:
                        for b in range(2):
                            wait_at(sp, q[f"zg_free{b}"], n + 1, ready)
                            sp.dma_start(zg[:, b], zg_in[bass.ds(n, 1), :, 2 * b:2 * b + 2].rearrange("g p t d -> p (g t) d")
                                         ).then_inc(zg_landed[b], 16)

                @block.gpsimd
                def _(pool):
                    with pool.Fori(0, BATCH) as n:
                        for t in range(CH):
                            k = CH * n + t
                            v = t % 2
                            wait_at(pool, q["y_ready"], k + 1, ready)
                            part = la[:, bass.ds(k, 1), :].rearrange("p o h -> p (o h)")
                            pool.tensor_tensor(steps_la[:, v], part.unsqueeze(2).to_broadcast([P, MH, P]),
                                               const.tri[:].unsqueeze(1).to_broadcast([P, MH, P]), ALU.mult
                                               ).then_inc(q["la_ready"], 1)
                            x = xs[:, bass.ds(k, 1), :].rearrange("p o (h d) -> p (o h) d", h=MH)
                            for out, by, name in ((xe, to_end, "xe_ready"), (xw, weight, "xw_ready"),
                                                  (xd, skip, "xd_ready")):
                                fac = by[:, bass.ds(k, 1), :].rearrange("p o h -> p (o h)")
                                pool.tensor_tensor(out[:, v], x, fac.unsqueeze(2).to_broadcast([P, MH, HP]), ALU.mult
                                                   ).then_inc(q[name], 1)

                @block.scalar
                def _(act):
                    act.sem_inc(q["bcT_ready"], 1)
                    act.sem_inc(q["yT_ready"], 1)
                    act.sem_inc(q["g_ready"], 1)
                    with act.Fori(0, BATCH) as n:
                        wait_at(act, q["state_ready"], CH * n + 1, ready)
                        act.activation(bcs[:], bc[:, bass.ds(CH * n, CH), :], ACT.Copy).then_inc(q["bcs_ready"], 1)
                        for half in range(2):
                            wait_at(act, q["bcT_psum"], 2 * n + (half + 1), ready)
                            act.activation(bcT[:, 2 * half:2 * half + 2], p_m[0:NS, :].rearrange("p (t a n) -> p t a n", t=2, a=2),
                                           ACT.Copy).then_inc(q["bcT_ready"], 1)
                        for t in range(CH):
                            k = CH * n + t
                            v = t % 2
                            wait_at(act, q["g_psum"], k + 1, ready)
                            act.activation(gsb[:, v], p_m[:, 0:P], ACT.Copy).then_inc(q["g_ready"], 1)
                            wait_at(act, q["diff_ready"], k + 2, ready)
                            act.activation(decay[:], decay[:], ACT.Exp).then_inc(q["exp_ready"], 1)
                            wait_at(act, q["yT_psum"], k + 1, ready)
                            act.activation(yT[:], p_m[:].rearrange("p (a n) -> p a n", n=P), ACT.Copy
                                           ).then_inc(q["yT_ready"], 1)

                @block.tensor
                def _(pe):
                    pe.wait_ge(wout_landed, 16)
                    with pe.Fori(0, BATCH) as n:
                        for half in range(2):
                            if half == 0:
                                wait_at(pe, q["bcs_ready"], n + 1, ready)
                                wait_at(pe, q["half_ready"], CH * n + 1, ready)
                            wait_at(pe, q["bcT_ready"], 2 * n + (half + 1), ready)
                            for t in range(2):
                                for a in range(2):
                                    last = pe.transpose(p_m[0:NS, (2 * t + a) * P:(2 * t + a + 1) * P],
                                                        bcs[:, 2 * half + t, a * NS:(a + 1) * NS], const.ident[:])
                            last.then_inc(q["bcT_psum"], 1)
                        wait_at(pe, q["bcT_ready"], 2 * n + 3, ready)
                        for t in range(CH):
                            k = CH * n + t
                            v = t % 2
                            if t:
                                wait_at(pe, q["half_ready"], k + 1, ready)
                            pe.matmul(p_m[:, 0:P], bcT[:, t, 0, :], bcT[:, t, 1, :], start=True, stop=True
                                      ).then_inc(q["g_psum"], 1)
                            wait_at(pe, q["la_ready"], k + 1, ready)
                            wait_at(pe, q["diff_ready"], k + 1, ready)
                            for b in range(4):
                                heads = slice(4 * b, 4 * b + 4)
                                pe.matmul(p_la[:, heads, :], const.ones[:], steps_la[:, v, heads, :], start=True, stop=False)
                                last = pe.matmul(p_la[:, heads, :], const.ident_b[:],
                                                 const.never[:].unsqueeze(1).to_broadcast([P, 4, P]), start=False, stop=True)
                            last.then_inc(q["sum_psum"], 1)
                            wait_at(pe, q["state_ready"], k + 1, ready)
                            wait_at(pe, q["scaled_ready"], k + 1, ready)
                            pe.matmul(p_in[:], bcT[:, t, 1, :], state[:].rearrange("p h d -> p (h d)"), start=True, stop=True
                                      ).then_inc(q["in_psum"], 1)
                            wait_at(pe, q["xe_ready"], k + 1, ready)
                            pe.matmul(p_st[0:NS, :], bcs[:, t, 0:NS], xe[:, v].rearrange("p h d -> p (h d)"), start=True, stop=True
                                      ).then_inc(q["st_psum"], 1)
                            wait_at(pe, q["xw_ready"], k + 1, ready)
                            wait_at(pe, q["mat_ready"], k + 1, ready)
                            wait_at(pe, q["added_ready"], k + 1, ready)
                            for h in range(MH):
                                last = pe.matmul(p_y[:, h * HP:(h + 1) * HP], mat[:, h, :], xw[:, v, h, :], start=True, stop=True)
                            last.then_inc(q["intra_psum"], 1)
                            wait_at(pe, q["y_ready"], k + 3, ready)
                            for a in range(MI // P):
                                last = pe.transpose(p_m[:, a * P:(a + 1) * P],
                                                    y[:, v, a * (P // HP):(a + 1) * (P // HP), :].rearrange("p h d -> p (h d)"),
                                                    const.ident[:])
                            last.then_inc(q["yT_psum"], 1)
                            wait_at(pe, q["yT_ready"], k + 2, ready)
                            for a in range(MI // P):
                                last = pe.matmul(p_m[:, 0:D], yT[:, a, :], wout[:, a, :], start=(a == 0), stop=(a == MI // P - 1))
                            last.then_inc(q["out_psum"], 1)

                @block.vector
                def _(dve):
                    tt, ts, stt = dve.tensor_tensor, dve.tensor_scalar, dve.scalar_tensor_tensor
                    dve.memset(state[:], 0.0).then_inc(q["state_ready"], 1)
                    dve.sem_inc(q["diff_ready"], 1)
                    dve.sem_inc(q["scaled_ready"], 1)
                    dve.sem_inc(q["added_ready"], 1)
                    dve.sem_inc(q["half_ready"], 1)
                    dve.sem_inc(q["y_ready"], 2)

                    def of(tensor, k):
                        return tensor[:, bass.ds(k, 1), :].rearrange("p o h -> p (o h)")

                    dve.sem_inc(q["zg_free0"], 1)
                    dve.sem_inc(q["zg_free1"], 1)
                    with dve.Fori(0, BATCH) as n:
                        for t in range(CH):
                            k = CH * n + t
                            v = t % 2
                            wait_at(dve, q["sum_psum"], k + 1, ready)
                            tt(decay[:], p_la[:], of(cum, k).unsqueeze(2).to_broadcast([P, MH, P]), ALU.subtract
                               ).then_inc(q["diff_ready"], 1)
                            wait_at(dve, q["in_psum"], k + 1, ready)
                            tt(y[:, v], p_in[:].rearrange("p (h d) -> p h d", h=MH),
                               of(grown, k).unsqueeze(2).to_broadcast([P, MH, HP]), ALU.mult).then_inc(q["scaled_ready"], 1)
                            wait_at(dve, q["st_psum"], k + 1, ready)
                            if t < CH - 1:
                                tt(state[:], state[:], across[0:NS, bass.ds(k, 1), :].rearrange("p o h -> p (o h)")
                                   .unsqueeze(2).to_broadcast([NS, MH, HP]), ALU.mult).then_inc(q["grown_ready"], 1)
                                wait_at(dve, q["grown_ready"], (CH - 1) * n + (t + 1), ready)
                                tt(state[:], state[:], p_st[0:NS, :].rearrange("p (h d) -> p h d", h=MH), ALU.add
                                   ).then_inc(q["state_ready"], 1)
                            else:
                                dve.memset(state[:], 0.0).then_inc(q["state_ready"], 1)
                            wait_at(dve, q["exp_ready"], k + 1, ready)
                            wait_at(dve, q["g_ready"], k + 2, ready)
                            tt(mat[:], decay[:], gsb[:, v].unsqueeze(1).to_broadcast([P, MH, P]), ALU.mult
                               ).then_inc(q["mat_ready"], 1)
                            wait_at(dve, q["xd_ready"], k + 1, ready)
                            wait_at(dve, q["scaled_ready"], k + 2, ready)
                            tt(y[:, v], y[:, v], xd[:, v], ALU.add).then_inc(q["skip_ready"], 1)
                            x = x_all[:].rearrange("p g t d -> p (g t) d")[:, bass.ds(k, 1), :].rearrange("p o d -> p (o d)")
                            ts(un[:], x, mean1[:, bass.ds(k, 1)], root1[:, bass.ds(k, 1)], ALU.subtract, ALU.mult
                               ).then_inc(q["un_ready"], 1)
                            wait_at(dve, q["un_ready"], k + 1, ready)
                            tt(x, x, un[:], ALU.add).then_inc(q["out_ready"], 1)
                            wait_at(dve, q["skip_ready"], k + 1, ready)
                            wait_at(dve, q["intra_psum"], k + 1, ready)
                            tt(y[:, v], y[:, v], p_y[:].rearrange("p (h d) -> p h d", h=MH), ALU.add
                               ).then_inc(q["added_ready"], 1)
                            wait_at(dve, q["added_ready"], k + 2, ready)
                            if v == 0:
                                wait_at(dve, zg_landed[t // 2], 16 * n + 16, ready)
                            tt(y[:, v], y[:, v], zg[:, t // 2, v].rearrange("p (h d) -> p h d", h=MH), ALU.mult
                               ).then_inc(q["y_ready"], 1)
                            wait_at(dve, q["out_psum"], k + 1, ready)
                            wait_at(dve, q["out_ready"], k + 1, ready)
                            tt(x, x, p_m[:, 0:D], ALU.add).then_inc(q["half_ready"], 1)
                            if v:
                                dve.sem_inc(q[f"zg_free{t // 2}"], 1)
            r.clear()
        s.clear()


def build(nc, a, out):
    def dram(name, width):
        return nc.dram_tensor(name, (TOKENS, width), F32, kind="Internal").ap()

    x1, x2, xn, gz = dram("x1", D), dram("x2", D), dram("xn", D), dram("gz", MI)
    with ExitStack() as ctx:
        const = Constants(nc, ctx)
        lasting = Space(nc, ctx, "all")
        x_all = lasting.sb("x", [P, GROUPS, GT, D])
        experts = (a["router"], a["w1"], a["b1"], a["w2"], a["b2"])
        mixer = (a["rwkv_r"], a["rwkv_k"], a["rwkv_v"], a["mu"])
        moe_stage(nc, lasting, const, "moe_a", True, x_all, a["x"], x1, xn, *experts)
        attention_stage(nc, const, x_all, x1, x2, a["wqkv"], a["wo"], a["attn_norm"], a["gamma"])
        moe_stage(nc, lasting, const, "moe_b", False, x_all, None, x2, xn, *experts)
        rwkv_stage(nc, const, "rwkv_a", True, x_all, x2, None, *mixer)
        mamba_stage(nc, const, x_all, gz, a["in_proj"], a["theta"], a["out_proj"], a["mamba_norm"], a["rows"])
        rwkv_stage(nc, const, "rwkv_b", False, x_all, None, out, *mixer)


def kernel(**inputs):
    import numpy as np
    import concourse.bacc as bacc
    from concourse.bass_utils import run_bass_kernel_spmd

    a = {k: np.asarray(v) for k, v in inputs.items()}
    L0, F0, L1, F1 = "L0_attn_", "L0_ffn_", "L1_attn_", "L1_ffn_"

    def by_chunk(w):
        return w.reshape(w.shape[0] // P, P, -1).transpose(1, 0, 2)

    def columns(*vectors):
        return np.stack(vectors).reshape(len(vectors), -1, P).transpose(2, 0, 1)

    E, S, M, K = EXPERTS, SLOTS, HID, YK
    layout = {
        "x": a[L0 + "tokens"].reshape(TOKENS, D),
        "router": by_chunk(a[F0 + "Wr"].T),
        "w1": a[F0 + "W1"].reshape(E, S, KC, P, M).transpose(0, 3, 2, 1, 4).reshape(E, P, KC, S * M),
        "b1": a[F0 + "b1"].reshape(E, HC, P).transpose(2, 0, 1),
        "w2": a[F0 + "W2"].reshape(E, HC, P, K).transpose(0, 2, 1, 3),
        "b2": a[F0 + "b2"].reshape(E, D),
        "wqkv": by_chunk(np.concatenate([a[L0 + "Wq"], a[L0 + "Wkv"]], 1)),
        "wo": by_chunk(a[L0 + "Wo"]),
        "attn_norm": columns(a[L0 + "norm_w"])[:, 0],
        "gamma": columns(a[L0 + "q_gamma"], a[L0 + "k_gamma"]),
        "rwkv_r": by_chunk(a[F1 + "W_r"].T),
        "rwkv_k": by_chunk(a[F1 + "W_k"].T),
        "rwkv_v": by_chunk(a[F1 + "W_v"].T),
        "mu": columns(a[F1 + "mu_r"], a[F1 + "mu_k"]),
        "in_proj": by_chunk(a[L1 + "in_proj_w"]),
        "theta": by_chunk(a[L1 + "theta_w"]),
        "out_proj": by_chunk(a[L1 + "out_proj_w"]),
        "mamba_norm": columns(a[L1 + "norm_scale"], a[L1 + "norm_bias"]),
        "rows": np.concatenate([a[L1 + n] for n in ("bcB_scale", "bcC_scale", "B_bias", "C_bias", "dt_bias", "A_log", "D")]),
    }
    nc = bacc.Bacc("TRN2", target_bir_lowering=False, num_devices=1)
    arrays, aps = {}, {}
    for name, value in layout.items():
        arrays["in_" + name] = np.ascontiguousarray(value)
        aps[name] = nc.dram_tensor("in_" + name, value.shape, mybir.dt.from_np(value.dtype), kind="ExternalInput").ap()
    out = nc.dram_tensor("out", (TOKENS, D), F32, kind="ExternalOutput").ap()
    build(nc, aps, out)
    result = run_bass_kernel_spmd(nc, [arrays], core_ids=[0])
    return result.results[0]["out"].reshape(BATCH, SEQ, D)
```

```python
from contextlib import ExitStack

import concourse.bass as bass
from concourse import mybir

F32 = mybir.dt.float32
BF16 = mybir.dt.bfloat16
U32 = mybir.dt.uint32
ALU = mybir.AluOpType
ACT = mybir.ActivationFunctionType
AX = mybir.AxisListType

P = 128
D = 256
KC = D // P
SEQ = 512
BATCH = 8
TOKENS = BATCH * SEQ
GT = SEQ // P
GROUPS = TOKENS // SEQ
LN_EPS = 1e-5


def wait_at(eng, sem, count, ready):
    if isinstance(count, int):
        eng.wait_ge(sem, count)
        return
    value = eng.snap(eng.to_reg(count))
    eng.wait_ge(ready, 1)
    eng.wait_ge(sem, value)


def ahead(i, u, k=1):
    return i + (u + k) // 2, (u + k) % 2


class Space:

    def __init__(self, nc, ctx, prefix):
        self.nc, self.ctx, self.prefix, self.counts = nc, ctx, prefix, []

    def sb(self, name, shape, dtype=F32):
        return self.ctx.enter_context(self.nc.sbuf_tensor(f"{self.prefix}_{name}", shape, dtype))

    def ps(self, name, shape, dtype=F32):
        return self.ctx.enter_context(self.nc.psum_tensor(f"{self.prefix}_{name}", shape, dtype))

    def sem(self, name):
        count = self.ctx.enter_context(self.nc.semaphore(f"{self.prefix}_{name}"))
        self.counts.append(count)
        return count

    def clear(self):
        numbers = sorted(c.num for c in self.counts)
        start = 0
        for k in range(1, len(numbers) + 1):
            if k == len(numbers) or numbers[k] != numbers[k - 1] + 1:
                self.nc.gpsimd.sem_clear(range(numbers[start], numbers[k - 1] + 1))
                start = k
        self.nc.all_engine_barrier()

    def sems(self, name, n):
        return [self.sem(f"{name}{k}") for k in range(n)]


class Constants:

    def __init__(self, nc, ctx):
        s = Space(nc, ctx, "const")
        self.ident = s.sb("ident", [P, P])
        self.ones = s.sb("ones", [P, P])
        self.flip = s.sb("flip", [P, P])
        self.first = s.sb("first", [P, P])
        self.last = s.sb("last", [P, P])
        self.tri = s.sb("tri", [P, P])
        self.shift = s.sb("shift", [P, P])
        self.wrap = s.sb("wrap", [P, P])
        self.ident_b = s.sb("ident_b", [P, P], BF16)
        self.never = s.sb("never", [P, P], BF16)
        self.pick = s.sb("pick", [3 * 16, 16, P], BF16)
        self.minus_half = s.sb("minus_half", [P, 64])
        self.half_offset = s.sb("half_offset", [P, 1])
        self.ready = s.sem("ready")
        made = s.sem("made")
        with nc.Block() as block:

            @block.gpsimd
            def _(pool):
                pool.memset(self.minus_half[:], -0.5)
                pool.memset(self.ones[:], 1.0).then_inc(made, 1)
                pool.memset(self.half_offset[:], float(TOKENS // 2)).then_inc(made, 1)
                pool.wait_ge(made, 2)
                pool.affine_select(out=self.half_offset[:], in_=self.half_offset[:], pattern=[[0, 1]],
                                   compare_op=ALU.is_ge, fill=0.0, base=-64, channel_multiplier=1)
                for out, pattern, base, cm in (
                    (self.ident, [[-1, P]], 0, 1),
                    (self.flip, [[1, P]], -(P - 1), 1),
                    (self.first, [[0, P]], 0, 1),
                    (self.last, [[0, P]], -(P - 1), 1),
                ):
                    pool.affine_select(out=out[:], in_=self.ones[:], pattern=pattern, compare_op=ALU.is_equal,
                                       fill=0.0, base=base, channel_multiplier=cm)
                pool.affine_select(out=self.tri[:], in_=self.ones[:], pattern=[[1, P]], compare_op=ALU.is_ge,
                                   fill=0.0, base=0, channel_multiplier=-1)
                pool.affine_select(out=self.shift[:], in_=self.ones[:], pattern=[[-1, P]], compare_op=ALU.is_equal,
                                   fill=0.0, base=-1, channel_multiplier=1)
                pool.affine_select(out=self.ident_b[:], in_=self.ones[:], pattern=[[-1, P]], compare_op=ALU.is_equal,
                                   fill=0.0, base=0, channel_multiplier=1)
                pool.memset(self.never[:], 0.0).then_inc(made, 1)
                pool.memset(self.wrap[:], 0.0).then_inc(made, 1)
                pool.memset(self.pick[:], 0.0).then_inc(made, 1)
                pool.wait_ge(made, 5)
                for part in range(3):
                    pool.affine_select(out=self.pick[:], in_=self.pick[:], pattern=[[-1, 16], [0, P]],
                                       compare_op=ALU.not_equal, fill=1.0, base=-16 * part, channel_multiplier=1
                                       ).then_inc(made, 1)
                    pool.wait_ge(made, 6 + part)
                pool.affine_select(out=self.never[:], in_=self.never[:], pattern=[[1, P]], compare_op=ALU.is_ge,
                                   fill=-1e30, base=0, channel_multiplier=-1)
                pool.affine_select(out=self.wrap[:], in_=self.wrap[:], pattern=[[-1, P]], compare_op=ALU.not_equal,
                                   fill=1.0, base=P - 1, channel_multiplier=1)
                pool.drain().then_inc(self.ready, 1)


class Norm:

    def __init__(self, s, x, banks=2, lead=0, unroll=2, turned=None, eps2=None):
        self.x = x
        self.unroll, self.eps2 = unroll, eps2
        self.lead, self.banks = lead, banks
        self.xn = s.sb("xn", [P, unroll, GT, D])
        self.stats = s.sb("stats", [P, unroll, GT, 6])
        self.moments = s.sb("moments", [P, unroll, GT, 2])
        self.var = s.sb("var", [P, unroll, GT])
        self.rstd = s.sb("rstd", [P, unroll, GT])
        self.xT = s.sb("xT", [P, unroll, KC, lead + SEQ])
        self.turned = s.ps("turned", [P, banks, KC, SEQ]) if turned is None else turned
        if eps2 is not None:
            self.eps2_tile = s.sb("eps2_tile", [P, GT])
            self.work = s.sb("work", [P, unroll, 3, GT])
            self.eps2_set = s.sem("eps2_set")
            self.norm2_step = s.sem("norm2_step")
        self.x_landed = s.sems("x_landed", 2)
        self.stats_ready = s.sem("stats_ready")
        self.moments_ready = s.sem("moments_ready")
        self.var_ready = s.sem("var_ready")
        self.rstd_ready = s.sem("rstd_ready")
        self.xn_ready = s.sem("xn_ready")
        self.xn_free = s.sem("xn_free")
        self.xn_stored = None
        self.turned_ready = s.sem("turned_ready")
        self.xT_ready = s.sem("xT_ready")
        self.xT_free = s.sem("xT_free")

    def load(self, sp, ready, x_dram, i, u, group):
        sp.dma_start(self.x[:, bass.ds(group, 1)].rearrange("p g t d -> p (g t) d"),
                     x_dram[bass.ds(group * SEQ, SEQ), :].rearrange("(t p) d -> p t d", p=P)
                     ).then_inc(self.x_landed[u], 16)

    def moments_of(self, dve, ready, i, u, group, loaded=True):
        n1 = self.unroll * i + (u + 1)
        if loaded:
            wait_at(dve, self.x_landed[u], 16 * i + 16, ready)
        x = self.x[:, bass.ds(group, 1)].rearrange("p g t d -> p (g t) d")
        for t in range(GT):
            last = dve.bn_stats(self.stats[:, u, t, :], x[:, t, :])
        last.then_inc(self.stats_ready, 1)
        wait_at(dve, self.stats_ready, n1, ready)
        for t in range(GT):
            last = dve.bn_aggr(self.moments[:, u, t, :], self.stats[:, u, t, :])
        last.then_inc(self.moments_ready, 1)
        wait_at(dve, self.moments_ready, n1, ready)
        dve.tensor_scalar(self.var[:, u, :], self.moments[:, u, :, 1], LN_EPS, None, ALU.add
                          ).then_inc(self.var_ready, 1)

    def root(self, pool, ready, const, i, u):
        n = self.unroll * i + u
        wait_at(pool, self.var_ready, n + 1, ready)
        half = const.minus_half[:, 0:GT]
        if self.eps2 is None:
            pool.tensor_tensor(self.rstd[:, u, :], self.var[:, u, :], half, ALU.pow).then_inc(self.rstd_ready, 1)
            return
        root, ms, fac = (self.work[:, u, k, :] for k in range(3))
        pool.tensor_tensor(root, self.var[:, u, :], half, ALU.pow).then_inc(self.norm2_step, 1)
        wait_at(pool, self.norm2_step, 5 * n + 1, ready)
        pool.tensor_tensor(ms, root, root, ALU.mult).then_inc(self.norm2_step, 1)
        wait_at(pool, self.norm2_step, 5 * n + 2, ready)
        pool.tensor_tensor(ms, ms, self.moments[:, u, :, 1], ALU.mult).then_inc(self.norm2_step, 1)
        wait_at(pool, self.norm2_step, 5 * n + 3, ready)
        pool.tensor_tensor(ms, ms, self.eps2_tile[:], ALU.add).then_inc(self.norm2_step, 1)
        wait_at(pool, self.norm2_step, 5 * n + 4, ready)
        pool.tensor_tensor(fac, ms, half, ALU.pow).then_inc(self.norm2_step, 1)
        wait_at(pool, self.norm2_step, 5 * n + 5, ready)
        pool.tensor_tensor(self.rstd[:, u, :], root, fac, ALU.mult).then_inc(self.rstd_ready, 1)

    def normalise(self, dve, ready, i, u, group):
        n1 = self.unroll * i + (u + 1)
        wait_at(dve, self.rstd_ready, n1, ready)
        wait_at(dve, self.xn_free, n1, ready)
        if self.xn_stored is not None:
            wait_at(dve, self.xn_stored, n1, ready)
        x = self.x[:, bass.ds(group, 1)].rearrange("p g t d -> p (g t) d")
        for t in range(GT):
            last = dve.tensor_scalar(self.xn[:, u, t, :], x[:, t, :], self.moments[:, u, t, 0:1],
                                     self.rstd[:, u, t:t + 1], ALU.subtract, ALU.mult)
        last.then_inc(self.xn_ready, 1)

    def turn(self, pe, ready, const, i, u):
        n1 = self.unroll * i + (u + 1)
        wait_at(pe, self.xn_ready, n1, ready)
        wait_at(pe, self.xT_ready, n1, ready)
        for c in range(KC):
            for t in range(GT):
                last = pe.transpose(self.turned[:, u % self.banks, c, t * P:(t + 1) * P],
                                    self.xn[:, u, t, c * P:(c + 1) * P], const.ident[:])
        last.then_inc(self.turned_ready, 1)

    def keep(self, act, ready, i, u, count=True):
        n1 = self.unroll * i + (u + 1)
        wait_at(act, self.turned_ready, n1, ready)
        act.sem_inc(self.xn_free, 1)
        wait_at(act, self.xT_free, n1, ready)
        copy = act.activation(self.xT[:, u, :, self.lead:], self.turned[:, u % self.banks], ACT.Copy)
        if count:
            copy.then_inc(self.xT_ready, 1)

    def kept(self, eng, ready, i, u):
        wait_at(eng, self.xT_ready, self.unroll * i + (u + 1 + self.banks), ready)


EXPERTS = 48
SLOTS = 4
HID = 256
HC = SLOTS * HID // P
YK = D // SLOTS
CAP = int(1.5 * TOKENS / EXPERTS)
EU = 4
HALF = TOKENS // 2
ROUNDS = CAP // 8


def moe_stage(nc, lasting, const, name, load, x_all, x_dram, acc_dram, xn_dram, wr_dram, w1_dram, b1_dram, w2_dram, b2_dram):
    with ExitStack() as ctx:
        s = Space(nc, ctx, name)
        ready = const.ready
        w1 = s.sb("w1", [P, EU, KC, SLOTS * HID])
        w2 = s.sb("w2", [P, EU, HC, YK])
        b2 = s.sb("b2", [1, EU, D])
        b1 = s.sb("b1", [P, EXPERTS, HC])
        b1_landed = s.sem("b1_landed")
        w_landed = s.sems("w_landed", EU)

        def fetch(sp, e, u):
            sp.dma_start(w1[:, u], w1_dram[bass.ds(e, 1)].rearrange("e p c n -> p (e c) n")).then_inc(w_landed[u], 16)
            sp.dma_start(w2[:, u], w2_dram[bass.ds(e, 1)].rearrange("e p c n -> p (e c) n")).then_inc(w_landed[u], 16)
            sp.dma_start(b2[:, u], b2_dram[bass.ds(e, 1), :]).then_inc(w_landed[u], 16)

        with ExitStack() as rctx:
            r = Space(nc, rctx, name + "_router")
            keep_vals = s.sb("sel_w", [P, EXPERTS])
            index = s.sb("index", [P, EXPERTS], U32)
            norm = Norm(r, x_all)
            wr = r.sb("wr", [P, KC, 64])
            logits = r.sb("logits", [P, HALF])
            vals = r.sb("vals", [P, CAP])
            idx = r.sb("idx", [P, CAP], U32)
            idxf = r.sb("idxf", [P, CAP])
            both = r.sb("both", [P, 2, P])
            swapped = r.sb("swapped", [P, 2, EXPERTS])
            take = r.sb("take", [P, EXPERTS])
            best = r.sb("best", [P, EXPERTS])
            diff = r.sb("diff", [P, EXPERTS])
            token = r.sb("token", [P, EXPERTS])
            top = r.sb("top", [P, 2, EXPERTS])
            peak = r.sb("peak", [P, EXPERTS])
            expo = r.sb("expo", [P, EXPERTS])
            total = r.sb("total", [P, EXPERTS])
            plog = r.ps("plog", [P, 2, SEQ])
            small = r.ps("small", [P, 512])
            small2 = r.ps("small2", [P, 512])
            wr_zero, wr_landed = r.sem("wr_zero"), r.sem("wr_landed")
            norm.xn_stored = r.sem("xn_stored")
            xn_store = lasting.sems(name + "_xn_store", 2)
            acc_set = r.sem("acc_set")
            logits_psum = r.sem("logits_psum")
            logits_kept = r.sem("logits_kept")
            chain = r.sem("topk_chain")
            pe_small, exp_ready = r.sem("pe_small"), r.sem("exp_ready")
            xn_out = xn_dram.rearrange("(g t p) d -> g p t d", t=GT, p=P)

            with nc.Block() as block:

                @block.sync
                def _(sp):
                    sp.wait_ge(wr_zero, 1)
                    sp.dma_start(wr[:, :, 0:EXPERTS], wr_dram).then_inc(wr_landed, 16)
                    if load:
                        sp.dma_start(acc_dram.rearrange("(a p) d -> p a d", p=P),
                                     x_dram.rearrange("(a p) d -> p a d", p=P)).then_inc(acc_set, 16)
                        with sp.Fori(0, GROUPS // 2) as i:
                            for u in range(2):
                                norm.load(sp, ready, x_dram, i, u, i + u * (GROUPS // 2))
                            for u in range(2):
                                wait_at(sp, norm.x_landed[u], 16 * i + 16, ready)
                    for u in range(EU):
                        fetch(sp, u, u)
                    sp.dma_start(b1[:], b1_dram).then_inc(b1_landed, 16)
                    if load:
                        sp.wait_ge(acc_set, 16)

                @block.vector
                def _(dve):
                    dve.memset(wr[:], 0.0).then_inc(wr_zero, 1)
                    with dve.Fori(0, GROUPS // 2) as i:
                        for u in range(2):
                            norm.moments_of(dve, ready, i, u, i + u * (GROUPS // 2), load)
                            norm.normalise(dve, ready, i, u, i + u * (GROUPS // 2))
                    steps = 0

                    def link(ins):
                        nonlocal steps
                        steps += 1
                        ins.then_inc(chain, 1)
                        dve.wait_ge(chain, steps)

                    dve.wait_ge(logits_kept, GROUPS + 2)
                    for k in range(ROUNDS):
                        eight = vals[:, 8 * k:8 * k + 8]
                        link(dve.max(eight, logits[:]))
                        link(dve.max_index(idx[:, 8 * k:8 * k + 8], eight, logits[:]))
                        if k < ROUNDS - 1:
                            link(dve.match_replace(logits[:], eight, logits[:], -3.4e38))
                    link(dve.tensor_copy(idxf[:], idx[:]))
                    link(dve.tensor_scalar(idxf[:], idxf[:], const.half_offset[:, 0:1], None, ALU.add))
                    dve.wait_ge(pe_small, 1)
                    link(dve.tensor_copy(both[:], small[:, 0:2 * P].rearrange("p (a b) -> p a b", a=2)))
                    dve.wait_ge(pe_small, 2)
                    link(dve.tensor_copy(swapped[:], small2[:, 0:2 * EXPERTS].rearrange("p (a b) -> p a b", a=2)))
                    link(dve.tensor_tensor(take[:], both[:, 0, 0:EXPERTS], swapped[:, 0, :], ALU.is_ge))
                    link(dve.tensor_tensor(best[:], both[:, 0, 0:EXPERTS], swapped[:, 0, :], ALU.max))
                    link(dve.tensor_tensor(diff[:], both[:, 1, 0:EXPERTS], swapped[:, 1, :], ALU.subtract))
                    link(dve.tensor_tensor(diff[:], diff[:], take[:], ALU.mult))
                    link(dve.tensor_tensor(token[:], diff[:], swapped[:, 1, :], ALU.add))
                    link(dve.tensor_copy(index[:], token[:]))
                    dve.wait_ge(pe_small, 3)
                    link(dve.tensor_copy(top[:], small[:, 256:256 + 2 * EXPERTS].rearrange("p (a b) -> p a b", a=2)))
                    link(dve.tensor_tensor(peak[:], top[:, 0, :], top[:, 1, :], ALU.max))
                    link(dve.tensor_tensor(best[:], best[:], peak[:], ALU.subtract))
                    dve.wait_ge(pe_small, 4)
                    link(dve.reciprocal(total[:], small2[:, 256:256 + EXPERTS]))
                    link(dve.scalar_tensor_tensor(out=keep_vals[:], in0=expo[:], scalar=0.5, in1=total[:],
                                                  op0=ALU.mult, op1=ALU.mult))

                @block.gpsimd
                def _(pool):
                    pool.sem_inc(norm.xn_stored, 2)
                    with pool.Fori(0, GROUPS // 2) as i:
                        for u in range(2):
                            norm.root(pool, ready, const, i, u)
                            wait_at(pool, norm.xn_ready, 2 * i + (u + 1), ready)
                            pool.dma_start(xn_out[bass.ds(i + u * (GROUPS // 2), 1)].rearrange("g p t d -> p (g t) d"),
                                           norm.xn[:, u]).then_inc(xn_store[u], 16)
                            wait_at(pool, xn_store[u], 16 * i + 16, ready)
                            pool.sem_inc(norm.xn_stored, 1)

                @block.tensor
                def _(pe):
                    pe.wait_ge(wr_landed, 16)
                    with pe.Fori(0, GROUPS // 2) as i:
                        for u in range(2):
                            norm.turn(pe, ready, const, i, u)
                            norm.kept(pe, ready, i, u)
                            wait_at(pe, logits_kept, 2 * i + (u + 1), ready)
                            for c in range(KC):
                                last = pe.matmul(plog[64 * u:64 * u + 64, u, :], wr[:, c, :], norm.xT[:, u, c, :],
                                                 start=(c == 0), stop=(c == KC - 1))
                            last.then_inc(logits_psum, 1)
                    pe.wait_ge(chain, 3 * ROUNDS + 1)
                    pe.transpose(small[:, 0:P], vals[:], const.ident[:])
                    pe.transpose(small[:, P:2 * P], idxf[:], const.ident[:]).then_inc(pe_small, 1)
                    pe.wait_ge(chain, 3 * ROUNDS + 2)
                    for a in range(2):
                        last = pe.matmul(small2[:, a * EXPERTS:(a + 1) * EXPERTS], const.flip[:],
                                         both[:, a, 64:64 + EXPERTS], start=True, stop=True)
                    last.then_inc(pe_small, 1)
                    pe.wait_ge(chain, 3 * ROUNDS + 9)
                    for a, row in enumerate((const.first, const.last)):
                        last = pe.matmul(small[:, 256 + a * EXPERTS:256 + (a + 1) * EXPERTS], row[:], best[:],
                                         start=True, stop=True)
                    last.then_inc(pe_small, 1)
                    pe.wait_ge(exp_ready, 1)
                    pe.matmul(small2[:, 256:256 + EXPERTS], const.ones[:], expo[:], start=True, stop=True
                              ).then_inc(pe_small, 1)

                @block.scalar
                def _(act):
                    act.sem_inc(norm.xT_free, 2)
                    act.sem_inc(norm.xn_free, 2)
                    act.sem_inc(norm.xT_ready, norm.banks)
                    act.sem_inc(logits_kept, 2)
                    with act.Fori(0, GROUPS // 2) as i:
                        for u in range(2):
                            norm.keep(act, ready, i, u)
                            wait_at(act, logits_psum, 2 * i + (u + 1), ready)
                            act.sem_inc(norm.xT_free, 1)
                            rows = slice(64 * u, 64 * u + 64)
                            act.activation(logits[rows, bass.ds(i * SEQ, SEQ)], plog[rows, u, :], ACT.Copy
                                           ).then_inc(logits_kept, 1)
                    act.wait_ge(chain, 3 * ROUNDS + 12)
                    act.activation(expo[:], best[:], ACT.Exp).then_inc(exp_ready, 1)
            r.clear()

        slot = s.sb("slot", [P, EU], U32)
        slot_out = s.sb("slot_out", [P, 2], U32)
        xg = s.sb("xg", [P, EU, D])
        xgT = s.sb("xgT", [P, 2, KC, P])
        hb = s.sb("hb", [P, 2, HC, P])
        h = s.sb("h", [P, 2, HC, P])
        y = s.sb("y", [P, EU, D])
        pT = s.ps("pT", [P, 2, 512])
        pH = s.ps("pH", [P, 2, HC, P])
        pY = s.ps("pY", [P, 2, 512])
        gathered = lasting.sems(name + "_gathered", EU)
        scattered = lasting.sem(name + "_scattered")
        slot_ready, gT_psum, gT_ready = s.sem("slot_ready"), s.sem("gT_psum"), s.sem("gT_ready")
        h_psum, h_ready, y_psum = s.sem("h_psum"), s.sem("h_ready"), s.sem("y_psum")
        h_biased = s.sem("h_biased")
        y_ready = s.sem("y_ready")
        y_free = s.sem("y_free")
        w_free = s.sem("w_free")

        def over_experts(eng, step):
            with eng.Fori(0, EXPERTS // EU - 1) as i:
                for u in range(EU):
                    step(i, u, EU)
            for u in range(EU):
                step(EXPERTS // EU - 1, u, EU - 1 - u)

        def later(i, u, k):
            return i + (u + k) // EU, (u + k) % EU

        def count(i, u, extra=1):
            return EU * i + (u + extra)

        with nc.Block() as block:

            @block.sync
            def _(sp):
                with sp.Fori(0, EXPERTS // EU - 1) as i:
                    for u in range(EU):
                        wait_at(sp, w_free, count(i, u), ready)
                        fetch(sp, EU * i + (EU + u), u)

            @block.gpsimd
            def _(pool):
                def gather(u):
                    pool.indirect_dma_start(xg[:, u, :], None, xn_dram, bass.IndirectOffsetOnAxis(slot[:, u:u + 1], 0)
                                            ).then_inc(gathered[u], 16)

                for u in range(EU):
                    pool.tensor_copy(slot[:, u:u + 1], index[:, u:u + 1]).then_inc(slot_ready, 1)
                    pool.wait_ge(slot_ready, u + 1)
                    gather(u)
                pool.tensor_copy(slot_out[:, 0:1], index[:, 0:1]).then_inc(slot_ready, 1)
                pool.sem_inc(y_free, EU)

                def step(i, u, more):
                    e = EU * i + u
                    wait_at(pool, slot_ready, 2 * e + (EU + 1) if more == EU else EXPERTS * 2 - EU + 1 + u, ready)
                    wait_at(pool, y_ready, count(i, u, 3), ready)
                    pool.indirect_dma_start(acc_dram, bass.IndirectOffsetOnAxis(slot_out[:, u % 2:u % 2 + 1], 0), y[:, u, :],
                                            None, compute_op=ALU.add).then_inc(scattered, 16)
                    if more:
                        pool.tensor_copy(slot_out[:, (u + 1) % 2:(u + 1) % 2 + 1], index[:, bass.ds(e + 1, 1)]
                                         ).then_inc(slot_ready, 1)
                    if more == EU:
                        wait_at(pool, gathered[u], 16 * i + 16, ready)
                        pool.tensor_copy(slot[:, u:u + 1], index[:, bass.ds(e + EU, 1)]).then_inc(slot_ready, 1)
                        wait_at(pool, slot_ready, 2 * e + (EU + 3), ready)
                        gather(u)
                    wait_at(pool, scattered, 16 * count(i, u), ready)
                    pool.sem_inc(y_free, 1)

                over_experts(pool, step)

            @block.tensor
            def _(pe):
                def turn(i, u):
                    v = u % 2
                    wait_at(pe, gathered[u], 16 * i + 16, ready)
                    for c in range(KC):
                        last = pe.transpose(pT[:, v, c * P:(c + 1) * P], xg[:, u, c * P:(c + 1) * P], const.ident[:])
                    last.then_inc(gT_psum, 1)

                def hidden(i, u):
                    v = u % 2
                    wait_at(pe, w_landed[u], 48 * i + 48, ready)
                    wait_at(pe, gT_ready, count(i, u), ready)
                    wait_at(pe, h_biased, count(i, u), ready)
                    for j in range(HC):
                        for c in range(KC):
                            last = pe.matmul(pH[:, v, j, :], w1[:, u, c, j * P:(j + 1) * P], xgT[:, v, c, :],
                                             start=(c == 0), stop=(c == KC - 1))
                    last.then_inc(h_psum, 1)

                def step(i, u, more):
                    v = u % 2
                    if more > 0:
                        hidden(*later(i, u, 1))
                    if more > 1:
                        turn(*later(i, u, 2))
                    wait_at(pe, h_ready, count(i, u), ready)
                    wait_at(pe, y_ready, count(i, u), ready)
                    pe.matmul(pY[:, v, 0:D], const.ones[0:1, :], b2[:, u, :], start=True, stop=False,
                              skip_group_check=True)
                    for j in range(HC):
                        q = j * P // HID
                        last = pe.matmul(pY[:, v, q * YK:(q + 1) * YK], h[:, v, j, :], w2[:, u, j, :],
                                         start=False, stop=(j == HC - 1), skip_group_check=True)
                    last.then_inc(y_psum, 1)

                turn(0, 0)
                hidden(0, 0)
                turn(0, 1)
                over_experts(pe, step)

            @block.scalar
            def _(act):
                def keep(i, u):
                    v = u % 2
                    wait_at(act, gT_psum, count(i, u), ready)
                    act.activation(xgT[:, v], pT[:, v, 0:D].rearrange("p (c n) -> p c n", c=KC), ACT.Copy
                                   ).then_inc(gT_ready, 1)

                def active(i, u):
                    wait_at(act, h_biased, count(i, u, 3), ready)
                    act.activation(h[:, u % 2], hb[:, u % 2], ACT.Gelu).then_inc(h_ready, 1)

                def step(i, u, more):
                    if more > 1:
                        keep(*later(i, u, 2))
                    if more > 0:
                        active(*later(i, u, 1))

                keep(0, 0)
                keep(0, 1)
                active(0, 0)
                over_experts(act, step)

            @block.vector
            def _(dve):
                def biased(i, u):
                    wait_at(dve, h_psum, count(i, u), ready)
                    bias = b1[:, bass.ds(EU * i + u, 1), :].rearrange("p e j -> p (e j)").unsqueeze(2).to_broadcast([P, HC, P])
                    dve.tensor_tensor(hb[:, u % 2], pH[:, u % 2], bias, ALU.add).then_inc(h_biased, 1)

                def step(i, u, more):
                    if more > 0:
                        biased(*later(i, u, 1))
                    wait_at(dve, y_free, count(i, u), ready)
                    wait_at(dve, y_psum, count(i, u), ready)
                    dve.sem_inc(w_free, 1)
                    dve.tensor_scalar(y[:, u, :], pY[:, u % 2, 0:D], keep_vals[:, bass.ds(EU * i + u, 1)], None, ALU.mult
                                      ).then_inc(y_ready, 1)

                dve.wait_ge(b1_landed, 16)
                dve.sem_inc(h_biased, 2)
                dve.sem_inc(y_ready, 2)
                biased(0, 0)
                over_experts(dve, step)
        s.clear()
HEADS = 16
DH = 64
DI = HEADS * DH
PAIRS = HEADS // 2
CLAMP = 50.0
RMS_EPS = 1.1920929e-07
QW = 512
CHUNKS = 3 * DI // QW
HV = QW // DH


def attention_stage(nc, const, x_all, x_dram, out_dram, wqkv_dram, wo_dram, nw_dram, gamma_dram):
    QKV_USE = 1
    TURN_USE = QKV_USE + GT * CHUNKS // 2
    WO_USE = TURN_USE + PAIRS
    MISC = WO_USE + GT // 2
    with ExitStack() as ctx:
        s = Space(nc, ctx, "attn")
        ready = const.ready
        misc = s.ps("misc", [P, 2, 512])
        norm = Norm(s, x_all, banks=1, unroll=1, turned=misc[:].unsqueeze(1), eps2=RMS_EPS)
        w = s.sb("w", [P, KC, 3 * DI])
        wo = s.sb("wo", [P, PAIRS, D])
        nw = s.sb("nw", [P, KC])
        gamma = s.sb("gamma", [P, 2, PAIRS])
        scale = s.sb("scale", [P, PAIRS])
        qk = s.sb("qk", [P, GT, 2, HEADS, DH])
        sq = s.sb("sq", [P, 2 * HEADS, DH])
        ss = s.sb("ss", [P, GT, 2 * HEADS])
        rn = s.sb("rn", [P, GT, 2 * HEADS])
        va = s.sb("va", [P, GT, PAIRS, 3, DH])
        qT = s.sb("qT", [P, 2, SEQ])
        kT = s.sb("kT", [P, 2, SEQ])
        th = s.sb("th", [P, 2, GT, SEQ])
        pr = s.sb("pr", [P, 2, GT, SEQ])
        rec = s.sb("rec", [P, SEQ])
        oT = s.sb("oT", [P, PAIRS, SEQ])
        pS = s.ps("pS", [P, 2, 2, SEQ])
        pO = s.ps("pO", [P, 2, SEQ])
        w_landed, setup = s.sem("w_landed"), s.sem("setup")
        misc_ready = s.sems("misc_ready", 2)
        misc_free = s.sems("misc_free", 2)
        sq_ready = s.sem("sq_ready")
        sum_ready = s.sem("sum_ready")
        ss_ready, rn_ready, qk_ready, v_ready = s.sem("ss_ready"), s.sem("rn_ready"), s.sem("qk_ready"), s.sem("v_ready")
        score_ready = s.sem("score_ready")
        tanh_ready = s.sem("tanh_ready")
        exp_ready = s.sem("exp_ready")
        pv_ready = s.sem("pv_ready")
        rec_ready = s.sem("rec_ready")
        o_ready = s.sem("o_ready")
        out_ready, stored = s.sem("out_ready"), s.sem("stored")

        def chunk_use(t, j):
            return j % 2, QKV_USE + (CHUNKS * t + j) // 2

        def wait_ready(eng, n, bank, use):
            wait_at(eng, misc_ready[bank], MISC * n + (use + 1), ready)

        with nc.Block() as block:

            @block.sync
            def _(sp):
                sp.dma_start(w[:], wqkv_dram).then_inc(w_landed, 16)
                sp.dma_start(wo[:], wo_dram).then_inc(w_landed, 16)
                sp.dma_start(nw[:], nw_dram).then_inc(w_landed, 16)
                sp.dma_start(gamma[:], gamma_dram).then_inc(w_landed, 16)
                with sp.Fori(0, GROUPS) as i:
                    norm.load(sp, ready, x_dram, i, 0, i)
                    wait_at(sp, norm.x_landed[0], 16 * i + 16, ready)
                with sp.Fori(0, GROUPS) as n:
                    wait_at(sp, out_ready, n * GT + GT, ready)
                    sp.dma_start(out_dram[bass.ds(n * SEQ, SEQ), :].rearrange("(t p) d -> p t d", p=P),
                                 x_all[:, bass.ds(n, 1)].rearrange("p g t d -> p (g t) d")).then_inc(stored, 16)
                    wait_at(sp, stored, 16 * n + 16, ready)

            @block.vector
            def _(dve):
                def project(n):
                    for t in range(GT):
                        wait_at(dve, sq_ready, GT * n + (t + 1), ready)
                        dve.tensor_reduce(ss[:, t, :], sq[:], AX.X, ALU.add).then_inc(sum_ready, 1)
                        wait_at(dve, sum_ready, GT * n + (t + 2), ready)
                        dve.tensor_scalar(ss[:, t, :], ss[:, t, :], 1e-24, None, ALU.max).then_inc(ss_ready, 1)
                        if t:
                            unit(n, t - 1)
                    unit(n, GT - 1)

                def unit(n, t):
                    wait_at(dve, rn_ready, GT * n + (t + 1), ready)
                    rows = qk[:, t].rearrange("p a h d -> p (a h) d")
                    dve.tensor_tensor(rows, rows, rn[:, t, :].unsqueeze(2).to_broadcast([P, 2 * HEADS, DH]), ALU.mult
                                      ).then_inc(qk_ready, 1)

                def turn_pair(n, p):
                    wait_ready(dve, n, 0, TURN_USE + p)
                    dve.tensor_scalar(qT[:, p % 2, :], misc[:, 0, :], scale[:, p:p + 1], None, ALU.mult
                                      ).then_inc(misc_free[0], 1)
                    wait_ready(dve, n, 1, TURN_USE + p)
                    dve.tensor_copy(kT[:, p % 2, :], misc[:, 1, :]).then_inc(misc_free[1], 1)

                def head(n, h):
                    v = h % 2
                    own, other = slice(DH * v, DH * v + DH), slice(DH * (1 - v), DH * (1 - v) + DH)
                    wait_at(dve, pv_ready, HEADS * n + (h + 3), ready)
                    dve.reciprocal(rec[own, :], pO[other, v, :]).then_inc(rec_ready, 1)
                    wait_at(dve, rec_ready, HEADS * n + (h + 1), ready)
                    dve.tensor_tensor(oT[own, h // 2, :], pO[own, v, :], rec[own, :], ALU.mult).then_inc(o_ready, 1)

                def batch(n, more):
                    project(n)
                    turn_pair(n, 0)
                    if more:
                        norm.moments_of(dve, ready, n + 1, 0, n + 1)
                    for h in range(HEADS):
                        if h:
                            head(n, h - 1)
                        if h % 2 == 0 and h // 2 + 1 < PAIRS:
                            turn_pair(n, h // 2 + 1)
                        if h == 2 and more:
                            norm.normalise(dve, ready, n + 1, 0, n + 1)
                    head(n, HEADS - 1)
                    for t in range(GT):
                        wait_ready(dve, n, t % 2, WO_USE + t // 2)
                        x = x_all[:, bass.ds(n, 1), t, :].rearrange("p g d -> p (g d)")
                        dve.tensor_tensor(x, x, misc[:, t % 2, 0:D], ALU.add).then_inc(misc_free[t % 2], 1)
                    dve.drain().then_inc(out_ready, GT)

                dve.sem_inc(misc_free[0], 1)
                dve.sem_inc(misc_free[1], 1)
                dve.sem_inc(sum_ready, 1)
                dve.sem_inc(o_ready, 2)
                dve.wait_ge(w_landed, 64)
                for c in range(KC):
                    dve.tensor_scalar(w[:, c, :], w[:, c, :], nw[:, c:c + 1], None, ALU.mult).then_inc(setup, 1)
                dve.memset(va[:, :, :, 1, :], 1.0).then_inc(setup, 1)
                dve.tensor_scalar(gamma[:], gamma[:], 1.0, None, ALU.add).then_inc(setup, 1)
                dve.wait_ge(setup, 4)
                dve.scalar_tensor_tensor(out=scale[:], in0=gamma[:, 0, :], scalar=DH / CLAMP, in1=gamma[:, 1, :],
                                         op0=ALU.mult, op1=ALU.mult).then_inc(setup, 1)
                dve.wait_ge(setup, 5)
                norm.moments_of(dve, ready, 0, 0, 0)
                norm.normalise(dve, ready, 0, 0, 0)
                with dve.Fori(0, GROUPS - 1) as n:
                    batch(n, True)
                batch(GROUPS - 1, False)

            @block.gpsimd
            def _(pool):
                def batch(n, more):
                    for t in range(GT):
                        wait_at(pool, ss_ready, GT * n + (t + 1), ready)
                        pool.tensor_tensor(rn[:, t, :], ss[:, t, :], const.minus_half[:, 0:2 * HEADS], ALU.pow
                                           ).then_inc(rn_ready, 1)
                    if more:
                        norm.root(pool, ready, const, n + 1, 0)

                pool.memset(norm.eps2_tile[:], RMS_EPS).then_inc(norm.eps2_set, 1)
                pool.wait_ge(norm.eps2_set, 1)
                norm.root(pool, ready, const, 0, 0)
                with pool.Fori(0, GROUPS - 1) as n:
                    batch(n, True)
                batch(GROUPS - 1, False)

            @block.scalar
            def _(act):
                act.sem_inc(norm.xT_free, 1)
                act.sem_inc(norm.xn_free, 1)
                act.sem_inc(norm.xT_ready, norm.banks)
                act.sem_inc(tanh_ready, 2)
                with act.Fori(0, GROUPS) as n:
                    norm.keep(act, ready, n, 0)
                    norm.kept(act, ready, n, 0)
                    act.sem_inc(misc_free[0], 1)
                    act.sem_inc(misc_free[1], 1)
                    for t in range(GT):
                        for j in range(CHUNKS):
                            bank, use = chunk_use(t, j)
                            wait_ready(act, n, bank, use)
                            if j < 4:
                                heads = slice((j % 2) * HV, (j % 2 + 1) * HV)
                                act.activation(qk[:, t, j // 2, heads, :],
                                               misc[:, bank, :].rearrange("p (h d) -> p h d", h=HV),
                                               ACT.Copy).then_inc(misc_free[bank], 1)
                            else:
                                pairs = slice((j - 4) * HV // 2, (j - 3) * HV // 2)
                                act.activation(va[:, t, pairs, 0:3:2, :],
                                               misc[:, bank, :].rearrange("p (q a d) -> p q a d", a=2, d=DH),
                                               ACT.Copy).then_inc(misc_free[bank], 1)
                        for bank in range(2):
                            wait_at(act, misc_free[bank], MISC * n + (chunk_use(t, 2)[1] + 2), ready)
                        wait_at(act, sum_ready, GT * n + (t + 1), ready)
                        act.activation(sq[:], qk[:, t].rearrange("p a h d -> p (a h) d"), ACT.Square
                                       ).then_inc(sq_ready, 1)
                    act.drain().then_inc(v_ready, 1)
                    act.sem_inc(norm.xT_free, 1)
                    for h in range(HEADS):
                        v = h % 2
                        for a in range(2):
                            wait_at(act, score_ready, 2 * HEADS * n + (2 * h + a + 1), ready)
                            act.activation(th[:, v, 2 * a:2 * a + 2, :], pS[:, a], ACT.Tanh).then_inc(tanh_ready, 1)
                        wait_at(act, tanh_ready, 2 * HEADS * n + (2 * h + 4), ready)
                        wait_at(act, pv_ready, HEADS * n + (h + 1), ready)
                        act.activation(pr[:, v], th[:, v], ACT.Exp, scale=CLAMP * DH ** -0.5).then_inc(exp_ready, 1)

            @block.tensor
            def _(pe):
                def wait_free(n, bank, use):
                    wait_at(pe, misc_free[bank], MISC * n + (use + 1), ready)

                def turn_pair(n, p):
                    for a in range(2):
                        wait_free(n, a, TURN_USE + p)
                        for t in range(GT):
                            last = pe.transpose(misc[:, a, t * P:(t + 1) * P],
                                                qk[:, t, a, 2 * p:2 * p + 2, :].rearrange("p h d -> p (h d)"),
                                                const.ident[:])
                        last.then_inc(misc_ready[a], 1)

                def scores(n, h):
                    if h % 2 == 0:
                        for a in range(2):
                            wait_at(pe, misc_free[a], MISC * n + (TURN_USE + h // 2 + 2), ready)
                    rows = slice(DH * (h % 2), DH * (h % 2) + DH)
                    for a in range(2):
                        wait_at(pe, tanh_ready, 2 * HEADS * n + (2 * h + a + 1), ready)
                        for b in range(2):
                            j = 2 * a + b
                            last = pe.matmul(pS[:, a, b, :], kT[rows, (h // 2) % 2, j * P:(j + 1) * P],
                                             qT[rows, (h // 2) % 2, :], start=True, stop=True)
                        last.then_inc(score_ready, 1)

                def values(n, h):
                    wait_at(pe, exp_ready, HEADS * n + (h + 1), ready)
                    wait_at(pe, o_ready, HEADS * n + (h + 1), ready)
                    v = h % 2
                    for j in range(GT):
                        last = pe.matmul(pO[:, v, :], va[:, j, h // 2, v:v + 2, :].rearrange("p a d -> p (a d)"),
                                         pr[:, v, j, :], start=(j == 0), stop=(j == GT - 1))
                    last.then_inc(pv_ready, 1)

                pe.sem_inc(pv_ready, 2)
                pe.wait_ge(setup, 5)
                with pe.Fori(0, GROUPS) as n:
                    wait_free(n, 0, 0)
                    wait_free(n, 1, 0)
                    norm.turn(pe, ready, const, n, 0)
                    norm.kept(pe, ready, n, 0)
                    pe.sem_inc(misc_ready[0], 1)
                    pe.sem_inc(misc_ready[1], 1)
                    for t in range(GT):
                        for j in range(CHUNKS):
                            bank, use = chunk_use(t, j)
                            wait_free(n, bank, use)
                            for c in range(KC):
                                last = pe.matmul(misc[:, bank, :], norm.xT[:, 0, c, t * P:(t + 1) * P],
                                                 w[:, c, j * QW:(j + 1) * QW], start=(c == 0), stop=(c == KC - 1))
                            last.then_inc(misc_ready[bank], 1)
                    wait_at(pe, qk_ready, GT * n + GT, ready)
                    wait_at(pe, v_ready, n + 1, ready)
                    turn_pair(n, 0)
                    for h in range(HEADS):
                        scores(n, h)
                        if h:
                            values(n, h - 1)
                        if h % 2 == 0 and h // 2 + 1 < PAIRS:
                            turn_pair(n, h // 2 + 1)
                    values(n, HEADS - 1)
                    wait_at(pe, o_ready, HEADS * n + (HEADS + 2), ready)
                    for t in range(GT):
                        wait_free(n, t % 2, WO_USE + t // 2)
                        for p in range(PAIRS):
                            last = pe.matmul(misc[:, t % 2, 0:D], oT[:, p, t * P:(t + 1) * P], wo[:, p, :],
                                             start=(p == 0), stop=(p == PAIRS - 1))
                        last.then_inc(misc_ready[t % 2], 1)
        s.clear()


def rwkv_stage(nc, const, name, load, x_all, x_dram, out_dram, wr_dram, wk_dram, wv_dram, mu_dram):
    with ExitStack() as ctx:
        s = Space(nc, ctx, name)
        ready = const.ready
        norm = Norm(s, x_all, banks=1, lead=1)
        wr, wk, wv = s.sb("wr", [P, KC, D]), s.sb("wk", [P, KC, D]), s.sb("wv", [P, KC, D])
        mu = s.sb("mu", [P, 2, KC])
        step_back = s.sb("step_back", [P, KC, SEQ])
        mixed = s.sb("mixed", [P, 2, 2, KC, SEQ])
        relu = s.sb("relu", [P, KC, SEQ])
        act2 = s.sb("act2", [P, KC, SEQ])
        gate = s.sb("gate", [P, GT, D])
        prod = s.sb("prod", [P, GT, D])
        pk = s.ps("pk", [P, KC, SEQ])
        pr = s.ps("pr", [P, GT, D])
        pv = s.ps("pv", [P, GT, D])
        w_landed = s.sem("w_landed")
        lead_clear = s.sem("lead_clear")
        step_ready, mixed_ready = s.sem("step_ready"), s.sem("mixed_ready")
        pk_ready, relu_ready, act2_ready = s.sem("pk_ready"), s.sem("relu_ready"), s.sem("act2_ready")
        pr_ready, gate_ready, pv_ready = s.sem("pr_ready"), s.sem("gate_ready"), s.sem("pv_ready")
        prod_ready = s.sem("prod_ready")
        out_ready = s.sem("out_ready")
        stored = s.sems("stored", 2)
        last_i = GROUPS // 2 - 1

        with nc.Block() as block:

            @block.sync
            def _(sp):
                sp.dma_start(wr[:], wr_dram).then_inc(w_landed, 16)
                sp.dma_start(wk[:], wk_dram).then_inc(w_landed, 16)
                sp.dma_start(wv[:], wv_dram).then_inc(w_landed, 16)
                sp.dma_start(mu[:], mu_dram).then_inc(w_landed, 16)
                if load:
                    with sp.Fori(0, GROUPS // 2) as i:
                        for u in range(2):
                            norm.load(sp, ready, x_dram, i, u, 2 * i + u)
                        for u in range(2):
                            wait_at(sp, norm.x_landed[u], 16 * i + 16, ready)
                if out_dram is not None:
                    with sp.Fori(0, GROUPS // 2) as i:
                        for u in range(2):
                            wait_at(sp, out_ready, 2 * i + (u + 1), ready)
                            sp.dma_start(out_dram[bass.ds((2 * i + u) * SEQ, SEQ), :].rearrange("(t p) d -> p t d", p=P),
                                         x_all[:, bass.ds(2 * i + u, 1)].rearrange("p g t d -> p (g t) d")
                                         ).then_inc(stored[u], 16)
                        for u in range(2):
                            wait_at(sp, stored[u], 16 * i + 16, ready)

            @block.vector
            def _(dve):
                def first(i, u):
                    norm.moments_of(dve, ready, i, u, 2 * i + u, load)
                    norm.normalise(dve, ready, i, u, 2 * i + u)

                def mix(i, u):
                    n1 = 2 * i + (u + 1)
                    norm.kept(dve, ready, i, u)
                    now, before = norm.xT[:, u, :, 1:], norm.xT[:, u, :, 0:SEQ]
                    dve.tensor_tensor(step_back[:], now, before, ALU.subtract).then_inc(step_ready, 1)
                    wait_at(dve, step_ready, n1, ready)
                    for r in range(2):
                        for c in range(KC):
                            last = dve.scalar_tensor_tensor(out=mixed[:, u, r, c, :], in0=step_back[:, c, :],
                                                            scalar=mu[:, r, c:c + 1], in1=before[:, c, :],
                                                            op0=ALU.mult, op1=ALU.add)
                    last.then_inc(mixed_ready, 1)

                def main(i, u):
                    n1 = 2 * i + (u + 1)
                    mix(i, u)
                    wait_at(dve, relu_ready, n1, ready)
                    dve.tensor_tensor(act2[:], pk[:], relu[:], ALU.mult).then_inc(act2_ready, 1)
                    wait_at(dve, gate_ready, n1, ready)
                    wait_at(dve, pv_ready, n1, ready)
                    dve.tensor_tensor(prod[:], pv[:], gate[:], ALU.mult).then_inc(prod_ready, 1)
                    wait_at(dve, prod_ready, n1 + 1, ready)
                    x = x_all[:, bass.ds(2 * i + u, 1)].rearrange("p g t d -> p (g t d)")
                    dve.scalar_tensor_tensor(out=x, in0=prod[:].rearrange("p t d -> p (t d)"), scalar=0.5, in1=x,
                                             op0=ALU.mult, op1=ALU.add).then_inc(out_ready, 1)

                dve.memset(norm.xT[:, :, :, 0:1], 0.0).then_inc(lead_clear, 1)
                dve.sem_inc(prod_ready, 1)
                dve.wait_ge(w_landed, 64)
                dve.wait_ge(lead_clear, 1)
                first(0, 0)
                with dve.Fori(0, last_i) as i:
                    for u in range(2):
                        first(*ahead(i, u))
                        main(i, u)
                first(last_i, 1)
                main(last_i, 0)
                main(last_i, 1)

            @block.gpsimd
            def _(pool):
                with pool.Fori(0, GROUPS // 2) as i:
                    for u in range(2):
                        norm.root(pool, ready, const, i, u)

            @block.scalar
            def _(act):
                def main(i, u):
                    n1 = 2 * i + (u + 1)
                    wait_at(act, mixed_ready, n1, ready)
                    act.sem_inc(norm.xT_free, 1)
                    wait_at(act, pk_ready, n1, ready)
                    act.activation(relu[:], pk[:], ACT.Relu).then_inc(relu_ready, 1)
                    wait_at(act, pr_ready, n1, ready)
                    act.activation(gate[:], pr[:], ACT.Sigmoid).then_inc(gate_ready, 1)

                act.sem_inc(norm.xT_free, 2)
                act.sem_inc(norm.xn_free, 2)
                act.sem_inc(norm.xT_ready, norm.banks)
                act.wait_ge(lead_clear, 1)
                norm.keep(act, ready, 0, 0)
                with act.Fori(0, last_i) as i:
                    for u in range(2):
                        norm.keep(act, ready, *ahead(i, u))
                        main(i, u)
                norm.keep(act, ready, last_i, 1)
                main(last_i, 0)
                main(last_i, 1)

            @block.tensor
            def _(pe):
                def main(i, u):
                    n1 = 2 * i + (u + 1)
                    wait_at(pe, mixed_ready, n1, ready)
                    for m in range(KC):
                        for c in range(KC):
                            last = pe.matmul(pk[:, m, :], wk[:, c, m * P:(m + 1) * P], mixed[:, u, 1, c, :],
                                             start=(c == 0), stop=(c == KC - 1))
                    last.then_inc(pk_ready, 1)
                    wait_at(pe, prod_ready, n1, ready)
                    for t in range(GT):
                        for c in range(KC):
                            last = pe.matmul(pr[:, t, :], mixed[:, u, 0, c, t * P:(t + 1) * P], wr[:, c, :],
                                             start=(c == 0), stop=(c == KC - 1))
                    last.then_inc(pr_ready, 1)
                    wait_at(pe, act2_ready, n1, ready)
                    for t in range(GT):
                        for c in range(KC):
                            last = pe.matmul(pv[:, t, :], act2[:, c, t * P:(t + 1) * P], wv[:, c, :],
                                             start=(c == 0), stop=(c == KC - 1))
                    last.then_inc(pv_ready, 1)

                pe.wait_ge(w_landed, 64)
                norm.turn(pe, ready, const, 0, 0)
                with pe.Fori(0, last_i) as i:
                    for u in range(2):
                        norm.turn(pe, ready, const, *ahead(i, u))
                        main(i, u)
                norm.turn(pe, ready, const, last_i, 1)
                main(last_i, 0)
                main(last_i, 1)
        s.clear()


MH = 16
HP = 32
MI = MH * HP
NS = 64
TILES = TOKENS // P
CH = SEQ // P
PC = 2 * NS + 2 * MH
TH = NS // 2
RMS2_EPS = 1e-6
TWO_PI = 6.283185307179586
PI = 3.1415925
HALF_PI = TWO_PI / 4
ROUND = 12582912.0


def mamba_stage(nc, const, x_all, gz_dram, w_dram, theta_dram, wout_dram, norm_dram, rows_dram):
    with ExitStack() as ctx:
        s = Space(nc, ctx, "mamba")
        ready = const.ready
        xs = s.sb("xs", [P, TILES, MI])
        bc = s.sb("bc", [P, TILES, 2 * NS])
        cumT = s.sb("cumT", [3 * MH, TILES, P], BF16)
        weight = s.sb("weight", [P, TILES, MH])
        to_end = s.sb("to_end", [P, TILES, MH])
        grown = s.sb("grown", [P, TILES, MH])
        across = s.sb("across", [P, TILES, MH])
        skip = s.sb("skip", [P, TILES, MH])
        mean1 = s.sb("mean1", [P, TILES])
        root1 = s.sb("root1", [P, TILES])
        rows = s.sb("rows", [P, 4 * NS + 3 * MH])
        rows_landed = s.sem("rows_landed")

        rctx = ctx.enter_context(ExitStack())
        raw = Space(nc, rctx, "mamba_raw").sb("raw", [P, TILES, PC + TH])
        unscale = Space(nc, rctx, "mamba_un").sb("unscale", [P, TILES])
        with ExitStack() as pctx:
            r = Space(nc, pctx, "mamba_proj")
            norm = Norm(r, x_all, banks=1, eps2=RMS2_EPS)
            w = r.sb("w", [P, KC, 2 * MI + PC])
            theta_w = r.sb("theta_w", [P, KC, TH])
            nrm = r.sb("nrm", [P, 2, KC])
            xi = r.sb("xi", [P, 2, KC, SEQ])
            sg = r.sb("sg", [P, 2, MI])
            gz = r.sb("gz", [P, 2, MI])
            pxz = r.ps("pxz", [P, 2, 2, MI])
            pbc = r.ps("pbc", [P, 2, 512])
            w_landed = r.sem("w_landed")
            xi_ready = r.sem("xi_ready")
            xz_psum, bc_psum = r.sem("xz_psum"), r.sem("bc_psum")
            sg_ready = r.sem("sg_ready")
            silu_ready = r.sem("silu_ready")
            raw_ready = r.sem("raw_ready")
            gz_stored = r.sems("gz_stored", 2)
            unscale_ready = r.sem("unscale_ready")
            gz_out = gz_dram.rearrange("(g p) d -> g p d", p=P)
            last_i = GROUPS // 2 - 1

            with nc.Block() as block:

                @block.sync
                def _(sp):
                    sp.dma_start(w[:], w_dram).then_inc(w_landed, 16)
                    sp.dma_start(theta_w[:], theta_dram).then_inc(w_landed, 16)
                    sp.dma_start(nrm[:], norm_dram).then_inc(w_landed, 16)
                    sp.dma_start(rows[:], rows_dram.rearrange("(o n) -> o n", o=1).to_broadcast([P, 4 * NS + 3 * MH])
                                 ).then_inc(rows_landed, 16)
                    with sp.Fori(0, TILES // 2) as i:
                        for v in range(2):
                            wait_at(sp, silu_ready, 4 * i + (2 * v + 6), ready)
                            sp.dma_start(gz_out[bass.ds(2 * i + v, 1)].rearrange("g p d -> p (g d)"), gz[:, v]
                                         ).then_inc(gz_stored[v], 16)
                    for v in range(2):
                        sp.wait_ge(gz_stored[v], 16 * TILES // 2)

                @block.vector
                def _(dve):
                    def first(i, u):
                        norm.moments_of(dve, ready, i, u, 2 * i + u, False)
                        norm.normalise(dve, ready, i, u, 2 * i + u)
                        tiles = bass.ds(GT * (2 * i + u), GT)
                        dve.tensor_copy(mean1[:, tiles], norm.moments[:, u, :, 0])
                        dve.tensor_copy(root1[:, tiles], norm.work[:, u, 0, :])

                    def main(i, u, before):
                        n = 2 * i + u
                        for t in range(GT):
                            tile = GT * n + t
                            v = t % 2
                            if before or t >= 2:
                                wait_at(dve, gz_stored[v], 32 * n + 16 * (t // 2), ready)
                            for a in range(2):
                                wait_at(dve, sg_ready, 2 * tile + (a + 1), ready)
                                out = gz[:, v, :] if a else xs[:, bass.ds(tile, 1), :].rearrange("p o d -> p (o d)")
                                dve.tensor_tensor(out, pxz[:, v, a, :], sg[:, a, :], ALU.mult
                                                  ).then_inc(silu_ready, 1)

                    dve.sem_inc(silu_ready, 4)
                    first(0, 0)
                    first(0, 1)
                    main(0, 0, False)
                    first(1, 0)
                    main(0, 1, True)
                    with dve.Fori(1, last_i) as i:
                        for u in range(2):
                            first(*ahead(i, u))
                            main(i, u, True)
                    first(last_i, 1)
                    main(last_i, 0, True)
                    main(last_i, 1, True)

                @block.gpsimd
                def _(pool):
                    pool.memset(norm.eps2_tile[:], RMS2_EPS).then_inc(norm.eps2_set, 1)
                    pool.wait_ge(norm.eps2_set, 1)
                    with pool.Fori(0, GROUPS // 2) as i:
                        for u in range(2):
                            norm.root(pool, ready, const, i, u)
                            pool.tensor_tensor(unscale[:, bass.ds(GT * (2 * i + u), GT)], norm.work[:, u, 1, :],
                                               norm.work[:, u, 2, :], ALU.mult).then_inc(unscale_ready, 1)

                @block.scalar
                def _(act):
                    def first(i, u):
                        norm.keep(act, ready, i, u, count=False)
                        for c in range(KC):
                            last = act.activation(xi[:, u, c, :], norm.turned[:, 0, c, :], ACT.Identity,
                                                  scale=nrm[:, 0, c:c + 1], bias=nrm[:, 1, c:c + 1])
                        last.then_inc(norm.xT_ready, 1)

                    def main(i, u):
                        n = 2 * i + u
                        for t in range(GT):
                            tile = GT * n + t
                            v = t % 2
                            for a in range(2):
                                wait_at(act, xz_psum, 2 * tile + (a + 1), ready)
                                wait_at(act, silu_ready, 2 * tile + (a + 3), ready)
                                act.activation(sg[:, a, :], pxz[:, v, a, :], ACT.Sigmoid).then_inc(sg_ready, 1)
                            wait_at(act, bc_psum, tile + 1, ready)
                            act.activation(raw[:, bass.ds(tile, 1), :].rearrange("p o d -> p (o d)"),
                                           pbc[:, v, 0:PC + TH], ACT.Copy).then_inc(raw_ready, 1)
                        act.sem_inc(norm.xT_free, 1)

                    act.sem_inc(norm.xT_free, 2)
                    act.sem_inc(norm.xn_free, 2)
                    act.sem_inc(norm.xT_ready, 1)
                    act.sem_inc(raw_ready, 2)
                    act.wait_ge(w_landed, 48)
                    first(0, 0)
                    with act.Fori(0, last_i) as i:
                        for u in range(2):
                            first(*ahead(i, u))
                            main(i, u)
                    first(last_i, 1)
                    main(last_i, 0)
                    main(last_i, 1)

                @block.tensor
                def _(pe):
                    def main(i, u):
                        n = 2 * i + u
                        norm.kept(pe, ready, i, u)
                        for t in range(GT):
                            tile = GT * n + t
                            v = t % 2
                            tokens = slice(t * P, (t + 1) * P)
                            for a in range(2):
                                wait_at(pe, silu_ready, 2 * tile + (a + 1), ready)
                                for c in range(KC):
                                    last = pe.matmul(pxz[:, v, a, :], xi[:, u, c, tokens], w[:, c, a * MI:(a + 1) * MI],
                                                     start=(c == 0), stop=(c == KC - 1))
                                last.then_inc(xz_psum, 1)
                            wait_at(pe, raw_ready, tile + 1, ready)
                            for c in range(KC):
                                pe.matmul(pbc[:, v, 0:PC], xi[:, u, c, tokens], w[:, c, 2 * MI:],
                                          start=(c == 0), stop=(c == KC - 1))
                            for c in range(KC):
                                last = pe.matmul(pbc[:, v, PC:PC + TH], norm.xT[:, u, c, tokens], theta_w[:, c, :],
                                                 start=(c == 0), stop=(c == KC - 1))
                            last.then_inc(bc_psum, 1)

                    pe.wait_ge(w_landed, 48)
                    norm.turn(pe, ready, const, 0, 0)
                    with pe.Fori(0, last_i) as i:
                        for u in range(2):
                            main_first = ahead(i, u)
                            norm.kept(pe, ready, i, u)
                            norm.turn(pe, ready, const, *main_first)
                            main(i, u)
                    norm.kept(pe, ready, last_i, 0)
                    norm.turn(pe, ready, const, last_i, 1)
                    main(last_i, 0)
                    main(last_i, 1)
            r.clear()

        with ExitStack() as ectx:
            r = Space(nc, ectx, "mamba_each")
            tri = const.tri
            vs = r.sb("vs", [P, 2, TILES * TH])
            v = vs[:, 0].rearrange("p (t d) -> p t d", d=TH)
            vp = vs[:, 1].rearrange("p (b t d) -> p b t d", t=CH, d=TH)
            cum = r.sb("cum", [P, TILES, MH])
            la = to_end
            e, q, lam, ends = grown, skip, across, across
            cparts = r.sb("cparts", [P, TILES, 3, MH], BF16)
            f = r.sb("f", [P, TILES, MH])
            dt = r.sb("dt", [P, TILES, MH])
            w2 = r.sb("w2", [P, TILES, MH])
            neg_a = r.sb("neg_a", [P, MH])
            tmean = r.sb("tmean", [P, TILES])
            phi = r.sb("phi", [P, TILES, 2, TH])
            turns = r.sb("turns", [P, TILES, 2, TH])
            ms = r.sb("ms", [P, TILES, 2])
            rms = r.sb("rms", [P, TILES, 2])
            big = vs[:].rearrange("p a (t x d) -> p (a t) x d", x=2, d=TH)
            big2 = turns
            gd = r.sb("gd", [P, TILES])
            pphi = r.ps("pphi", [P, 2, 512])
            pcum = r.ps("pcum", [P, 512])
            pend = r.ps("pend", [P, 512])
            pshift = r.ps("pshift", [P, 512])
            pparts = r.ps("pparts", [P, 2, TILES // 4, P], BF16)
            parts_ready, parts_psum = r.sem("parts_ready"), r.sem("parts_psum")
            parts_kept = r.sem("parts_kept")
            chain = r.sem("chain")
            a_ready, neg_ready, lam_ready, sin_ready = r.sem("a_ready"), r.sem("neg_ready"), r.sem("lam_ready"), r.sem("sin_ready")
            v_ready, sums_ready, gr_ready = r.sem("v_ready"), r.sem("sums_ready"), r.sem("gr_ready")
            abs_ready, angle_ready, cum_ready = r.sem("abs_ready"), r.sem("angle_ready"), r.sem("cum_ready")
            ms_ready, rms_ready = r.sem("ms_ready"), r.sem("rms_ready")
            dt_bias, a_log, d_row = (rows[:, 4 * NS + k * MH:4 * NS + (k + 1) * MH] for k in range(3))

            def over_tiles(row, n):
                return row.unsqueeze(1).to_broadcast([P, TILES, n])

            with nc.Block() as block:

                @block.scalar
                def _(act):
                    act.wait_ge(rows_landed, 16)
                    act.activation(neg_a[:], a_log, ACT.Exp).then_inc(a_ready, 1)
                    act.wait_ge(abs_ready, 1)
                    act.activation(e[:], e[:], ACT.Exp, scale=-1.0).then_inc(neg_ready, 1)
                    act.activation(lam[:], raw[:, :, 2 * NS + MH:PC], ACT.Sigmoid).then_inc(lam_ready, 1)
                    act.wait_ge(angle_ready, 1)
                    act.activation(phi[:], phi[:], ACT.Sin).then_inc(sin_ready, 1)
                    act.wait_ge(cum_ready, 1)
                    act.activation(grown[:], cum[:], ACT.Exp).then_inc(gr_ready, 1)
                    act.activation(to_end[:], to_end[:], ACT.Exp).then_inc(gr_ready, 1)
                    act.activation(across[:], ends[:], ACT.Exp).then_inc(gr_ready, 1)
                    act.sem_inc(parts_kept, 2)
                    for k in range(4):
                        act.wait_ge(parts_psum, k + 1)
                        act.activation(cumT[:, k * TILES // 4:(k + 1) * TILES // 4, :], pparts[0:3 * MH, k % 2],
                                       ACT.Copy).then_inc(parts_kept, 1)

                @block.gpsimd
                def _(pool):
                    pool.wait_ge(ms_ready, 1)
                    pool.tensor_tensor(rms[:], ms[:], const.minus_half[:].rearrange("p (a b) -> p a b", b=2), ALU.pow
                                       ).then_inc(rms_ready, 1)

                @block.tensor
                def _(pe):
                    pe.wait_ge(v_ready, 1)
                    flat_v, flat_vp = vs[:, 0], vs[:, 1]
                    flat_la, flat_w2 = la[:].rearrange("p t d -> p (t d)"), w2[:].rearrange("p t d -> p (t d)")
                    for k in range(2):
                        part = slice(512 * k, 512 * k + 512)
                        pe.matmul(pphi[:, k, :], const.tri[:], flat_v[:, part], start=True, stop=False)
                        pe.matmul(pphi[:, k, :], const.ones[:], flat_vp[:, part], start=False, stop=True)
                    pe.matmul(pcum[:], const.tri[:], flat_la, start=True, stop=True)
                    pe.matmul(pend[:], const.ones[:], flat_la, start=True, stop=True)
                    pe.matmul(pshift[:], const.shift[:], flat_w2, start=True, stop=False)
                    w2_next = w2[:].rearrange("p (b t) h -> p b t h", t=CH)[:, :, 1:CH, :]
                    shift_out = pshift[:].rearrange("p (b t h) -> p b t h", t=CH, h=MH)[:, :, 0:CH - 1, :]
                    pe.matmul(shift_out, const.wrap[:], w2_next, start=False, stop=True).then_inc(sums_ready, 1)
                    pe.wait_ge(parts_ready, 1)
                    for k in range(4):
                        pe.wait_ge(parts_kept, k + 1)
                        for t in range(TILES // 4):
                            last = pe.transpose(pparts[0:3 * MH, k % 2, t, :],
                                                cparts[:, k * TILES // 4 + t].rearrange("p a h -> p (a h)"),
                                                const.ident_b[:])
                        last.then_inc(parts_psum, 1)

                @block.vector
                def _(dve):
                    steps = 0

                    def link(ins, also=None):
                        nonlocal steps
                        if also is not None:
                            ins.then_inc(also, 1)
                            dve.wait_ge(also, 1)
                            return
                        steps += 1
                        ins.then_inc(chain, 1)
                        dve.wait_ge(chain, steps)

                    tt, ts, stt = dve.tensor_tensor, dve.tensor_scalar, dve.scalar_tensor_tensor
                    dve.wait_ge(rows_landed, 16)
                    link(tt(dt[:], raw[:, :, 2 * NS:2 * NS + MH], over_tiles(dt_bias, MH), ALU.add))
                    link(ts(q[:], dt[:], -1.0, None, ALU.mult))
                    link(tt(e[:], dt[:], q[:], ALU.max), abs_ready)
                    link(ts(dt[:], dt[:], 0.0, None, ALU.max))
                    bcr = raw[:, :, 0:2 * NS]
                    halves = bcr.rearrange("p t (a d) -> p t a d", a=2)
                    link(tt(bc[:], bcr, bcr, ALU.mult))
                    link(dve.tensor_reduce(ms[:], bc[:].rearrange("p t (a d) -> p t a d", a=2), AX.X, ALU.add))
                    link(ts(ms[:], ms[:], 1.0 / NS, RMS2_EPS, ALU.mult, ALU.add), ms_ready)
                    dve.wait_ge(neg_ready, 1)
                    link(ts(f[:], e[:], 2.0, None, ALU.add))
                    link(dve.reciprocal(f[:], f[:]))
                    link(tt(e[:], e[:], f[:], ALU.mult))
                    link(tt(q[:], e[:], e[:], ALU.mult))
                    link(ts(f[:], q[:], 1.0 / 17, None, ALU.mult))
                    for k in range(15, 1, -2):
                        link(stt(out=f[:], in0=f[:], scalar=1.0 / k, in1=q[:], op0=ALU.add, op1=ALU.mult))
                    link(stt(out=f[:], in0=f[:], scalar=1.0, in1=e[:], op0=ALU.add, op1=ALU.mult))
                    link(stt(out=dt[:], in0=f[:], scalar=2.0, in1=dt[:], op0=ALU.mult, op1=ALU.add))
                    dve.wait_ge(a_ready, 1)
                    link(ts(neg_a[:], neg_a[:], -1.0, None, ALU.mult))
                    link(tt(la[:], dt[:], over_tiles(neg_a[:], MH), ALU.mult))
                    link(dve.tensor_reduce(tmean[:], dt[:], AX.X, ALU.add))
                    link(stt(out=tmean[:], in0=tmean[:], scalar=1.0 / MH, in1=unscale[:], op0=ALU.mult, op1=ALU.mult))
                    link(tt(v, raw[:, :, PC:], tmean[:].unsqueeze(2).to_broadcast([P, TILES, TH]), ALU.mult))
                    v4 = v.rearrange("p (b t) d -> p b t d", t=CH)
                    link(dve.memset(vp[:, :, 0, :], 0.0))
                    for t in range(1, CH):
                        link(tt(vp[:, :, t, :], vp[:, :, t - 1, :], v4[:, :, t - 1, :], ALU.add))
                    dve.wait_ge(lam_ready, 1)
                    link(tt(weight[:], dt[:], lam[:], ALU.mult))
                    link(tt(w2[:], dt[:], weight[:], ALU.subtract), v_ready)
                    dve.wait_ge(rms_ready, 1)
                    bc4 = bc[:].rearrange("p t (a d) -> p t a d", a=2)
                    link(tt(bc4, halves, rms[:].unsqueeze(3).to_broadcast([P, TILES, 2, NS]), ALU.mult))
                    link(tt(bc[:], bc[:], over_tiles(rows[:, 0:2 * NS], 2 * NS), ALU.mult))
                    link(tt(bc[:], bc[:], over_tiles(rows[:, 2 * NS:4 * NS], 2 * NS), ALU.add))
                    dve.wait_ge(sums_ready, 1)
                    phase = pphi[:].rearrange("p a (t d) -> p (a t) d", d=TH)
                    link(dve.tensor_copy(phi[:, :, 0, :], phase))
                    link(ts(phi[:, :, 1, :], phi[:, :, 0, :], HALF_PI, None, ALU.add))
                    link(ts(turns[:], phi[:], 1.0 / TWO_PI, ROUND, ALU.mult, ALU.add))
                    link(ts(turns[:], turns[:], ROUND, None, ALU.subtract))
                    for part in (6.28125, 0.0019340515136718750, TWO_PI - 6.28125 - 0.0019340515136718750):
                        link(stt(out=phi[:], in0=turns[:], scalar=-part, in1=phi[:], op0=ALU.mult, op1=ALU.add))
                    link(ts(phi[:], phi[:], PI, -PI, ALU.min, ALU.max), angle_ready)
                    link(dve.tensor_copy(cum[:], pcum[:].rearrange("p (t h) -> p t h", h=MH)))
                    link(dve.tensor_copy(cparts[:, :, 0, :], cum[:]))
                    link(tt(f[:], cum[:], cparts[:, :, 0, :], ALU.subtract))
                    link(dve.tensor_copy(cparts[:, :, 1, :], f[:]))
                    link(tt(f[:], f[:], cparts[:, :, 1, :], ALU.subtract))
                    link(dve.tensor_copy(cparts[:, :, 2, :], f[:]), parts_ready)
                    link(dve.tensor_copy(ends[:], pend[:].rearrange("p (t h) -> p t h", h=MH)))
                    link(tt(to_end[:], ends[:], cum[:], ALU.subtract), cum_ready)
                    nxt = pshift[:].rearrange("p (t h) -> p t h", h=MH)
                    link(dve.tensor_copy(w2[:], nxt))
                    link(tt(weight[:], weight[:], w2[:], ALU.add))
                    dve.wait_ge(sin_ready, 1)
                    sine = phi[:, :, 0, :].unsqueeze(2).to_broadcast([P, TILES, 2, TH])
                    cosine = phi[:, :, 1, :].unsqueeze(2).to_broadcast([P, TILES, 2, TH])
                    re, im = bc4[:, :, :, 0:TH], bc4[:, :, :, TH:NS]
                    link(tt(big, im, sine, ALU.mult))
                    link(tt(big2[:], re, sine, ALU.mult))
                    link(tt(re, re, cosine, ALU.mult))
                    link(tt(im, im, cosine, ALU.mult))
                    link(tt(re, re, big, ALU.subtract))
                    link(tt(im, im, big2[:], ALU.add))
                    dot = big.rearrange("p t a d -> p t (a d)")
                    link(tt(dot, bc[:, :, 0:NS], bc[:, :, NS:2 * NS], ALU.mult))
                    link(dve.tensor_reduce(gd[:], dot, AX.X, ALU.add))
                    link(tt(w2[:], w2[:], gd[:].unsqueeze(2).to_broadcast([P, TILES, MH]), ALU.mult))
                    link(tt(skip[:], over_tiles(d_row, MH), w2[:], ALU.subtract))
                    dve.wait_ge(gr_ready, 3)
                    link(tt(to_end[:], to_end[:], weight[:], ALU.mult))
            r.clear()
        rctx.close()

        with ExitStack() as sctx:
            r = Space(nc, sctx, "mamba_scan")
            wout = r.sb("wout", [P, CH, D])
            zg = r.sb("zg", [P, 2, 2, MI])
            bcs = r.sb("bcs", [P, 2, 2 * NS])
            bcT = r.sb("bcT", [NS, 2, 2, P])
            cneg = r.sb("cneg", [3 * MH, 2, P], BF16)
            decay = r.sb("decay", [P, MH, P])
            mat = r.sb("mat", [P, MH, P])
            gsb = r.sb("gsb", [P, 2, P])
            xw = r.sb("xw", [P, 2, MH, HP])
            xe = r.sb("xe", [P, 2, MH, HP])
            xd = r.sb("xd", [P, 2, MH, HP])
            state = r.sb("state", [NS, MH, HP])
            y = r.sb("y", [P, 2, MH, HP])
            yT = r.sb("yT", [P, MI // P, P])
            un = r.sb("un", [P, D])
            p_la = r.ps("p_la", [P, MH, P])
            p_y = r.ps("p_y", [P, 512])
            p_in = r.ps("p_in", [P, 512])
            p_st = r.ps("p_st", [P, 512])
            p_m = r.ps("p_m", [P, 512])
            wout_landed = r.sem("wout_landed")
            zg_landed, zg_free = r.sems("zg_landed", 2), r.sems("zg_free", 2)
            xe_ready, xw_ready, xd_ready = r.sem("xe_ready"), r.sem("xw_ready"), r.sem("xd_ready")
            copies_ready = r.sem("copies_ready")
            sum_psum, exp_ready = r.sem("sum_psum"), r.sem("exp_ready")
            bcT_psum, bcT_ready, g_psum, g_ready = r.sem("bcT_psum"), r.sem("bcT_ready"), r.sem("g_psum"), r.sem("g_ready")
            mat_ready, in_psum, intra_psum = r.sem("mat_ready"), r.sem("in_psum"), r.sem("intra_psum")
            st_psum = r.sem("st_psum")
            state_ready = r.sem("state_ready")
            grown_ready, scaled_ready, skip_ready = r.sem("grown_ready"), r.sem("scaled_ready"), r.sem("skip_ready")
            added_ready = r.sem("added_ready")
            y_ready = r.sem("y_ready")
            yT_psum, yT_ready, out_psum = r.sem("yT_psum"), r.sem("yT_ready"), r.sem("out_psum")
            un_ready, res_ready = r.sem("un_ready"), r.sem("res_ready")
            out_ready = r.sem("out_ready")

            def of(tensor, k):
                return tensor[:, bass.ds(k, 1), :].rearrange("p o h -> p (o h)")

            def over_chunks(eng, step):
                with eng.Fori(0, BATCH - 1) as n:
                    for t in range(CH):
                        step(n, t, CH * n + t, True)
                for t in range(CH):
                    step(BATCH - 1, t, CH * (BATCH - 1) + t, t < CH - 1)

            with nc.Block() as block:

                @block.sync
                def _(sp):
                    zg_in = gz_dram.rearrange("(g t p) d -> g p t d", t=CH, p=P)
                    sp.dma_start(wout[:], wout_dram).then_inc(wout_landed, 16)
                    with sp.Fori(0, BATCH) as n:
                        for b in range(2):
                            wait_at(sp, zg_free[b], n + 1, ready)
                            sp.dma_start(zg[:, b], zg_in[bass.ds(n, 1), :, 2 * b:2 * b + 2].rearrange("g p t d -> p (g t) d")
                                         ).then_inc(zg_landed[b], 16)

                @block.gpsimd
                def _(pool):
                    with pool.Fori(0, TILES // 2) as i:
                        for v in range(2):
                            k = 2 * i + v
                            wait_at(pool, y_ready, k + 1, ready)
                            x = xs[:, bass.ds(k, 1), :].rearrange("p o (h d) -> p (o h) d", h=MH)
                            for out, by, count in ((xe, to_end, xe_ready), (xw, weight, xw_ready), (xd, skip, xd_ready)):
                                pool.tensor_tensor(out[:, v], x, of(by, k).unsqueeze(2).to_broadcast([P, MH, HP]), ALU.mult
                                                   ).then_inc(count, 1)

                @block.scalar
                def _(act):
                    def copies(k, v):
                        wait_at(act, st_psum, k, ready)
                        act.activation(bcs[:, v], of(bc, k), ACT.Copy)
                        act.activation(cneg[:, v], of(cumT, k), ACT.Copy, scale=-1.0).then_inc(copies_ready, 1)

                    def turned(k, v):
                        wait_at(act, bcT_psum, k + 1, ready)
                        act.activation(bcT[:, v], p_m[0:NS, 0:2 * P].rearrange("p (a n) -> p a n", a=2), ACT.Copy
                                       ).then_inc(bcT_ready, 1)

                    def decays(k, v):
                        wait_at(act, g_psum, k + 1, ready)
                        act.activation(gsb[:, v], p_in[:, 0:P], ACT.Copy).then_inc(g_ready, 1)
                        wait_at(act, sum_psum, k + 1, ready)
                        if not isinstance(k, int) or k:
                            wait_at(act, mat_ready, k, ready)
                        act.activation(decay[:], p_la[:], ACT.Exp).then_inc(exp_ready, 1)

                    def step(n, t, k, more):
                        v, v1 = t % 2, (t + 1) % 2
                        if more:
                            copies(k + 1, v1)
                            turned(k + 1, v1)
                        wait_at(act, yT_psum, k + 1, ready)
                        act.activation(yT[:], p_y[:].rearrange("p (a n) -> p a n", n=P), ACT.Copy).then_inc(yT_ready, 1)
                        if more:
                            decays(k + 1, v1)

                    act.activation(bcs[:, 0], of(bc, 0), ACT.Copy)
                    act.activation(cneg[:, 0], of(cumT, 0), ACT.Copy, scale=-1.0).then_inc(copies_ready, 1)
                    turned(0, 0)
                    decays(0, 0)
                    over_chunks(act, step)

                @block.tensor
                def _(pe):
                    def differences(k, v):
                        wait_at(pe, copies_ready, k + 1, ready)
                        if not isinstance(k, int) or k:
                            wait_at(pe, exp_ready, k, ready)
                        for b in range(4):
                            heads = slice(4 * b, 4 * b + 4)
                            pe.matmul(p_la[:, heads, :], cneg[:, v], const.pick[:, heads, :], start=True, stop=False,
                                      skip_group_check=True)
                            for h in range(4 * b, 4 * b + 4):
                                pe.matmul(p_la[:, h, :], const.pick[:, h, :], of(cumT, k), start=False, stop=False,
                                          skip_group_check=True)
                            last = pe.matmul(p_la[:, heads, :], const.ident_b[:],
                                             const.never[:].unsqueeze(1).to_broadcast([P, 4, P]), start=False, stop=True,
                                             skip_group_check=True)
                        last.then_inc(sum_psum, 1)

                    def turn(k, v):
                        wait_at(pe, out_ready, k, ready)
                        for a in range(2):
                            last = pe.transpose(p_m[0:NS, a * P:(a + 1) * P], bcs[:, v, a * NS:(a + 1) * NS], const.ident[:])
                        last.then_inc(bcT_psum, 1)

                    def products(k, v):
                        wait_at(pe, bcT_ready, k + 1, ready)
                        pe.matmul(p_in[:, 0:P], bcT[:, v, 0, :], bcT[:, v, 1, :], start=True, stop=True).then_inc(g_psum, 1)

                    def step(n, t, k, more):
                        v, v1 = t % 2, (t + 1) % 2
                        wait_at(pe, state_ready, k + 1, ready)
                        wait_at(pe, g_ready, k + 1, ready)
                        pe.matmul(p_in[:], bcT[:, v, 1, :], state[:].rearrange("p h d -> p (h d)"), start=True, stop=True
                                  ).then_inc(in_psum, 1)
                        wait_at(pe, xe_ready, k + 1, ready)
                        pe.matmul(p_st[0:NS, :], bcs[:, v, 0:NS], xe[:, v].rearrange("p h d -> p (h d)"), start=True, stop=True
                                  ).then_inc(st_psum, 1)
                        wait_at(pe, xw_ready, k + 1, ready)
                        wait_at(pe, mat_ready, k + 1, ready)
                        for h in range(MH):
                            last = pe.matmul(p_y[:, h * HP:(h + 1) * HP], mat[:, h, :], xw[:, v, h, :], start=True, stop=True)
                        last.then_inc(intra_psum, 1)
                        if more:
                            differences(k + 1, v1)
                            turn(k + 1, v1)
                        wait_at(pe, y_ready, k + 3, ready)
                        for a in range(MI // P):
                            last = pe.transpose(p_y[:, a * P:(a + 1) * P],
                                                y[:, v, a * (P // HP):(a + 1) * (P // HP), :].rearrange("p h d -> p (h d)"),
                                                const.ident[:])
                        last.then_inc(yT_psum, 1)
                        if more:
                            products(k + 1, v1)
                        wait_at(pe, yT_ready, k + 1, ready)
                        for a in range(MI // P):
                            last = pe.matmul(p_m[:, 0:D], yT[:, a, :], wout[:, a, :], start=(a == 0), stop=(a == MI // P - 1))
                        last.then_inc(out_psum, 1)

                    pe.sem_inc(st_psum, 1)
                    pe.wait_ge(wout_landed, 16)
                    differences(0, 0)
                    for a in range(2):
                        last = pe.transpose(p_m[0:NS, a * P:(a + 1) * P], bcs[:, 0, a * NS:(a + 1) * NS], const.ident[:])
                    last.then_inc(bcT_psum, 1)
                    products(0, 0)
                    over_chunks(pe, step)

                @block.vector
                def _(dve):
                    tt, ts = dve.tensor_tensor, dve.tensor_scalar

                    def decayed(k, v):
                        wait_at(dve, g_ready, k + 1, ready)
                        wait_at(dve, exp_ready, k + 1, ready)
                        tt(mat[:], decay[:], gsb[:, v].unsqueeze(1).to_broadcast([P, MH, P]), ALU.mult).then_inc(mat_ready, 1)

                    def step(n, t, k, more):
                        v, v1 = t % 2, (t + 1) % 2
                        x = x_all[:].rearrange("p g t d -> p (g t) d")[:, bass.ds(k, 1), :].rearrange("p o d -> p (o d)")
                        ts(un[:], x, mean1[:, bass.ds(k, 1)], root1[:, bass.ds(k, 1)], ALU.subtract, ALU.mult
                           ).then_inc(un_ready, 1)
                        wait_at(dve, in_psum, k + 1, ready)
                        tt(y[:, v], p_in[:].rearrange("p (h d) -> p h d", h=MH),
                           of(grown, k).unsqueeze(2).to_broadcast([P, MH, HP]), ALU.mult).then_inc(scaled_ready, 1)
                        wait_at(dve, st_psum, k + 2, ready)
                        if t < CH - 1:
                            tt(state[:], state[:], across[0:NS, bass.ds(k, 1), :].rearrange("p o h -> p (o h)")
                               .unsqueeze(2).to_broadcast([NS, MH, HP]), ALU.mult).then_inc(grown_ready, 1)
                            wait_at(dve, un_ready, k + 1, ready)
                            tt(x, x, un[:], ALU.add).then_inc(res_ready, 1)
                            wait_at(dve, grown_ready, (CH - 1) * n + (t + 1), ready)
                            tt(state[:], state[:], p_st[0:NS, :].rearrange("p (h d) -> p h d", h=MH), ALU.add
                               ).then_inc(state_ready, 1)
                        else:
                            dve.memset(state[:], 0.0).then_inc(state_ready, 1)
                            wait_at(dve, un_ready, k + 1, ready)
                            tt(x, x, un[:], ALU.add).then_inc(res_ready, 1)
                        wait_at(dve, xd_ready, k + 1, ready)
                        wait_at(dve, scaled_ready, k + 1, ready)
                        tt(y[:, v], y[:, v], xd[:, v], ALU.add).then_inc(skip_ready, 1)
                        wait_at(dve, skip_ready, k + 1, ready)
                        wait_at(dve, intra_psum, k + 1, ready)
                        tt(y[:, v], y[:, v], p_y[:].rearrange("p (h d) -> p h d", h=MH), ALU.add).then_inc(added_ready, 1)
                        wait_at(dve, added_ready, k + 1, ready)
                        if v == 0:
                            wait_at(dve, zg_landed[t // 2], 16 * n + 16, ready)
                        tt(y[:, v], y[:, v], zg[:, t // 2, v].rearrange("p (h d) -> p h d", h=MH), ALU.mult
                           ).then_inc(y_ready, 1)
                        if more:
                            decayed(k + 1, v1)
                        wait_at(dve, out_psum, k + 1, ready)
                        if v:
                            dve.sem_inc(zg_free[t // 2], 1)
                        wait_at(dve, res_ready, k + 1, ready)
                        tt(x, x, p_m[:, 0:D], ALU.add).then_inc(out_ready, 1)

                    dve.sem_inc(y_ready, 2)
                    dve.sem_inc(out_ready, 1)
                    dve.sem_inc(zg_free[0], 1)
                    dve.sem_inc(zg_free[1], 1)
                    dve.memset(state[:], 0.0).then_inc(state_ready, 1)
                    decayed(0, 0)
                    over_chunks(dve, step)

            r.clear()
        s.clear()


def build(nc, a, out):
    def dram(name, width):
        return nc.dram_tensor(name, (TOKENS, width), F32, kind="Internal").ap()

    x1, x2, xn, gz = dram("x1", D), dram("x2", D), dram("xn", D), dram("gz", MI)
    with ExitStack() as ctx:
        const = Constants(nc, ctx)
        lasting = Space(nc, ctx, "all")
        x_all = lasting.sb("x", [P, GROUPS, GT, D])
        experts = (a["router"], a["w1"], a["b1"], a["w2"], a["b2"])
        mixer = (a["rwkv_r"], a["rwkv_k"], a["rwkv_v"], a["mu"])
        moe_stage(nc, lasting, const, "moe_a", True, x_all, a["x"], x1, xn, *experts)
        attention_stage(nc, const, x_all, x1, x2, a["wqkv"], a["wo"], a["attn_norm"], a["gamma"])
        moe_stage(nc, lasting, const, "moe_b", False, x_all, None, x2, xn, *experts)
        rwkv_stage(nc, const, "rwkv_a", True, x_all, x2, None, *mixer)
        mamba_stage(nc, const, x_all, gz, a["in_proj"], a["theta"], a["out_proj"], a["mamba_norm"], a["rows"])
        rwkv_stage(nc, const, "rwkv_b", False, x_all, None, out, *mixer)


def kernel(**inputs):
    import numpy as np
    import concourse.bacc as bacc
    from concourse.bass_utils import run_bass_kernel_spmd

    a = {k: np.asarray(v) for k, v in inputs.items()}
    L0, F0, L1, F1 = "L0_attn_", "L0_ffn_", "L1_attn_", "L1_ffn_"

    def by_chunk(w):
        return w.reshape(w.shape[0] // P, P, -1).transpose(1, 0, 2)

    def columns(*vectors):
        return np.stack(vectors).reshape(len(vectors), -1, P).transpose(2, 0, 1)

    E, S, M, K = EXPERTS, SLOTS, HID, YK
    layout = {
        "x": a[L0 + "tokens"].reshape(TOKENS, D),
        "router": by_chunk(a[F0 + "Wr"].T),
        "w1": a[F0 + "W1"].reshape(E, S, KC, P, M).transpose(0, 3, 2, 1, 4).reshape(E, P, KC, S * M),
        "b1": a[F0 + "b1"].reshape(E, HC, P).transpose(2, 0, 1),
        "w2": a[F0 + "W2"].reshape(E, HC, P, K).transpose(0, 2, 1, 3),
        "b2": a[F0 + "b2"].reshape(E, D),
        "wqkv": by_chunk(np.concatenate([a[L0 + "Wq"], a[L0 + "Wkv"]], 1)),
        "wo": by_chunk(a[L0 + "Wo"]),
        "attn_norm": columns(a[L0 + "norm_w"])[:, 0],
        "gamma": columns(a[L0 + "q_gamma"], a[L0 + "k_gamma"]),
        "rwkv_r": by_chunk(a[F1 + "W_r"].T),
        "rwkv_k": by_chunk(a[F1 + "W_k"].T),
        "rwkv_v": by_chunk(a[F1 + "W_v"].T),
        "mu": columns(a[F1 + "mu_r"], a[F1 + "mu_k"]),
        "in_proj": by_chunk(a[L1 + "in_proj_w"]),
        "theta": by_chunk(a[L1 + "theta_w"]),
        "out_proj": by_chunk(a[L1 + "out_proj_w"]),
        "mamba_norm": columns(a[L1 + "norm_scale"], a[L1 + "norm_bias"]),
        "rows": np.concatenate([a[L1 + n] for n in ("bcB_scale", "bcC_scale", "B_bias", "C_bias", "dt_bias", "A_log", "D")]),
    }
    nc = bacc.Bacc("TRN2", target_bir_lowering=False, num_devices=1)
    arrays, aps = {}, {}
    for name, value in layout.items():
        arrays["in_" + name] = np.ascontiguousarray(value)
        aps[name] = nc.dram_tensor("in_" + name, value.shape, mybir.dt.from_np(value.dtype), kind="ExternalInput").ap()
    out = nc.dram_tensor("out", (TOKENS, D), F32, kind="ExternalOutput").ap()
    build(nc, aps, out)
    result = run_bass_kernel_spmd(nc, [arrays], core_ids=[0])
    return result.results[0]["out"].reshape(BATCH, SEQ, D)
```

```python
from contextlib import ExitStack

import concourse.bass as bass
from concourse import mybir

F32 = mybir.dt.float32
BF16 = mybir.dt.bfloat16
F32R = mybir.dt.float32r
U32 = mybir.dt.uint32
ALU = mybir.AluOpType
ACT = mybir.ActivationFunctionType
AX = mybir.AxisListType

P = 128
D = 256
KC = D // P
SEQ = 512
BATCH = 8
TOKENS = BATCH * SEQ
GT = SEQ // P
GROUPS = TOKENS // SEQ
LN_EPS = 1e-5


def wait_at(eng, sem, count, ready):
    if isinstance(count, int):
        eng.wait_ge(sem, count)
        return
    value = eng.snap(eng.to_reg(count))
    eng.wait_ge(ready, 1)
    eng.wait_ge(sem, value)


def ahead(i, u, k=1):
    return i + (u + k) // 2, (u + k) % 2


class Space:

    def __init__(self, nc, ctx, prefix):
        self.nc, self.ctx, self.prefix, self.counts = nc, ctx, prefix, []

    def sb(self, name, shape, dtype=F32):
        return self.ctx.enter_context(self.nc.sbuf_tensor(f"{self.prefix}_{name}", shape, dtype))

    def ps(self, name, shape, dtype=F32):
        return self.ctx.enter_context(self.nc.psum_tensor(f"{self.prefix}_{name}", shape, dtype))

    def sem(self, name):
        count = self.ctx.enter_context(self.nc.semaphore(f"{self.prefix}_{name}"))
        self.counts.append(count)
        return count

    def clear(self):
        numbers = sorted(c.num for c in self.counts)
        start = 0
        for k in range(1, len(numbers) + 1):
            if k == len(numbers) or numbers[k] != numbers[k - 1] + 1:
                self.nc.gpsimd.sem_clear(range(numbers[start], numbers[k - 1] + 1))
                start = k
        self.nc.all_engine_barrier()

    def sems(self, name, n):
        return [self.sem(f"{name}{k}") for k in range(n)]


class Constants:

    def __init__(self, nc, ctx):
        s = Space(nc, ctx, "const")
        self.ident = s.sb("ident", [P, P])
        self.ones = s.sb("ones", [P, P])
        self.flip = s.sb("flip", [P, P])
        self.first = s.sb("first", [P, P])
        self.last = s.sb("last", [P, P])
        self.tri = s.sb("tri", [P, P])
        self.shift = s.sb("shift", [P, P])
        self.wrap = s.sb("wrap", [P, P])
        self.ident_b = s.sb("ident_b", [P, P], BF16)
        self.never = s.sb("never", [P, P], BF16)
        self.pick = s.sb("pick", [3 * 16, 16, P], BF16)
        self.minus_half = s.sb("minus_half", [P, 64])
        self.half_offset = s.sb("half_offset", [P, 1])
        self.ready = s.sem("ready")
        made = s.sem("made")
        with nc.Block() as block:

            @block.gpsimd
            def _(pool):
                pool.memset(self.minus_half[:], -0.5)
                pool.memset(self.ones[:], 1.0).then_inc(made, 1)
                pool.memset(self.half_offset[:], float(TOKENS // 2)).then_inc(made, 1)
                pool.wait_ge(made, 2)
                pool.affine_select(out=self.half_offset[:], in_=self.half_offset[:], pattern=[[0, 1]],
                                   compare_op=ALU.is_ge, fill=0.0, base=-64, channel_multiplier=1)
                for out, pattern, base, cm in (
                    (self.ident, [[-1, P]], 0, 1),
                    (self.flip, [[1, P]], -(P - 1), 1),
                    (self.first, [[0, P]], 0, 1),
                    (self.last, [[0, P]], -(P - 1), 1),
                ):
                    pool.affine_select(out=out[:], in_=self.ones[:], pattern=pattern, compare_op=ALU.is_equal,
                                       fill=0.0, base=base, channel_multiplier=cm)
                pool.affine_select(out=self.tri[:], in_=self.ones[:], pattern=[[1, P]], compare_op=ALU.is_ge,
                                   fill=0.0, base=0, channel_multiplier=-1)
                pool.affine_select(out=self.shift[:], in_=self.ones[:], pattern=[[-1, P]], compare_op=ALU.is_equal,
                                   fill=0.0, base=-1, channel_multiplier=1)
                pool.affine_select(out=self.ident_b[:], in_=self.ones[:], pattern=[[-1, P]], compare_op=ALU.is_equal,
                                   fill=0.0, base=0, channel_multiplier=1)
                pool.memset(self.never[:], 0.0).then_inc(made, 1)
                pool.memset(self.wrap[:], 0.0).then_inc(made, 1)
                pool.memset(self.pick[:], 0.0).then_inc(made, 1)
                pool.wait_ge(made, 5)
                for part in range(3):
                    pool.affine_select(out=self.pick[:], in_=self.pick[:], pattern=[[-1, 16], [0, P]],
                                       compare_op=ALU.not_equal, fill=1.0, base=-16 * part, channel_multiplier=1
                                       ).then_inc(made, 1)
                    pool.wait_ge(made, 6 + part)
                pool.affine_select(out=self.never[:], in_=self.never[:], pattern=[[1, P]], compare_op=ALU.is_ge,
                                   fill=-1e30, base=0, channel_multiplier=-1)
                pool.affine_select(out=self.wrap[:], in_=self.wrap[:], pattern=[[-1, P]], compare_op=ALU.not_equal,
                                   fill=1.0, base=P - 1, channel_multiplier=1)
                pool.drain().then_inc(self.ready, 1)


class Norm:

    def __init__(self, s, x, banks=2, lead=0, unroll=2, turned=None, eps2=None, dtype=F32):
        self.x = x
        self.unroll, self.eps2 = unroll, eps2
        self.lead, self.banks = lead, banks
        self.xn = s.sb("xn", [P, unroll, GT, D])
        self.stats = s.sb("stats", [P, unroll, GT, 6])
        self.moments = s.sb("moments", [P, unroll, GT, 2])
        self.var = s.sb("var", [P, unroll, GT])
        self.rstd = s.sb("rstd", [P, unroll, GT])
        self.xT = s.sb("xT", [P, unroll, KC, lead + SEQ], dtype)
        self.turned = s.ps("turned", [P, banks, KC, SEQ]) if turned is None else turned
        if eps2 is not None:
            self.eps2_tile = s.sb("eps2_tile", [P, GT])
            self.work = s.sb("work", [P, unroll, 3, GT])
            self.eps2_set = s.sem("eps2_set")
            self.norm2_step = s.sem("norm2_step")
        self.x_landed = s.sems("x_landed", 2)
        self.stats_ready = s.sem("stats_ready")
        self.moments_ready = s.sem("moments_ready")
        self.var_ready = s.sem("var_ready")
        self.rstd_ready = s.sem("rstd_ready")
        self.xn_ready = s.sem("xn_ready")
        self.xn_free = s.sem("xn_free")
        self.xn_stored = None
        self.turned_ready = s.sem("turned_ready")
        self.xT_ready = s.sem("xT_ready")
        self.xT_free = s.sem("xT_free")

    def load(self, sp, ready, x_dram, i, u, group):
        sp.dma_start(self.x[:, bass.ds(group, 1)].rearrange("p g t d -> p (g t) d"),
                     x_dram[bass.ds(group * SEQ, SEQ), :].rearrange("(t p) d -> p t d", p=P)
                     ).then_inc(self.x_landed[u], 16)

    def moments_of(self, dve, ready, i, u, group, loaded=True):
        n1 = self.unroll * i + (u + 1)
        if loaded:
            wait_at(dve, self.x_landed[u], 16 * i + 16, ready)
        x = self.x[:, bass.ds(group, 1)].rearrange("p g t d -> p (g t) d")
        for t in range(GT):
            last = dve.bn_stats(self.stats[:, u, t, :], x[:, t, :])
        last.then_inc(self.stats_ready, 1)
        wait_at(dve, self.stats_ready, n1, ready)
        for t in range(GT):
            last = dve.bn_aggr(self.moments[:, u, t, :], self.stats[:, u, t, :])
        last.then_inc(self.moments_ready, 1)
        wait_at(dve, self.moments_ready, n1, ready)
        dve.tensor_scalar(self.var[:, u, :], self.moments[:, u, :, 1], LN_EPS, None, ALU.add
                          ).then_inc(self.var_ready, 1)

    def root(self, pool, ready, const, i, u):
        n = self.unroll * i + u
        wait_at(pool, self.var_ready, n + 1, ready)
        half = const.minus_half[:, 0:GT]
        if self.eps2 is None:
            pool.tensor_tensor(self.rstd[:, u, :], self.var[:, u, :], half, ALU.pow).then_inc(self.rstd_ready, 1)
            return
        root, ms, fac = (self.work[:, u, k, :] for k in range(3))
        pool.tensor_tensor(root, self.var[:, u, :], half, ALU.pow).then_inc(self.norm2_step, 1)
        wait_at(pool, self.norm2_step, 5 * n + 1, ready)
        pool.tensor_tensor(ms, root, root, ALU.mult).then_inc(self.norm2_step, 1)
        wait_at(pool, self.norm2_step, 5 * n + 2, ready)
        pool.tensor_tensor(ms, ms, self.moments[:, u, :, 1], ALU.mult).then_inc(self.norm2_step, 1)
        wait_at(pool, self.norm2_step, 5 * n + 3, ready)
        pool.tensor_tensor(ms, ms, self.eps2_tile[:], ALU.add).then_inc(self.norm2_step, 1)
        wait_at(pool, self.norm2_step, 5 * n + 4, ready)
        pool.tensor_tensor(fac, ms, half, ALU.pow).then_inc(self.norm2_step, 1)
        wait_at(pool, self.norm2_step, 5 * n + 5, ready)
        pool.tensor_tensor(self.rstd[:, u, :], root, fac, ALU.mult).then_inc(self.rstd_ready, 1)

    def normalise(self, dve, ready, i, u, group):
        n1 = self.unroll * i + (u + 1)
        wait_at(dve, self.rstd_ready, n1, ready)
        wait_at(dve, self.xn_free, n1, ready)
        if self.xn_stored is not None:
            wait_at(dve, self.xn_stored, n1, ready)
        x = self.x[:, bass.ds(group, 1)].rearrange("p g t d -> p (g t) d")
        for t in range(GT):
            last = dve.tensor_scalar(self.xn[:, u, t, :], x[:, t, :], self.moments[:, u, t, 0:1],
                                     self.rstd[:, u, t:t + 1], ALU.subtract, ALU.mult)
        last.then_inc(self.xn_ready, 1)

    def turn(self, pe, ready, const, i, u):
        n1 = self.unroll * i + (u + 1)
        wait_at(pe, self.xn_ready, n1, ready)
        wait_at(pe, self.xT_ready, n1, ready)
        for c in range(KC):
            for t in range(GT):
                last = pe.transpose(self.turned[:, u % self.banks, c, t * P:(t + 1) * P],
                                    self.xn[:, u, t, c * P:(c + 1) * P], const.ident[:])
        last.then_inc(self.turned_ready, 1)

    def keep(self, act, ready, i, u, count=True):
        n1 = self.unroll * i + (u + 1)
        wait_at(act, self.turned_ready, n1, ready)
        act.sem_inc(self.xn_free, 1)
        wait_at(act, self.xT_free, n1, ready)
        copy = act.activation(self.xT[:, u, :, self.lead:], self.turned[:, u % self.banks], ACT.Copy)
        if count:
            copy.then_inc(self.xT_ready, 1)

    def kept(self, eng, ready, i, u):
        wait_at(eng, self.xT_ready, self.unroll * i + (u + 1 + self.banks), ready)


EXPERTS = 48
SLOTS = 4
HID = 256
HC = SLOTS * HID // P
YK = D // SLOTS
CAP = int(1.5 * TOKENS / EXPERTS)
EU = 4
HALF = TOKENS // 2
ROUNDS = CAP // 8


def moe_stage(nc, lasting, const, name, load, x_all, x_dram, acc_dram, xn_dram, wr_dram, w1_dram, b1_dram, w2_dram, b2_dram):
    with ExitStack() as ctx:
        s = Space(nc, ctx, name)
        ready = const.ready
        w1 = s.sb("w1", [P, EU, KC, SLOTS * HID])
        w2 = s.sb("w2", [P, EU, HC, YK])
        b2 = s.sb("b2", [1, EU, D])
        b1 = s.sb("b1", [P, EXPERTS, HC])
        b1_landed = s.sem("b1_landed")
        w_landed = s.sems("w_landed", EU)

        def fetch(sp, e, u):
            sp.dma_start(w1[:, u], w1_dram[bass.ds(e, 1)].rearrange("e p c n -> p (e c) n")).then_inc(w_landed[u], 16)
            sp.dma_start(w2[:, u], w2_dram[bass.ds(e, 1)].rearrange("e p c n -> p (e c) n")).then_inc(w_landed[u], 16)
            sp.dma_start(b2[:, u], b2_dram[bass.ds(e, 1), :]).then_inc(w_landed[u], 16)

        with ExitStack() as rctx:
            r = Space(nc, rctx, name + "_router")
            keep_vals = s.sb("sel_w", [P, EXPERTS])
            index = s.sb("index", [P, EXPERTS], U32)
            norm = Norm(r, x_all)
            wr = r.sb("wr", [P, KC, 64])
            logits = r.sb("logits", [P, HALF])
            vals = r.sb("vals", [P, CAP])
            idx = r.sb("idx", [P, CAP], U32)
            idxf = r.sb("idxf", [P, CAP])
            both = r.sb("both", [P, 2, P])
            swapped = r.sb("swapped", [P, 2, EXPERTS])
            take = r.sb("take", [P, EXPERTS])
            best = r.sb("best", [P, EXPERTS])
            diff = r.sb("diff", [P, EXPERTS])
            token = r.sb("token", [P, EXPERTS])
            top = r.sb("top", [P, 2, EXPERTS])
            peak = r.sb("peak", [P, EXPERTS])
            expo = r.sb("expo", [P, EXPERTS])
            total = r.sb("total", [P, EXPERTS])
            plog = r.ps("plog", [P, 2, SEQ])
            small = r.ps("small", [P, 512])
            small2 = r.ps("small2", [P, 512])
            wr_zero, wr_landed = r.sem("wr_zero"), r.sem("wr_landed")
            norm.xn_stored = r.sem("xn_stored")
            xn_store = r.sems("xn_store", 2)
            acc_set = r.sem("acc_set")
            logits_psum = r.sem("logits_psum")
            logits_kept = r.sem("logits_kept")
            chain = r.sem("topk_chain")
            pe_small, exp_ready = r.sem("pe_small"), r.sem("exp_ready")
            last_i = GROUPS // 2 - 1
            xn_out = xn_dram.rearrange("(g t p) d -> g p t d", t=GT, p=P)

            with nc.Block() as block:

                @block.sync
                def _(sp):
                    sp.wait_ge(wr_zero, 1)
                    sp.dma_start(wr[:, :, 0:EXPERTS], wr_dram).then_inc(wr_landed, 16)
                    def fetch_x(i):
                        for u in range(2):
                            norm.load(sp, ready, x_dram, i, u, i + u * (GROUPS // 2))

                    def store_xn(i):
                        for u in range(2):
                            wait_at(sp, norm.xn_ready, 2 * i + (u + 1), ready)
                            sp.dma_start(xn_out[bass.ds(i + u * (GROUPS // 2), 1)].rearrange("g p t d -> p (g t) d"),
                                         norm.xn[:, u]).then_inc(xn_store[u], 16)
                            wait_at(sp, xn_store[u], 16 * i + 16, ready)
                            sp.sem_inc(norm.xn_stored, 1)

                    sp.sem_inc(norm.xn_stored, 2)
                    if load:
                        fetch_x(0)
                    with sp.Fori(0, last_i) as i:
                        if load:
                            for u in range(2):
                                wait_at(sp, norm.x_landed[u], 16 * i + 16, ready)
                            fetch_x(i + 1)
                        store_xn(i)
                    store_xn(last_i)
                    if load:
                        sp.dma_start(acc_dram.rearrange("(a p) d -> p a d", p=P),
                                     x_dram.rearrange("(a p) d -> p a d", p=P)).then_inc(acc_set, 16)
                    for u in range(EU):
                        fetch(sp, u, u)
                    sp.dma_start(b1[:], b1_dram).then_inc(b1_landed, 16)
                    if load:
                        sp.wait_ge(acc_set, 16)

                @block.vector
                def _(dve):
                    dve.memset(wr[:], 0.0).then_inc(wr_zero, 1)

                    def moments(i, u):
                        norm.moments_of(dve, ready, i, u, i + u * (GROUPS // 2), load)

                    def normalise(i, u):
                        norm.normalise(dve, ready, i, u, i + u * (GROUPS // 2))

                    moments(0, 0)
                    with dve.Fori(0, last_i) as i:
                        for u in range(2):
                            moments(*ahead(i, u))
                            normalise(i, u)
                    moments(last_i, 1)
                    normalise(last_i, 0)
                    normalise(last_i, 1)
                    steps = 0

                    def link(ins):
                        nonlocal steps
                        steps += 1
                        ins.then_inc(chain, 1)
                        dve.wait_ge(chain, steps)

                    dve.wait_ge(logits_kept, GROUPS + 2)
                    for k in range(ROUNDS):
                        eight = vals[:, 8 * k:8 * k + 8]
                        link(dve.max(eight, logits[:]))
                        link(dve.max_index(idx[:, 8 * k:8 * k + 8], eight, logits[:]))
                        if k < ROUNDS - 1:
                            link(dve.match_replace(logits[:], eight, logits[:], -3.4e38))
                    link(dve.tensor_copy(idxf[:], idx[:]))
                    link(dve.tensor_scalar(idxf[:], idxf[:], const.half_offset[:, 0:1], None, ALU.add))
                    dve.wait_ge(pe_small, 1)
                    link(dve.tensor_copy(both[:], small[:, 0:2 * P].rearrange("p (a b) -> p a b", a=2)))
                    dve.wait_ge(pe_small, 2)
                    link(dve.tensor_copy(swapped[:], small2[:, 0:2 * EXPERTS].rearrange("p (a b) -> p a b", a=2)))
                    link(dve.tensor_tensor(take[:], both[:, 0, 0:EXPERTS], swapped[:, 0, :], ALU.is_ge))
                    link(dve.tensor_tensor(best[:], both[:, 0, 0:EXPERTS], swapped[:, 0, :], ALU.max))
                    link(dve.tensor_tensor(diff[:], both[:, 1, 0:EXPERTS], swapped[:, 1, :], ALU.subtract))
                    link(dve.tensor_tensor(diff[:], diff[:], take[:], ALU.mult))
                    link(dve.tensor_tensor(token[:], diff[:], swapped[:, 1, :], ALU.add))
                    link(dve.tensor_copy(index[:], token[:]))
                    dve.wait_ge(pe_small, 3)
                    link(dve.tensor_copy(top[:], small[:, 256:256 + 2 * EXPERTS].rearrange("p (a b) -> p a b", a=2)))
                    link(dve.tensor_tensor(peak[:], top[:, 0, :], top[:, 1, :], ALU.max))
                    link(dve.tensor_tensor(best[:], best[:], peak[:], ALU.subtract))
                    dve.wait_ge(pe_small, 4)
                    link(dve.reciprocal(total[:], small2[:, 256:256 + EXPERTS]))
                    link(dve.scalar_tensor_tensor(out=keep_vals[:], in0=expo[:], scalar=0.5, in1=total[:],
                                                  op0=ALU.mult, op1=ALU.mult))

                @block.gpsimd
                def _(pool):
                    with pool.Fori(0, GROUPS // 2) as i:
                        for u in range(2):
                            norm.root(pool, ready, const, i, u)

                @block.tensor
                def _(pe):
                    pe.wait_ge(wr_landed, 16)

                    def route(i, u):
                        norm.kept(pe, ready, i, u)
                        wait_at(pe, logits_kept, 2 * i + (u + 1), ready)
                        for c in range(KC):
                            last = pe.matmul(plog[64 * u:64 * u + 64, u, :], wr[:, c, :], norm.xT[:, u, c, :],
                                             start=(c == 0), stop=(c == KC - 1))
                        last.then_inc(logits_psum, 1)

                    norm.turn(pe, ready, const, 0, 0)
                    with pe.Fori(0, last_i) as i:
                        for u in range(2):
                            norm.turn(pe, ready, const, *ahead(i, u))
                            route(i, u)
                    norm.turn(pe, ready, const, last_i, 1)
                    route(last_i, 0)
                    route(last_i, 1)
                    pe.wait_ge(chain, 3 * ROUNDS + 1)
                    pe.transpose(small[:, 0:P], vals[:], const.ident[:])
                    pe.transpose(small[:, P:2 * P], idxf[:], const.ident[:]).then_inc(pe_small, 1)
                    pe.wait_ge(chain, 3 * ROUNDS + 2)
                    for a in range(2):
                        last = pe.matmul(small2[:, a * EXPERTS:(a + 1) * EXPERTS], const.flip[:],
                                         both[:, a, 64:64 + EXPERTS], start=True, stop=True)
                    last.then_inc(pe_small, 1)
                    pe.wait_ge(chain, 3 * ROUNDS + 9)
                    for a, row in enumerate((const.first, const.last)):
                        last = pe.matmul(small[:, 256 + a * EXPERTS:256 + (a + 1) * EXPERTS], row[:], best[:],
                                         start=True, stop=True)
                    last.then_inc(pe_small, 1)
                    pe.wait_ge(exp_ready, 1)
                    pe.matmul(small2[:, 256:256 + EXPERTS], const.ones[:], expo[:], start=True, stop=True
                              ).then_inc(pe_small, 1)

                @block.scalar
                def _(act):
                    act.sem_inc(norm.xT_free, 2)
                    act.sem_inc(norm.xn_free, 2)
                    act.sem_inc(norm.xT_ready, norm.banks)
                    act.sem_inc(logits_kept, 2)

                    def keep_logits(i, u):
                        wait_at(act, logits_psum, 2 * i + (u + 1), ready)
                        act.sem_inc(norm.xT_free, 1)
                        rows = slice(64 * u, 64 * u + 64)
                        act.activation(logits[rows, bass.ds(i * SEQ, SEQ)], plog[rows, u, :], ACT.Copy
                                       ).then_inc(logits_kept, 1)

                    norm.keep(act, ready, 0, 0)
                    with act.Fori(0, last_i) as i:
                        for u in range(2):
                            norm.keep(act, ready, *ahead(i, u))
                            keep_logits(i, u)
                    norm.keep(act, ready, last_i, 1)
                    keep_logits(last_i, 0)
                    keep_logits(last_i, 1)
                    act.wait_ge(chain, 3 * ROUNDS + 12)
                    act.activation(expo[:], best[:], ACT.Exp).then_inc(exp_ready, 1)
            r.clear()

        slot = s.sb("slot", [P, EU], U32)
        slot_out = s.sb("slot_out", [P, 2], U32)
        xg = s.sb("xg", [P, EU, D])
        xgT = s.sb("xgT", [P, 2, KC, P])
        hb = s.sb("hb", [P, 2, HC, P])
        h = s.sb("h", [P, 2, HC, P])
        y = s.sb("y", [P, EU, D])
        pT = s.ps("pT", [P, 2, 512])
        pH = s.ps("pH", [P, 2, HC, P])
        pY = s.ps("pY", [P, 2, 512])
        gathered = lasting.sems(name + "_gathered", EU)
        scattered = lasting.sem(name + "_scattered")
        slot_ready, gT_psum, gT_ready = s.sem("slot_ready"), s.sem("gT_psum"), s.sem("gT_ready")
        h_psum, h_ready, y_psum = s.sem("h_psum"), s.sem("h_ready"), s.sem("y_psum")
        h_biased = s.sem("h_biased")
        y_ready = s.sem("y_ready")
        y_free = s.sem("y_free")
        w_free = s.sem("w_free")

        def over_experts(eng, step):
            with eng.Fori(0, EXPERTS // EU - 1) as i:
                for u in range(EU):
                    step(i, u, EU)
            for u in range(EU):
                step(EXPERTS // EU - 1, u, EU - 1 - u)

        def later(i, u, k):
            return i + (u + k) // EU, (u + k) % EU

        def count(i, u, extra=1):
            return EU * i + (u + extra)

        with nc.Block() as block:

            @block.sync
            def _(sp):
                with sp.Fori(0, EXPERTS // EU - 1) as i:
                    for u in range(EU):
                        wait_at(sp, w_free, count(i, u), ready)
                        fetch(sp, EU * i + (EU + u), u)

            @block.gpsimd
            def _(pool):
                def gather(u):
                    pool.indirect_dma_start(xg[:, u, :], None, xn_dram, bass.IndirectOffsetOnAxis(slot[:, u:u + 1], 0)
                                            ).then_inc(gathered[u], 16)

                for u in range(EU):
                    pool.tensor_copy(slot[:, u:u + 1], index[:, u:u + 1]).then_inc(slot_ready, 1)
                    pool.wait_ge(slot_ready, u + 1)
                    gather(u)
                pool.tensor_copy(slot_out[:, 0:1], index[:, 0:1]).then_inc(slot_ready, 1)
                pool.sem_inc(y_free, EU)

                def step(i, u, more):
                    e = EU * i + u
                    wait_at(pool, slot_ready, 2 * e + (EU + 1) if more == EU else EXPERTS * 2 - EU + 1 + u, ready)
                    wait_at(pool, y_ready, count(i, u, 3), ready)
                    pool.indirect_dma_start(acc_dram, bass.IndirectOffsetOnAxis(slot_out[:, u % 2:u % 2 + 1], 0), y[:, u, :],
                                            None, compute_op=ALU.add).then_inc(scattered, 16)
                    if more:
                        pool.tensor_copy(slot_out[:, (u + 1) % 2:(u + 1) % 2 + 1], index[:, bass.ds(e + 1, 1)]
                                         ).then_inc(slot_ready, 1)
                    if more == EU:
                        wait_at(pool, gathered[u], 16 * i + 16, ready)
                        pool.tensor_copy(slot[:, u:u + 1], index[:, bass.ds(e + EU, 1)]).then_inc(slot_ready, 1)
                        wait_at(pool, slot_ready, 2 * e + (EU + 3), ready)
                        gather(u)
                    wait_at(pool, scattered, 16 * count(i, u), ready)
                    pool.sem_inc(y_free, 1)

                over_experts(pool, step)

            @block.tensor
            def _(pe):
                def turn(i, u):
                    v = u % 2
                    wait_at(pe, gathered[u], 16 * i + 16, ready)
                    for c in range(KC):
                        last = pe.transpose(pT[:, v, c * P:(c + 1) * P], xg[:, u, c * P:(c + 1) * P], const.ident[:])
                    last.then_inc(gT_psum, 1)

                def hidden(i, u):
                    v = u % 2
                    wait_at(pe, w_landed[u], 48 * i + 48, ready)
                    wait_at(pe, gT_ready, count(i, u), ready)
                    wait_at(pe, h_biased, count(i, u), ready)
                    for j in range(HC):
                        for c in range(KC):
                            last = pe.matmul(pH[:, v, j, :], w1[:, u, c, j * P:(j + 1) * P], xgT[:, v, c, :],
                                             start=(c == 0), stop=(c == KC - 1))
                    last.then_inc(h_psum, 1)

                def step(i, u, more):
                    v = u % 2
                    if more > 0:
                        hidden(*later(i, u, 1))
                    if more > 1:
                        turn(*later(i, u, 2))
                    wait_at(pe, h_ready, count(i, u), ready)
                    wait_at(pe, y_ready, count(i, u), ready)
                    pe.matmul(pY[:, v, 0:D], const.ones[0:1, :], b2[:, u, :], start=True, stop=False,
                              skip_group_check=True)
                    for j in range(HC):
                        q = j * P // HID
                        last = pe.matmul(pY[:, v, q * YK:(q + 1) * YK], h[:, v, j, :], w2[:, u, j, :],
                                         start=False, stop=(j == HC - 1), skip_group_check=True)
                    last.then_inc(y_psum, 1)

                turn(0, 0)
                hidden(0, 0)
                turn(0, 1)
                over_experts(pe, step)

            @block.scalar
            def _(act):
                def keep(i, u):
                    v = u % 2
                    wait_at(act, gT_psum, count(i, u), ready)
                    act.activation(xgT[:, v], pT[:, v, 0:D].rearrange("p (c n) -> p c n", c=KC), ACT.Copy
                                   ).then_inc(gT_ready, 1)

                def active(i, u):
                    wait_at(act, h_biased, count(i, u, 3), ready)
                    act.activation(h[:, u % 2], hb[:, u % 2], ACT.Gelu).then_inc(h_ready, 1)

                def step(i, u, more):
                    if more > 1:
                        keep(*later(i, u, 2))
                    if more > 0:
                        active(*later(i, u, 1))

                keep(0, 0)
                keep(0, 1)
                active(0, 0)
                over_experts(act, step)

            @block.vector
            def _(dve):
                def biased(i, u):
                    wait_at(dve, h_psum, count(i, u), ready)
                    bias = b1[:, bass.ds(EU * i + u, 1), :].rearrange("p e j -> p (e j)").unsqueeze(2).to_broadcast([P, HC, P])
                    dve.tensor_tensor(hb[:, u % 2], pH[:, u % 2], bias, ALU.add).then_inc(h_biased, 1)

                def step(i, u, more):
                    if more > 0:
                        biased(*later(i, u, 1))
                    wait_at(dve, y_free, count(i, u), ready)
                    wait_at(dve, y_psum, count(i, u), ready)
                    dve.sem_inc(w_free, 1)
                    dve.tensor_scalar(y[:, u, :], pY[:, u % 2, 0:D], keep_vals[:, bass.ds(EU * i + u, 1)], None, ALU.mult
                                      ).then_inc(y_ready, 1)

                dve.wait_ge(b1_landed, 16)
                dve.sem_inc(h_biased, 2)
                dve.sem_inc(y_ready, 2)
                biased(0, 0)
                over_experts(dve, step)
        s.clear()
HEADS = 16
DH = 64
DI = HEADS * DH
PAIRS = HEADS // 2
CLAMP = 50.0
RMS_EPS = 1.1920929e-07
QW = 512
CHUNKS = 3 * DI // QW
HV = QW // DH


def attention_stage(nc, const, x_all, x_dram, out_dram, wqkv_dram, wo_dram, nw_dram, gamma_dram):
    QKV_USE = 1
    TURN_USE = QKV_USE + GT * CHUNKS // 2
    MISC = TURN_USE + PAIRS
    with ExitStack() as ctx:
        s = Space(nc, ctx, "attn")
        ready = const.ready
        misc = s.ps("misc", [P, 2, 512])
        norm = Norm(s, x_all, banks=1, unroll=1, turned=misc[:].unsqueeze(1), eps2=RMS_EPS, dtype=F32R)
        xT_lo = s.sb("xT_lo", [P, KC, SEQ], F32R)
        w = s.sb("w", [P, KC, 3 * DI], F32R)
        w_lo = s.sb("w_lo", [P, KC, 3 * DI], F32R)
        wo = s.sb("wo", [P, PAIRS, D])
        nw = s.sb("nw", [P, KC])
        gamma = s.sb("gamma", [P, 2, PAIRS])
        scale = s.sb("scale", [P, PAIRS])
        qk = s.sb("qk", [P, GT, 2, HEADS, DH])
        ss = s.sb("ss", [P, GT, 2 * HEADS])
        rn = s.sb("rn", [P, GT, 2 * HEADS])
        va = s.sb("va", [P, GT, PAIRS, 3, DH])
        qT, qT_lo = s.sb("qT", [P, 2, SEQ], F32R), s.sb("qT_lo", [P, 2, SEQ], F32R)
        kT, kT_lo = s.sb("kT", [P, 2, SEQ], F32R), s.sb("kT_lo", [P, 2, SEQ], F32R)
        pr = s.sb("pr", [P, 2, GT, SEQ])
        sq = pr[:, 0].rearrange("p t (h d) -> p (t h) d", d=DH)
        w_raw = qk[:].rearrange("p t a h d -> p (t a h d)")[:, 0:KC * 3 * DI].rearrange("p (c n) -> p c n", c=KC)
        rec = s.sb("rec", [P, SEQ])

        def outputs(t, p):
            return qk[:, t, 0, 2 * p:2 * p + 2, :].rearrange("p h d -> p (h d)")

        pS = s.ps("pS", [P, 2, 2, SEQ])
        pO = s.ps("pO", [P, 2, SEQ])
        w_landed, setup, w_split = s.sem("w_landed"), s.sem("setup"), s.sem("w_split")
        misc_ready = s.sems("misc_ready", 2)
        misc_free = s.sems("misc_free", 2)
        sq_ready = s.sem("sq_ready")
        sum_ready = s.sem("sum_ready")
        ss_ready, rn_ready, qk_ready, v_ready = s.sem("ss_ready"), s.sem("rn_ready"), s.sem("qk_ready"), s.sem("v_ready")
        hi_ready = s.sem("hi_ready")
        score_ready = s.sem("score_ready")
        tanh_ready = s.sem("tanh_ready")
        exp_ready = s.sem("exp_ready")
        pv_ready = s.sem("pv_ready")
        rec_ready = s.sem("rec_ready")
        o_ready = s.sem("o_ready")
        wo_psum, stored = s.sem("wo_psum"), s.sem("stored")
        wo_read = s.sem("wo_read")

        qk_chunks = [(t, j) for t in range(GT) for j in range(4)]
        v_chunks = [(t, j) for t in range(GT) for j in range(4, CHUNKS)]

        def chunk_use(t, j):
            return j % 2, QKV_USE + (qk_chunks + v_chunks).index((t, j)) // 2

        def wait_ready(eng, n, bank, use):
            wait_at(eng, misc_ready[bank], MISC * n + (use + 1), ready)

        with nc.Block() as block:

            @block.sync
            def _(sp):
                sp.dma_start(w_raw, wqkv_dram).then_inc(w_landed, 16)
                sp.dma_start(wo[:], wo_dram).then_inc(w_landed, 16)
                sp.dma_start(nw[:], nw_dram).then_inc(w_landed, 16)
                sp.dma_start(gamma[:], gamma_dram).then_inc(w_landed, 16)
                with sp.Fori(0, GROUPS) as i:
                    norm.load(sp, ready, x_dram, i, 0, i)
                    wait_at(sp, norm.x_landed[0], 16 * i + 16, ready)
                with sp.Fori(0, GROUPS) as n:
                    wait_at(sp, wo_read, n * GT + (GT + 1), ready)
                    sp.dma_start(out_dram[bass.ds(n * SEQ, SEQ), :].rearrange("(t p) d -> p t d", p=P),
                                 x_all[:, bass.ds(n, 1)].rearrange("p g t d -> p (g t) d")).then_inc(stored, 16)
                    wait_at(sp, stored, 16 * n + 16, ready)

            @block.vector
            def _(dve):
                def project(n):
                    for t in range(GT):
                        wait_at(dve, sq_ready, GT * n + (t + 1), ready)
                        dve.tensor_reduce(ss[:, t, :], sq, AX.X, ALU.add).then_inc(sum_ready, 1)
                        wait_at(dve, sum_ready, GT * n + (t + 2), ready)
                        dve.tensor_scalar(ss[:, t, :], ss[:, t, :], 1e-24, None, ALU.max).then_inc(ss_ready, 1)
                        if t:
                            unit(n, t - 1)
                    unit(n, GT - 1)

                def unit(n, t):
                    wait_at(dve, rn_ready, GT * n + (t + 1), ready)
                    rows = qk[:, t].rearrange("p a h d -> p (a h) d")
                    dve.tensor_tensor(rows, rows, rn[:, t, :].unsqueeze(2).to_broadcast([P, 2 * HEADS, DH]), ALU.mult
                                      ).then_inc(qk_ready, 1)

                def turn_pair(n, p):
                    v = p % 2
                    wait_ready(dve, n, 0, TURN_USE + p)
                    dve.tensor_scalar(qT[:, v, :], misc[:, 0, :], scale[:, p:p + 1], None, ALU.mult).then_inc(hi_ready, 1)
                    wait_ready(dve, n, 1, TURN_USE + p)
                    dve.tensor_copy(kT[:, v, :], misc[:, 1, :]).then_inc(hi_ready, 1)
                    wait_at(dve, hi_ready, 2 * PAIRS * n + (2 * p + 1), ready)
                    dve.scalar_tensor_tensor(out=qT_lo[:, v, :], in0=misc[:, 0, :], scalar=scale[:, p:p + 1],
                                             in1=qT[:, v, :].bitcast(F32), op0=ALU.mult, op1=ALU.subtract
                                             ).then_inc(misc_free[0], 1)
                    wait_at(dve, hi_ready, 2 * PAIRS * n + (2 * p + 2), ready)
                    dve.tensor_tensor(kT_lo[:, v, :], misc[:, 1, :], kT[:, v, :].bitcast(F32), ALU.subtract
                                      ).then_inc(misc_free[1], 1)

                def head(n, h):
                    v = h % 2
                    own, other = slice(DH * v, DH * v + DH), slice(DH * (1 - v), DH * (1 - v) + DH)
                    wait_at(dve, pv_ready, HEADS * n + (h + 3), ready)
                    dve.reciprocal(rec[own, :], pO[other, v, :]).then_inc(rec_ready, 1)
                    wait_at(dve, rec_ready, HEADS * n + (h + 1), ready)
                    dve.tensor_tensor(qk[own, :, 0, h - v:h - v + 2, :].rearrange("p t h d -> p t (h d)"),
                                      pO[own, v, :].rearrange("p (t n) -> p t n", t=GT),
                                      rec[own, :].rearrange("p (t n) -> p t n", t=GT), ALU.mult).then_inc(o_ready, 1)

                def lower(n):
                    norm.kept(dve, ready, n, 0)
                    for c in range(KC):
                        dve.tensor_tensor(xT_lo[:, c, :], misc[:, c, :], norm.xT[:, 0, c, :].bitcast(F32), ALU.subtract
                                          ).then_inc(misc_free[c], 1)

                def batch(n, more):
                    project(n)
                    turn_pair(n, 0)
                    if more:
                        norm.moments_of(dve, ready, n + 1, 0, n + 1)
                    for h in range(HEADS):
                        if h % 2 == 0 and h // 2 + 1 < PAIRS:
                            turn_pair(n, h // 2 + 1)
                        if h:
                            head(n, h - 1)
                        if h == 2 and more:
                            norm.normalise(dve, ready, n + 1, 0, n + 1)
                    head(n, HEADS - 1)
                    if more:
                        lower(n + 1)
                    for t in range(GT):
                        wait_at(dve, wo_psum, GT * n + (t + 1), ready)
                        x = x_all[:, bass.ds(n, 1), t, :].rearrange("p g d -> p (g d)")
                        dve.tensor_tensor(x, x, pS[:, t // 2, t % 2, 0:D], ALU.add).then_inc(wo_read, 1)

                dve.sem_inc(misc_free[0], 1)
                dve.sem_inc(misc_free[1], 1)
                dve.sem_inc(sum_ready, 1)
                dve.sem_inc(o_ready, 2)
                dve.sem_inc(wo_read, 1)
                dve.wait_ge(w_landed, 64)
                for c in range(KC):
                    dve.tensor_scalar(w[:, c, :], w_raw[:, c, :], nw[:, c:c + 1], None, ALU.mult).then_inc(w_split, 1)
                for c in range(KC):
                    dve.wait_ge(w_split, c + 1)
                    dve.scalar_tensor_tensor(out=w_lo[:, c, :], in0=w_raw[:, c, :], scalar=nw[:, c:c + 1],
                                             in1=w[:, c, :].bitcast(F32), op0=ALU.mult, op1=ALU.subtract).then_inc(setup, 1)
                dve.memset(va[:, :, :, 1, :], 1.0).then_inc(setup, 1)
                dve.tensor_scalar(gamma[:], gamma[:], 1.0, None, ALU.add).then_inc(setup, 1)
                dve.wait_ge(setup, 4)
                dve.scalar_tensor_tensor(out=scale[:], in0=gamma[:, 0, :], scalar=DH / CLAMP, in1=gamma[:, 1, :],
                                         op0=ALU.mult, op1=ALU.mult).then_inc(setup, 1)
                dve.wait_ge(setup, 5)
                norm.moments_of(dve, ready, 0, 0, 0)
                norm.normalise(dve, ready, 0, 0, 0)
                lower(0)
                with dve.Fori(0, GROUPS - 1) as n:
                    batch(n, True)
                batch(GROUPS - 1, False)

            @block.gpsimd
            def _(pool):
                def batch(n, more):
                    for t in range(GT):
                        wait_at(pool, ss_ready, GT * n + (t + 1), ready)
                        pool.tensor_tensor(rn[:, t, :], ss[:, t, :], const.minus_half[:, 0:2 * HEADS], ALU.pow
                                           ).then_inc(rn_ready, 1)
                    if more:
                        norm.root(pool, ready, const, n + 1, 0)

                pool.memset(norm.eps2_tile[:], RMS_EPS).then_inc(norm.eps2_set, 1)
                pool.wait_ge(norm.eps2_set, 1)
                norm.root(pool, ready, const, 0, 0)
                with pool.Fori(0, GROUPS - 1) as n:
                    batch(n, True)
                batch(GROUPS - 1, False)

            @block.scalar
            def _(act):
                def batch(n, more):
                    for t, j in qk_chunks:
                        bank, use = chunk_use(t, j)
                        wait_ready(act, n, bank, use)
                        heads = slice((j % 2) * HV, (j % 2 + 1) * HV)
                        act.activation(qk[:, t, j // 2, heads, :], misc[:, bank, :].rearrange("p (h d) -> p h d", h=HV),
                                       ACT.Copy).then_inc(misc_free[bank], 1)
                        if j < 3:
                            continue
                        for bank in range(2):
                            wait_at(act, misc_free[bank], MISC * n + (chunk_use(t, 2)[1] + 2), ready)
                        wait_at(act, sum_ready, GT * n + (t + 1), ready)
                        act.activation(sq, qk[:, t].rearrange("p a h d -> p (a h) d"), ACT.Square
                                       ).then_inc(sq_ready, 1)
                    for t, j in v_chunks:
                        bank, use = chunk_use(t, j)
                        wait_ready(act, n, bank, use)
                        pairs = slice((j - 4) * HV // 2, (j - 3) * HV // 2)
                        act.activation(va[:, t, pairs, 0:3:2, :], misc[:, bank, :].rearrange("p (q a d) -> p q a d", a=2, d=DH),
                                       ACT.Copy).then_inc(misc_free[bank], 1)
                    act.drain().then_inc(v_ready, 1)
                    act.sem_inc(norm.xT_free, 1)
                    for h in range(HEADS):
                        v = h % 2
                        wait_at(act, pv_ready, HEADS * n + (h + 1), ready)
                        for a in range(2):
                            wait_at(act, score_ready, 2 * HEADS * n + (2 * h + a + 1), ready)
                            act.activation(pr[:, v, 2 * a:2 * a + 2, :], pS[:, a], ACT.Tanh).then_inc(tanh_ready, 1)
                        wait_at(act, tanh_ready, 2 * HEADS * n + (2 * h + 4), ready)
                        act.activation(pr[:, v], pr[:, v], ACT.Exp, scale=CLAMP * DH ** -0.5).then_inc(exp_ready, 1)
                    if more:
                        norm.keep(act, ready, n + 1, 0)

                act.sem_inc(norm.xT_free, 1)
                act.sem_inc(norm.xn_free, 1)
                act.sem_inc(norm.xT_ready, norm.banks)
                act.sem_inc(tanh_ready, 2)
                norm.keep(act, ready, 0, 0)
                with act.Fori(0, GROUPS - 1) as n:
                    batch(n, True)
                batch(GROUPS - 1, False)

            @block.tensor
            def _(pe):
                def wait_free(n, bank, use):
                    wait_at(pe, misc_free[bank], MISC * n + (use + 1), ready)

                def turn_pair(n, p):
                    for a in range(2):
                        wait_free(n, a, TURN_USE + p)
                        for t in range(GT):
                            last = pe.transpose(misc[:, a, t * P:(t + 1) * P],
                                                qk[:, t, a, 2 * p:2 * p + 2, :].rearrange("p h d -> p (h d)"),
                                                const.ident[:])
                        last.then_inc(misc_ready[a], 1)

                def scores(n, h):
                    if h % 2 == 0:
                        for a in range(2):
                            wait_at(pe, misc_free[a], MISC * n + (TURN_USE + h // 2 + 2), ready)
                    rows = slice(DH * (h % 2), DH * (h % 2) + DH)
                    for a in range(2):
                        wait_at(pe, tanh_ready, 2 * HEADS * n + (2 * h + a + 1), ready)
                        for b in range(2):
                            j = 2 * a + b
                            for k, (keys, queries) in enumerate(((kT, qT), (kT, qT_lo), (kT_lo, qT))):
                                last = pe.matmul(pS[:, a, b, :], keys[rows, (h // 2) % 2, j * P:(j + 1) * P],
                                                 queries[rows, (h // 2) % 2, :], start=(k == 0), stop=(k == 2))
                        last.then_inc(score_ready, 1)

                def values(n, h):
                    wait_at(pe, exp_ready, HEADS * n + (h + 1), ready)
                    wait_at(pe, o_ready, HEADS * n + (h + 1), ready)
                    v = h % 2
                    for j in range(GT):
                        last = pe.matmul(pO[:, v, :], va[:, j, h // 2, v:v + 2, :].rearrange("p a d -> p (a d)"),
                                         pr[:, v, j, :], start=(j == 0), stop=(j == GT - 1))
                    last.then_inc(pv_ready, 1)

                def turn_tokens(n):
                    wait_free(n, 0, 0)
                    wait_free(n, 1, 0)
                    norm.turn(pe, ready, const, n, 0)

                def batch(n, more):
                    norm.kept(pe, ready, n, 0)
                    pe.sem_inc(misc_ready[0], 1)
                    pe.sem_inc(misc_ready[1], 1)
                    wait_free(n, 0, QKV_USE)
                    wait_free(n, 1, QKV_USE)
                    for t, j in qk_chunks + v_chunks:
                        bank, use = chunk_use(t, j)
                        wait_free(n, bank, use)
                        tokens, columns = slice(t * P, (t + 1) * P), slice(j * QW, (j + 1) * QW)
                        for c in range(KC):
                            for k, (x, by) in enumerate(((norm.xT[:, 0], w), (norm.xT[:, 0], w_lo), (xT_lo, w))):
                                last = pe.matmul(misc[:, bank, :], x[:, c, tokens], by[:, c, columns],
                                                 start=(c == 0 and k == 0), stop=(c == KC - 1 and k == 2))
                        last.then_inc(misc_ready[bank], 1)
                    wait_at(pe, qk_ready, GT * n + GT, ready)
                    wait_at(pe, v_ready, n + 1, ready)
                    turn_pair(n, 0)
                    wait_at(pe, wo_read, GT * n + 1, ready)
                    for h in range(HEADS):
                        scores(n, h)
                        if h:
                            values(n, h - 1)
                        if h % 2 == 0 and h // 2 + 1 < PAIRS:
                            turn_pair(n, h // 2 + 1)
                    values(n, HEADS - 1)
                    if more:
                        turn_tokens(n + 1)
                    out = [pS[:, t // 2, t % 2, 0:D] for t in range(GT)]
                    for t in range(GT):
                        for p in range(PAIRS - 1):
                            pe.matmul(out[t], outputs(t, p), wo[:, p, :], start=(p == 0), stop=False)
                    wait_at(pe, o_ready, HEADS * n + (HEADS + 2), ready)
                    for t in range(GT):
                        pe.matmul(out[t], outputs(t, PAIRS - 1), wo[:, PAIRS - 1, :], start=False, stop=True
                                  ).then_inc(wo_psum, 1)

                pe.sem_inc(pv_ready, 2)
                pe.wait_ge(setup, 5)
                turn_tokens(0)
                with pe.Fori(0, GROUPS - 1) as n:
                    batch(n, True)
                batch(GROUPS - 1, False)
        s.clear()


def rwkv_stage(nc, const, name, load, x_all, x_dram, out_dram, wr_dram, wk_dram, wv_dram, mu_dram):
    with ExitStack() as ctx:
        s = Space(nc, ctx, name)
        ready = const.ready
        norm = Norm(s, x_all, banks=1, lead=1)
        wr, wk, wv = s.sb("wr", [P, KC, D]), s.sb("wk", [P, KC, D]), s.sb("wv", [P, KC, D])
        mu = s.sb("mu", [P, 2, KC])
        step_back = s.sb("step_back", [P, KC, SEQ])
        mixed = s.sb("mixed", [P, 2, 2, KC, SEQ])
        relu = s.sb("relu", [P, KC, SEQ])
        act2 = s.sb("act2", [P, KC, SEQ])
        gate = s.sb("gate", [P, GT, D])
        prod = s.sb("prod", [P, GT, D])
        pk = s.ps("pk", [P, KC, SEQ])
        pr = s.ps("pr", [P, GT, D])
        pv = s.ps("pv", [P, GT, D])
        w_landed = s.sem("w_landed")
        lead_clear = s.sem("lead_clear")
        step_ready, mixed_ready = s.sem("step_ready"), s.sem("mixed_ready")
        pk_ready, relu_ready, act2_ready = s.sem("pk_ready"), s.sem("relu_ready"), s.sem("act2_ready")
        pr_ready, gate_ready, pv_ready = s.sem("pr_ready"), s.sem("gate_ready"), s.sem("pv_ready")
        prod_ready = s.sem("prod_ready")
        out_ready = s.sem("out_ready")
        stored = s.sems("stored", 2)
        last_i = GROUPS // 2 - 1

        with nc.Block() as block:

            @block.sync
            def _(sp):
                sp.dma_start(wr[:], wr_dram).then_inc(w_landed, 16)
                sp.dma_start(wk[:], wk_dram).then_inc(w_landed, 16)
                sp.dma_start(wv[:], wv_dram).then_inc(w_landed, 16)
                sp.dma_start(mu[:], mu_dram).then_inc(w_landed, 16)
                if load:
                    with sp.Fori(0, GROUPS // 2) as i:
                        for u in range(2):
                            norm.load(sp, ready, x_dram, i, u, 2 * i + u)
                        for u in range(2):
                            wait_at(sp, norm.x_landed[u], 16 * i + 16, ready)
                if out_dram is not None:
                    with sp.Fori(0, GROUPS // 2) as i:
                        for u in range(2):
                            wait_at(sp, out_ready, 2 * i + (u + 1), ready)
                            sp.dma_start(out_dram[bass.ds((2 * i + u) * SEQ, SEQ), :].rearrange("(t p) d -> p t d", p=P),
                                         x_all[:, bass.ds(2 * i + u, 1)].rearrange("p g t d -> p (g t) d")
                                         ).then_inc(stored[u], 16)
                        for u in range(2):
                            wait_at(sp, stored[u], 16 * i + 16, ready)

            @block.vector
            def _(dve):
                def moments(i, u):
                    norm.moments_of(dve, ready, i, u, 2 * i + u, load)

                def normalise(i, u):
                    norm.normalise(dve, ready, i, u, 2 * i + u)

                def mix(i, u):
                    n1 = 2 * i + (u + 1)
                    norm.kept(dve, ready, i, u)
                    now, before = norm.xT[:, u, :, 1:], norm.xT[:, u, :, 0:SEQ]
                    dve.tensor_tensor(step_back[:], now, before, ALU.subtract).then_inc(step_ready, 1)
                    wait_at(dve, step_ready, n1, ready)
                    for r in range(2):
                        for c in range(KC):
                            last = dve.scalar_tensor_tensor(out=mixed[:, u, r, c, :], in0=step_back[:, c, :],
                                                            scalar=mu[:, r, c:c + 1], in1=before[:, c, :],
                                                            op0=ALU.mult, op1=ALU.add)
                    last.then_inc(mixed_ready, 1)

                def main(i, u, next_mix=None, next_norm=None):
                    n1 = 2 * i + (u + 1)
                    wait_at(dve, relu_ready, n1, ready)
                    dve.tensor_tensor(act2[:], pk[:], relu[:], ALU.mult).then_inc(act2_ready, 1)
                    if next_mix:
                        mix(*next_mix)
                    if next_norm:
                        moments(*next_norm)
                    wait_at(dve, gate_ready, n1, ready)
                    wait_at(dve, pv_ready, n1, ready)
                    dve.tensor_tensor(prod[:], pv[:], gate[:], ALU.mult).then_inc(prod_ready, 1)
                    wait_at(dve, prod_ready, n1 + 1, ready)
                    x = x_all[:, bass.ds(2 * i + u, 1)].rearrange("p g t d -> p (g t d)")
                    dve.scalar_tensor_tensor(out=x, in0=prod[:].rearrange("p t d -> p (t d)"), scalar=0.5, in1=x,
                                             op0=ALU.mult, op1=ALU.add).then_inc(out_ready, 1)
                    if next_norm:
                        normalise(*next_norm)

                dve.memset(norm.xT[:, :, :, 0:1], 0.0).then_inc(lead_clear, 1)
                dve.sem_inc(prod_ready, 1)
                dve.wait_ge(w_landed, 64)
                dve.wait_ge(lead_clear, 1)
                moments(0, 0)
                normalise(0, 0)
                moments(0, 1)
                mix(0, 0)
                normalise(0, 1)
                with dve.Fori(0, last_i) as i:
                    for u in range(2):
                        main(i, u, ahead(i, u), ahead(i, u, 2))
                main(last_i, 0, (last_i, 1))
                main(last_i, 1)

            @block.gpsimd
            def _(pool):
                with pool.Fori(0, GROUPS // 2) as i:
                    for u in range(2):
                        norm.root(pool, ready, const, i, u)

            @block.scalar
            def _(act):
                def main(i, u, coming=None):
                    n1 = 2 * i + (u + 1)
                    wait_at(act, mixed_ready, n1, ready)
                    act.sem_inc(norm.xT_free, 1)
                    wait_at(act, pk_ready, n1, ready)
                    act.activation(relu[:], pk[:], ACT.Relu).then_inc(relu_ready, 1)
                    if coming:
                        norm.keep(act, ready, *coming)
                    wait_at(act, pr_ready, n1, ready)
                    act.activation(gate[:], pr[:], ACT.Sigmoid).then_inc(gate_ready, 1)

                act.sem_inc(norm.xT_free, 2)
                act.sem_inc(norm.xn_free, 2)
                act.sem_inc(norm.xT_ready, norm.banks)
                act.wait_ge(lead_clear, 1)
                norm.keep(act, ready, 0, 0)
                with act.Fori(0, last_i) as i:
                    for u in range(2):
                        main(i, u, ahead(i, u))
                main(last_i, 0, (last_i, 1))
                main(last_i, 1)

            @block.tensor
            def _(pe):
                def main(i, u, coming=None):
                    n1 = 2 * i + (u + 1)
                    wait_at(pe, mixed_ready, n1, ready)
                    for m in range(KC):
                        for c in range(KC):
                            last = pe.matmul(pk[:, m, :], wk[:, c, m * P:(m + 1) * P], mixed[:, u, 1, c, :],
                                             start=(c == 0), stop=(c == KC - 1))
                    last.then_inc(pk_ready, 1)
                    if coming:
                        norm.turn(pe, ready, const, *coming)
                    wait_at(pe, prod_ready, n1, ready)
                    for t in range(GT):
                        for c in range(KC):
                            last = pe.matmul(pr[:, t, :], mixed[:, u, 0, c, t * P:(t + 1) * P], wr[:, c, :],
                                             start=(c == 0), stop=(c == KC - 1))
                    last.then_inc(pr_ready, 1)
                    wait_at(pe, act2_ready, n1, ready)
                    for t in range(GT):
                        for c in range(KC):
                            last = pe.matmul(pv[:, t, :], act2[:, c, t * P:(t + 1) * P], wv[:, c, :],
                                             start=(c == 0), stop=(c == KC - 1))
                    last.then_inc(pv_ready, 1)

                pe.wait_ge(w_landed, 64)
                norm.turn(pe, ready, const, 0, 0)
                with pe.Fori(0, last_i) as i:
                    for u in range(2):
                        main(i, u, ahead(i, u))
                main(last_i, 0, (last_i, 1))
                main(last_i, 1)
        s.clear()


MH = 16
HP = 32
MI = MH * HP
NS = 64
TILES = TOKENS // P
CH = SEQ // P
PC = 2 * NS + 2 * MH
TH = NS // 2
RMS2_EPS = 1e-6
TWO_PI = 6.283185307179586
PI = 3.1415925
HALF_PI = TWO_PI / 4
ROUND = 12582912.0


def mamba_stage(nc, const, x_all, gz_dram, w_dram, theta_dram, wout_dram, norm_dram, rows_dram):
    with ExitStack() as ctx:
        s = Space(nc, ctx, "mamba")
        ready = const.ready
        xs = s.sb("xs", [P, TILES, MI])
        bc = s.sb("bc", [P, TILES, 2 * NS])
        cumT = s.sb("cumT", [3 * MH, TILES, P], BF16)
        weight = s.sb("weight", [P, TILES, MH])
        to_end = s.sb("to_end", [P, TILES, MH])
        grown = s.sb("grown", [P, TILES, MH])
        across = s.sb("across", [P, TILES, MH])
        skip = s.sb("skip", [P, TILES, MH])
        mean1 = s.sb("mean1", [P, TILES])
        root1 = s.sb("root1", [P, TILES])
        rows = s.sb("rows", [P, 4 * NS + 3 * MH])
        rows_landed = s.sem("rows_landed")

        rctx = ctx.enter_context(ExitStack())
        raw = Space(nc, rctx, "mamba_raw").sb("raw", [P, TILES, PC + TH])
        unscale = Space(nc, rctx, "mamba_un").sb("unscale", [P, TILES])
        with ExitStack() as pctx:
            r = Space(nc, pctx, "mamba_proj")
            norm = Norm(r, x_all, banks=1, eps2=RMS2_EPS)
            w = r.sb("w", [P, KC, 2 * MI + PC])
            theta_w = r.sb("theta_w", [P, KC, TH])
            nrm = r.sb("nrm", [P, 2, KC])
            xi = r.sb("xi", [P, 2, KC, SEQ])
            sg = r.sb("sg", [P, 2, MI])
            gz = r.sb("gz", [P, 2, MI])
            pxz = r.ps("pxz", [P, 2, 2, MI])
            pbc = r.ps("pbc", [P, 2, 512])
            w_landed = r.sem("w_landed")
            xi_ready = r.sem("xi_ready")
            xz_psum, bc_psum = r.sem("xz_psum"), r.sem("bc_psum")
            sg_ready = r.sem("sg_ready")
            silu_ready = r.sem("silu_ready")
            raw_ready = r.sem("raw_ready")
            gz_stored = r.sems("gz_stored", 2)
            unscale_ready = r.sem("unscale_ready")
            gz_out = gz_dram.rearrange("(g p) d -> g p d", p=P)
            last_i = GROUPS // 2 - 1

            with nc.Block() as block:

                @block.sync
                def _(sp):
                    sp.dma_start(w[:], w_dram).then_inc(w_landed, 16)
                    sp.dma_start(theta_w[:], theta_dram).then_inc(w_landed, 16)
                    sp.dma_start(nrm[:], norm_dram).then_inc(w_landed, 16)
                    sp.dma_start(rows[:], rows_dram.rearrange("(o n) -> o n", o=1).to_broadcast([P, 4 * NS + 3 * MH])
                                 ).then_inc(rows_landed, 16)
                    with sp.Fori(0, TILES // 2) as i:
                        for v in range(2):
                            wait_at(sp, silu_ready, 4 * i + (2 * v + 6), ready)
                            sp.dma_start(gz_out[bass.ds(2 * i + v, 1)].rearrange("g p d -> p (g d)"), gz[:, v]
                                         ).then_inc(gz_stored[v], 16)
                    for v in range(2):
                        sp.wait_ge(gz_stored[v], 16 * TILES // 2)

                @block.vector
                def _(dve):
                    def moments(i, u):
                        norm.moments_of(dve, ready, i, u, 2 * i + u, False)

                    def normalise(i, u):
                        norm.normalise(dve, ready, i, u, 2 * i + u)
                        tiles = bass.ds(GT * (2 * i + u), GT)
                        dve.tensor_copy(mean1[:, tiles], norm.moments[:, u, :, 0])
                        dve.tensor_copy(root1[:, tiles], norm.work[:, u, 0, :])

                    def main(i, u, before, coming=None):
                        n = 2 * i + u
                        if coming:
                            moments(*coming)
                        for t in range(GT):
                            tile = GT * n + t
                            if coming and t == 1:
                                normalise(*coming)
                            v = t % 2
                            if before or t >= 2:
                                wait_at(dve, gz_stored[v], 32 * n + 16 * (t // 2), ready)
                            for a in range(2):
                                wait_at(dve, sg_ready, 2 * tile + (a + 1), ready)
                                out = gz[:, v, :] if a else xs[:, bass.ds(tile, 1), :].rearrange("p o d -> p (o d)")
                                dve.tensor_tensor(out, pxz[:, v, a, :], sg[:, a, :], ALU.mult
                                                  ).then_inc(silu_ready, 1)

                    dve.sem_inc(silu_ready, 4)
                    moments(0, 0)
                    normalise(0, 0)
                    main(0, 0, False, (0, 1))
                    main(0, 1, True, (1, 0))
                    with dve.Fori(1, last_i) as i:
                        for u in range(2):
                            main(i, u, True, ahead(i, u))
                    main(last_i, 0, True, (last_i, 1))
                    main(last_i, 1, True)

                @block.gpsimd
                def _(pool):
                    pool.memset(norm.eps2_tile[:], RMS2_EPS).then_inc(norm.eps2_set, 1)
                    pool.wait_ge(norm.eps2_set, 1)
                    with pool.Fori(0, GROUPS // 2) as i:
                        for u in range(2):
                            norm.root(pool, ready, const, i, u)
                            pool.tensor_tensor(unscale[:, bass.ds(GT * (2 * i + u), GT)], norm.work[:, u, 1, :],
                                               norm.work[:, u, 2, :], ALU.mult).then_inc(unscale_ready, 1)

                @block.scalar
                def _(act):
                    def first(i, u):
                        norm.keep(act, ready, i, u, count=False)
                        for c in range(KC):
                            last = act.activation(xi[:, u, c, :], norm.turned[:, 0, c, :], ACT.Identity,
                                                  scale=nrm[:, 0, c:c + 1], bias=nrm[:, 1, c:c + 1])
                        last.then_inc(norm.xT_ready, 1)

                    def main(i, u, coming=None):
                        n = 2 * i + u
                        for t in range(GT):
                            tile = GT * n + t
                            v = t % 2
                            if coming and t == 2:
                                first(*coming)
                            for a in range(2):
                                wait_at(act, xz_psum, 2 * tile + (a + 1), ready)
                                wait_at(act, silu_ready, 2 * tile + (a + 3), ready)
                                act.activation(sg[:, a, :], pxz[:, v, a, :], ACT.Sigmoid).then_inc(sg_ready, 1)
                            wait_at(act, bc_psum, tile + 1, ready)
                            act.activation(raw[:, bass.ds(tile, 1), :].rearrange("p o d -> p (o d)"),
                                           pbc[:, v, 0:PC + TH], ACT.Copy).then_inc(raw_ready, 1)
                        act.sem_inc(norm.xT_free, 1)

                    act.sem_inc(norm.xT_free, 2)
                    act.sem_inc(norm.xn_free, 2)
                    act.sem_inc(norm.xT_ready, 1)
                    act.sem_inc(raw_ready, 2)
                    act.wait_ge(w_landed, 48)
                    first(0, 0)
                    with act.Fori(0, last_i) as i:
                        for u in range(2):
                            main(i, u, ahead(i, u))
                    main(last_i, 0, (last_i, 1))
                    main(last_i, 1)

                @block.tensor
                def _(pe):
                    def main(i, u, coming=None):
                        n = 2 * i + u
                        norm.kept(pe, ready, i, u)
                        for t in range(GT):
                            if coming and t == 2:
                                norm.turn(pe, ready, const, *coming)
                            tile = GT * n + t
                            v = t % 2
                            tokens = slice(t * P, (t + 1) * P)
                            for a in range(2):
                                wait_at(pe, silu_ready, 2 * tile + (a + 1), ready)
                                for c in range(KC):
                                    last = pe.matmul(pxz[:, v, a, :], xi[:, u, c, tokens], w[:, c, a * MI:(a + 1) * MI],
                                                     start=(c == 0), stop=(c == KC - 1))
                                last.then_inc(xz_psum, 1)
                            wait_at(pe, raw_ready, tile + 1, ready)
                            for c in range(KC):
                                pe.matmul(pbc[:, v, 0:PC], xi[:, u, c, tokens], w[:, c, 2 * MI:],
                                          start=(c == 0), stop=(c == KC - 1))
                            for c in range(KC):
                                last = pe.matmul(pbc[:, v, PC:PC + TH], norm.xT[:, u, c, tokens], theta_w[:, c, :],
                                                 start=(c == 0), stop=(c == KC - 1))
                            last.then_inc(bc_psum, 1)

                    pe.wait_ge(w_landed, 48)
                    norm.turn(pe, ready, const, 0, 0)
                    with pe.Fori(0, last_i) as i:
                        for u in range(2):
                            main(i, u, ahead(i, u))
                    main(last_i, 0, (last_i, 1))
                    main(last_i, 1)
            r.clear()

        with ExitStack() as ectx:
            r = Space(nc, ectx, "mamba_each")
            tri = const.tri
            vs = r.sb("vs", [P, 2, TILES * TH])
            v = vs[:, 0].rearrange("p (t d) -> p t d", d=TH)
            vp = vs[:, 1].rearrange("p (b t d) -> p b t d", t=CH, d=TH)
            cum = r.sb("cum", [P, TILES, MH])
            la = to_end
            e, q, lam, ends = grown, skip, across, across
            cparts = r.sb("cparts", [P, TILES, 3, MH], BF16)
            f = r.sb("f", [P, TILES, MH])
            dt = r.sb("dt", [P, TILES, MH])
            w2 = r.sb("w2", [P, TILES, MH])
            neg_a = r.sb("neg_a", [P, MH])
            tmean = r.sb("tmean", [P, TILES])
            phi = r.sb("phi", [P, TILES, 2, TH])
            turns = r.sb("turns", [P, TILES, 2, TH])
            ms = r.sb("ms", [P, TILES, 2])
            rms = r.sb("rms", [P, TILES, 2])
            big = vs[:].rearrange("p a (t x d) -> p (a t) x d", x=2, d=TH)
            big2 = turns
            gd = r.sb("gd", [P, TILES])
            pphi = r.ps("pphi", [P, 2, 512])
            pcum = r.ps("pcum", [P, 512])
            pend = r.ps("pend", [P, 512])
            pshift = r.ps("pshift", [P, 512])
            pparts = r.ps("pparts", [P, 2, TILES // 4, P], BF16)
            parts_ready, parts_psum = r.sem("parts_ready"), r.sem("parts_psum")
            parts_kept = r.sem("parts_kept")
            chain = r.sem("chain")
            a_ready, neg_ready, lam_ready, sin_ready = r.sem("a_ready"), r.sem("neg_ready"), r.sem("lam_ready"), r.sem("sin_ready")
            v_ready, sums_ready, gr_ready = r.sem("v_ready"), r.sem("sums_ready"), r.sem("gr_ready")
            abs_ready, angle_ready, cum_ready = r.sem("abs_ready"), r.sem("angle_ready"), r.sem("cum_ready")
            ms_ready, rms_ready = r.sem("ms_ready"), r.sem("rms_ready")
            dt_bias, a_log, d_row = (rows[:, 4 * NS + k * MH:4 * NS + (k + 1) * MH] for k in range(3))

            def over_tiles(row, n):
                return row.unsqueeze(1).to_broadcast([P, TILES, n])

            with nc.Block() as block:

                @block.scalar
                def _(act):
                    act.wait_ge(rows_landed, 16)
                    act.activation(neg_a[:], a_log, ACT.Exp).then_inc(a_ready, 1)
                    act.wait_ge(abs_ready, 1)
                    act.activation(e[:], e[:], ACT.Exp, scale=-1.0).then_inc(neg_ready, 1)
                    act.activation(lam[:], raw[:, :, 2 * NS + MH:PC], ACT.Sigmoid).then_inc(lam_ready, 1)
                    act.wait_ge(angle_ready, 1)
                    act.activation(phi[:], phi[:], ACT.Sin).then_inc(sin_ready, 1)
                    act.wait_ge(cum_ready, 1)
                    act.activation(grown[:], cum[:], ACT.Exp).then_inc(gr_ready, 1)
                    act.activation(to_end[:], to_end[:], ACT.Exp).then_inc(gr_ready, 1)
                    act.activation(across[:], ends[:], ACT.Exp).then_inc(gr_ready, 1)
                    act.sem_inc(parts_kept, 2)
                    for k in range(4):
                        act.wait_ge(parts_psum, k + 1)
                        act.activation(cumT[:, k * TILES // 4:(k + 1) * TILES // 4, :], pparts[0:3 * MH, k % 2],
                                       ACT.Copy).then_inc(parts_kept, 1)

                @block.gpsimd
                def _(pool):
                    pool.wait_ge(ms_ready, 1)
                    pool.tensor_tensor(rms[:], ms[:], const.minus_half[:].rearrange("p (a b) -> p a b", b=2), ALU.pow
                                       ).then_inc(rms_ready, 1)

                @block.tensor
                def _(pe):
                    pe.wait_ge(v_ready, 1)
                    flat_v, flat_vp = vs[:, 0], vs[:, 1]
                    flat_la, flat_w2 = la[:].rearrange("p t d -> p (t d)"), w2[:].rearrange("p t d -> p (t d)")
                    for k in range(2):
                        part = slice(512 * k, 512 * k + 512)
                        pe.matmul(pphi[:, k, :], const.tri[:], flat_v[:, part], start=True, stop=False)
                        pe.matmul(pphi[:, k, :], const.ones[:], flat_vp[:, part], start=False, stop=True)
                    pe.matmul(pcum[:], const.tri[:], flat_la, start=True, stop=True)
                    pe.matmul(pend[:], const.ones[:], flat_la, start=True, stop=True)
                    pe.matmul(pshift[:], const.shift[:], flat_w2, start=True, stop=False)
                    w2_next = w2[:].rearrange("p (b t) h -> p b t h", t=CH)[:, :, 1:CH, :]
                    shift_out = pshift[:].rearrange("p (b t h) -> p b t h", t=CH, h=MH)[:, :, 0:CH - 1, :]
                    pe.matmul(shift_out, const.wrap[:], w2_next, start=False, stop=True).then_inc(sums_ready, 1)
                    pe.wait_ge(parts_ready, 1)
                    for k in range(4):
                        pe.wait_ge(parts_kept, k + 1)
                        for t in range(TILES // 4):
                            last = pe.transpose(pparts[0:3 * MH, k % 2, t, :],
                                                cparts[:, k * TILES // 4 + t].rearrange("p a h -> p (a h)"),
                                                const.ident_b[:])
                        last.then_inc(parts_psum, 1)

                @block.vector
                def _(dve):
                    steps = 0

                    def link(ins, also=None):
                        nonlocal steps
                        if also is not None:
                            ins.then_inc(also, 1)
                            dve.wait_ge(also, 1)
                            return
                        steps += 1
                        ins.then_inc(chain, 1)
                        dve.wait_ge(chain, steps)

                    tt, ts, stt = dve.tensor_tensor, dve.tensor_scalar, dve.scalar_tensor_tensor
                    dve.wait_ge(rows_landed, 16)
                    link(tt(dt[:], raw[:, :, 2 * NS:2 * NS + MH], over_tiles(dt_bias, MH), ALU.add))
                    link(ts(q[:], dt[:], -1.0, None, ALU.mult))
                    link(tt(e[:], dt[:], q[:], ALU.max), abs_ready)
                    link(ts(dt[:], dt[:], 0.0, None, ALU.max))
                    bcr = raw[:, :, 0:2 * NS]
                    halves = bcr.rearrange("p t (a d) -> p t a d", a=2)
                    link(tt(bc[:], bcr, bcr, ALU.mult))
                    link(dve.tensor_reduce(ms[:], bc[:].rearrange("p t (a d) -> p t a d", a=2), AX.X, ALU.add))
                    link(ts(ms[:], ms[:], 1.0 / NS, RMS2_EPS, ALU.mult, ALU.add), ms_ready)
                    dve.wait_ge(neg_ready, 1)
                    link(ts(f[:], e[:], 2.0, None, ALU.add))
                    link(dve.reciprocal(f[:], f[:]))
                    link(tt(e[:], e[:], f[:], ALU.mult))
                    link(tt(q[:], e[:], e[:], ALU.mult))
                    link(ts(f[:], q[:], 1.0 / 17, None, ALU.mult))
                    for k in range(15, 1, -2):
                        link(stt(out=f[:], in0=f[:], scalar=1.0 / k, in1=q[:], op0=ALU.add, op1=ALU.mult))
                    link(stt(out=f[:], in0=f[:], scalar=1.0, in1=e[:], op0=ALU.add, op1=ALU.mult))
                    link(stt(out=dt[:], in0=f[:], scalar=2.0, in1=dt[:], op0=ALU.mult, op1=ALU.add))
                    dve.wait_ge(a_ready, 1)
                    link(ts(neg_a[:], neg_a[:], -1.0, None, ALU.mult))
                    link(tt(la[:], dt[:], over_tiles(neg_a[:], MH), ALU.mult))
                    link(dve.tensor_reduce(tmean[:], dt[:], AX.X, ALU.add))
                    link(stt(out=tmean[:], in0=tmean[:], scalar=1.0 / MH, in1=unscale[:], op0=ALU.mult, op1=ALU.mult))
                    link(tt(v, raw[:, :, PC:], tmean[:].unsqueeze(2).to_broadcast([P, TILES, TH]), ALU.mult))
                    v4 = v.rearrange("p (b t) d -> p b t d", t=CH)
                    link(dve.memset(vp[:, :, 0, :], 0.0))
                    for t in range(1, CH):
                        link(tt(vp[:, :, t, :], vp[:, :, t - 1, :], v4[:, :, t - 1, :], ALU.add))
                    dve.wait_ge(lam_ready, 1)
                    link(tt(weight[:], dt[:], lam[:], ALU.mult))
                    link(tt(w2[:], dt[:], weight[:], ALU.subtract), v_ready)
                    dve.wait_ge(rms_ready, 1)
                    bc4 = bc[:].rearrange("p t (a d) -> p t a d", a=2)
                    link(tt(bc4, halves, rms[:].unsqueeze(3).to_broadcast([P, TILES, 2, NS]), ALU.mult))
                    link(tt(bc[:], bc[:], over_tiles(rows[:, 0:2 * NS], 2 * NS), ALU.mult))
                    link(tt(bc[:], bc[:], over_tiles(rows[:, 2 * NS:4 * NS], 2 * NS), ALU.add))
                    dve.wait_ge(sums_ready, 1)
                    phase = pphi[:].rearrange("p a (t d) -> p (a t) d", d=TH)
                    link(dve.tensor_copy(phi[:, :, 0, :], phase))
                    link(ts(phi[:, :, 1, :], phi[:, :, 0, :], HALF_PI, None, ALU.add))
                    link(ts(turns[:], phi[:], 1.0 / TWO_PI, ROUND, ALU.mult, ALU.add))
                    link(ts(turns[:], turns[:], ROUND, None, ALU.subtract))
                    for part in (6.28125, 0.0019340515136718750, TWO_PI - 6.28125 - 0.0019340515136718750):
                        link(stt(out=phi[:], in0=turns[:], scalar=-part, in1=phi[:], op0=ALU.mult, op1=ALU.add))
                    link(ts(phi[:], phi[:], PI, -PI, ALU.min, ALU.max), angle_ready)
                    link(dve.tensor_copy(cum[:], pcum[:].rearrange("p (t h) -> p t h", h=MH)))
                    link(dve.tensor_copy(cparts[:, :, 0, :], cum[:]))
                    link(tt(f[:], cum[:], cparts[:, :, 0, :], ALU.subtract))
                    link(dve.tensor_copy(cparts[:, :, 1, :], f[:]))
                    link(tt(f[:], f[:], cparts[:, :, 1, :], ALU.subtract))
                    link(dve.tensor_copy(cparts[:, :, 2, :], f[:]), parts_ready)
                    link(dve.tensor_copy(ends[:], pend[:].rearrange("p (t h) -> p t h", h=MH)))
                    link(tt(to_end[:], ends[:], cum[:], ALU.subtract), cum_ready)
                    nxt = pshift[:].rearrange("p (t h) -> p t h", h=MH)
                    link(dve.tensor_copy(w2[:], nxt))
                    link(tt(weight[:], weight[:], w2[:], ALU.add))
                    dve.wait_ge(sin_ready, 1)
                    sine = phi[:, :, 0, :].unsqueeze(2).to_broadcast([P, TILES, 2, TH])
                    cosine = phi[:, :, 1, :].unsqueeze(2).to_broadcast([P, TILES, 2, TH])
                    re, im = bc4[:, :, :, 0:TH], bc4[:, :, :, TH:NS]
                    link(tt(big, im, sine, ALU.mult))
                    link(tt(big2[:], re, sine, ALU.mult))
                    link(tt(re, re, cosine, ALU.mult))
                    link(tt(im, im, cosine, ALU.mult))
                    link(tt(re, re, big, ALU.subtract))
                    link(tt(im, im, big2[:], ALU.add))
                    dot = big.rearrange("p t a d -> p t (a d)")
                    link(tt(dot, bc[:, :, 0:NS], bc[:, :, NS:2 * NS], ALU.mult))
                    link(dve.tensor_reduce(gd[:], dot, AX.X, ALU.add))
                    link(tt(w2[:], w2[:], gd[:].unsqueeze(2).to_broadcast([P, TILES, MH]), ALU.mult))
                    link(tt(skip[:], over_tiles(d_row, MH), w2[:], ALU.subtract))
                    dve.wait_ge(gr_ready, 3)
                    link(tt(to_end[:], to_end[:], weight[:], ALU.mult))
            r.clear()
        rctx.close()

        with ExitStack() as sctx:
            r = Space(nc, sctx, "mamba_scan")
            wout = r.sb("wout", [P, CH, D])
            zg = r.sb("zg", [P, 2, 2, MI])
            bcs = r.sb("bcs", [P, 2, 2 * NS])
            bcT = r.sb("bcT", [NS, 2, 2, P])
            cneg = r.sb("cneg", [3 * MH, 2, P], BF16)
            decay = r.sb("decay", [P, MH, P])
            mat = r.sb("mat", [P, MH, P])
            gsb = r.sb("gsb", [P, 2, P])
            xw = r.sb("xw", [P, 2, MH, HP])
            xe = r.sb("xe", [P, 2, MH, HP])
            xd = r.sb("xd", [P, 2, MH, HP])
            state = r.sb("state", [NS, MH, HP])
            y = r.sb("y", [P, 2, MH, HP])
            yT = r.sb("yT", [P, MI // P, P])
            un = r.sb("un", [P, D])
            p_la = r.ps("p_la", [P, MH, P])
            p_y = r.ps("p_y", [P, 512])
            p_in = r.ps("p_in", [P, 512])
            p_st = r.ps("p_st", [P, 512])
            p_m = r.ps("p_m", [P, 512])
            wout_landed = r.sem("wout_landed")
            zg_landed, zg_free = r.sems("zg_landed", 2), r.sems("zg_free", 2)
            xe_ready, xw_ready, xd_ready = r.sem("xe_ready"), r.sem("xw_ready"), r.sem("xd_ready")
            copies_ready = r.sem("copies_ready")
            sum_psum, exp_ready = r.sem("sum_psum"), r.sem("exp_ready")
            bcT_psum, bcT_ready, g_psum, g_ready = r.sem("bcT_psum"), r.sem("bcT_ready"), r.sem("g_psum"), r.sem("g_ready")
            mat_ready, in_psum, intra_psum = r.sem("mat_ready"), r.sem("in_psum"), r.sem("intra_psum")
            st_psum = r.sem("st_psum")
            state_ready = r.sem("state_ready")
            grown_ready, scaled_ready, skip_ready = r.sem("grown_ready"), r.sem("scaled_ready"), r.sem("skip_ready")
            added_ready = r.sem("added_ready")
            y_ready = r.sem("y_ready")
            yT_psum, yT_ready, out_psum = r.sem("yT_psum"), r.sem("yT_ready"), r.sem("out_psum")
            un_ready, res_ready = r.sem("un_ready"), r.sem("res_ready")
            out_ready = r.sem("out_ready")

            halves = [slice(0, MH // 2), slice(MH // 2, MH)]

            def of(tensor, k):
                return tensor[:, bass.ds(k, 1), :].rearrange("p o h -> p (o h)")

            def over_chunks(eng, step):
                with eng.Fori(0, BATCH - 1) as n:
                    for t in range(CH):
                        step(n, t, CH * n + t, CH)
                for t in range(CH):
                    step(BATCH - 1, t, CH * (BATCH - 1) + t, CH - 1 - t)

            with nc.Block() as block:

                @block.sync
                def _(sp):
                    zg_in = gz_dram.rearrange("(g t p) d -> g p t d", t=CH, p=P)
                    sp.dma_start(wout[:], wout_dram).then_inc(wout_landed, 16)
                    with sp.Fori(0, BATCH) as n:
                        for b in range(2):
                            wait_at(sp, zg_free[b], n + 1, ready)
                            sp.dma_start(zg[:, b], zg_in[bass.ds(n, 1), :, 2 * b:2 * b + 2].rearrange("g p t d -> p (g t) d")
                                         ).then_inc(zg_landed[b], 16)

                @block.gpsimd
                def _(pool):
                    with pool.Fori(0, TILES // 2) as i:
                        for v in range(2):
                            k = 2 * i + v
                            wait_at(pool, y_ready, k + 1, ready)
                            x = xs[:, bass.ds(k, 1), :].rearrange("p o (h d) -> p (o h) d", h=MH)
                            for out, by, count in ((xe, to_end, xe_ready), (xw, weight, xw_ready), (xd, skip, xd_ready)):
                                pool.tensor_tensor(out[:, v], x, of(by, k).unsqueeze(2).to_broadcast([P, MH, HP]), ALU.mult
                                                   ).then_inc(count, 1)

                @block.scalar
                def _(act):
                    def copies(k, v):
                        wait_at(act, st_psum, k, ready)
                        act.activation(bcs[:, v], of(bc, k), ACT.Copy)
                        act.activation(cneg[:, v], of(cumT, k), ACT.Copy, scale=-1.0).then_inc(copies_ready, 1)

                    def turned(k, v):
                        wait_at(act, bcT_psum, k + 1, ready)
                        act.activation(bcT[:, v], p_m[0:NS, 0:2 * P].rearrange("p (a n) -> p a n", a=2), ACT.Copy
                                       ).then_inc(bcT_ready, 1)
                        wait_at(act, g_psum, k + 1, ready)
                        act.activation(gsb[:, v], p_in[:, 0:P], ACT.Copy).then_inc(g_ready, 1)

                    def decays(k):
                        for a in range(2):
                            wait_at(act, sum_psum, 2 * k + (a + 1), ready)
                            if not isinstance(k, int) or k:
                                wait_at(act, mat_ready, 2 * k + (a - 1), ready)
                            act.activation(decay[:, halves[a]], p_la[:, halves[a]], ACT.Exp).then_inc(exp_ready, 1)

                    def step(n, t, k, more):
                        v, v1 = t % 2, (t + 1) % 2
                        if more:
                            turned(k + 1, v1)
                            decays(k + 1)
                        wait_at(act, yT_psum, k + 1, ready)
                        act.activation(yT[:], p_y[:].rearrange("p (a n) -> p a n", n=P), ACT.Copy).then_inc(yT_ready, 1)
                        if more > 1:
                            copies(k + 2, v)

                    act.activation(bcs[:, 0], of(bc, 0), ACT.Copy)
                    act.activation(cneg[:, 0], of(cumT, 0), ACT.Copy, scale=-1.0).then_inc(copies_ready, 1)
                    copies(1, 1)
                    turned(0, 0)
                    decays(0)
                    over_chunks(act, step)

                @block.tensor
                def _(pe):
                    def differences(k, v, a):
                        wait_at(pe, copies_ready, k + 1, ready)
                        if not isinstance(k, int) or k:
                            wait_at(pe, exp_ready, 2 * k + (a - 1), ready)
                        for b in range(2 * a, 2 * a + 2):
                            heads = slice(4 * b, 4 * b + 4)
                            pe.matmul(p_la[:, heads, :], cneg[:, v], const.pick[:, heads, :], start=True, stop=False,
                                      skip_group_check=True)
                            for h in range(4 * b, 4 * b + 4):
                                pe.matmul(p_la[:, h, :], const.pick[:, h, :], of(cumT, k), start=False, stop=False,
                                          skip_group_check=True)
                            last = pe.matmul(p_la[:, heads, :], const.ident_b[:],
                                             const.never[:].unsqueeze(1).to_broadcast([P, 4, P]), start=False, stop=True,
                                             skip_group_check=True)
                        last.then_inc(sum_psum, 1)

                    def turn(k, v):
                        wait_at(pe, copies_ready, k + 1, ready)
                        wait_at(pe, out_ready, k, ready)
                        for a in range(2):
                            last = pe.transpose(p_m[0:NS, a * P:(a + 1) * P], bcs[:, v, a * NS:(a + 1) * NS], const.ident[:])
                        last.then_inc(bcT_psum, 1)

                    def products(k, v):
                        wait_at(pe, bcT_ready, k + 1, ready)
                        if not isinstance(k, int) or k:
                            wait_at(pe, scaled_ready, k, ready)
                        pe.matmul(p_in[:, 0:P], bcT[:, v, 0, :], bcT[:, v, 1, :], start=True, stop=True).then_inc(g_psum, 1)

                    def through_state(k, v):
                        wait_at(pe, state_ready, k + 1, ready)
                        wait_at(pe, g_ready, k + 1, ready)
                        pe.matmul(p_in[:], bcT[:, v, 1, :], state[:].rearrange("p h d -> p (h d)"), start=True, stop=True
                                  ).then_inc(in_psum, 1)
                        wait_at(pe, xe_ready, k + 1, ready)
                        pe.matmul(p_st[0:NS, :], bcs[:, v, 0:NS], xe[:, v].rearrange("p h d -> p (h d)"), start=True, stop=True
                                  ).then_inc(st_psum, 1)

                    def step(n, t, k, more):
                        v, v1 = t % 2, (t + 1) % 2
                        wait_at(pe, xw_ready, k + 1, ready)
                        wait_at(pe, mat_ready, 2 * k + 2, ready)
                        for h in range(MH):
                            last = pe.matmul(p_y[:, h * HP:(h + 1) * HP], mat[:, h, :], xw[:, v, h, :], start=True, stop=True)
                        last.then_inc(intra_psum, 1)
                        if more:
                            turn(k + 1, v1)
                            differences(k + 1, v1, 0)
                            products(k + 1, v1)
                            differences(k + 1, v1, 1)
                        wait_at(pe, y_ready, k + 3, ready)
                        for a in range(MI // P):
                            last = pe.transpose(p_y[:, a * P:(a + 1) * P],
                                                y[:, v, a * (P // HP):(a + 1) * (P // HP), :].rearrange("p h d -> p (h d)"),
                                                const.ident[:])
                        last.then_inc(yT_psum, 1)
                        if more:
                            through_state(k + 1, v1)
                        wait_at(pe, yT_ready, k + 1, ready)
                        for a in range(MI // P):
                            last = pe.matmul(p_m[:, 0:D], yT[:, a, :], wout[:, a, :], start=(a == 0), stop=(a == MI // P - 1))
                        last.then_inc(out_psum, 1)

                    pe.sem_inc(st_psum, 1)
                    pe.wait_ge(wout_landed, 16)
                    differences(0, 0, 0)
                    differences(0, 0, 1)
                    for a in range(2):
                        last = pe.transpose(p_m[0:NS, a * P:(a + 1) * P], bcs[:, 0, a * NS:(a + 1) * NS], const.ident[:])
                    last.then_inc(bcT_psum, 1)
                    products(0, 0)
                    through_state(0, 0)
                    over_chunks(pe, step)

                @block.vector
                def _(dve):
                    tt, ts = dve.tensor_tensor, dve.tensor_scalar

                    def decayed(k, v):
                        wait_at(dve, g_ready, k + 1, ready)
                        for a in range(2):
                            wait_at(dve, exp_ready, 2 * k + (a + 1), ready)
                            tt(mat[:, halves[a]], decay[:, halves[a]], gsb[:, v].unsqueeze(1).to_broadcast([P, MH // 2, P]),
                               ALU.mult).then_inc(mat_ready, 1)

                    def step(n, t, k, more):
                        v, v1 = t % 2, (t + 1) % 2
                        x = x_all[:].rearrange("p g t d -> p (g t) d")[:, bass.ds(k, 1), :].rearrange("p o d -> p (o d)")
                        ts(un[:], x, mean1[:, bass.ds(k, 1)], root1[:, bass.ds(k, 1)], ALU.subtract, ALU.mult
                           ).then_inc(un_ready, 1)
                        wait_at(dve, in_psum, k + 1, ready)
                        tt(y[:, v], p_in[:].rearrange("p (h d) -> p h d", h=MH),
                           of(grown, k).unsqueeze(2).to_broadcast([P, MH, HP]), ALU.mult).then_inc(scaled_ready, 1)
                        wait_at(dve, st_psum, k + 2, ready)
                        if t < CH - 1:
                            tt(state[:], state[:], across[0:NS, bass.ds(k, 1), :].rearrange("p o h -> p (o h)")
                               .unsqueeze(2).to_broadcast([NS, MH, HP]), ALU.mult).then_inc(grown_ready, 1)
                            wait_at(dve, un_ready, k + 1, ready)
                            tt(x, x, un[:], ALU.add).then_inc(res_ready, 1)
                            wait_at(dve, grown_ready, (CH - 1) * n + (t + 1), ready)
                            tt(state[:], state[:], p_st[0:NS, :].rearrange("p (h d) -> p h d", h=MH), ALU.add
                               ).then_inc(state_ready, 1)
                        else:
                            dve.memset(state[:], 0.0).then_inc(state_ready, 1)
                            wait_at(dve, un_ready, k + 1, ready)
                            tt(x, x, un[:], ALU.add).then_inc(res_ready, 1)
                        wait_at(dve, xd_ready, k + 1, ready)
                        wait_at(dve, scaled_ready, k + 1, ready)
                        tt(y[:, v], y[:, v], xd[:, v], ALU.add).then_inc(skip_ready, 1)
                        wait_at(dve, skip_ready, k + 1, ready)
                        wait_at(dve, intra_psum, k + 1, ready)
                        tt(y[:, v], y[:, v], p_y[:].rearrange("p (h d) -> p h d", h=MH), ALU.add).then_inc(added_ready, 1)
                        wait_at(dve, added_ready, k + 1, ready)
                        if v == 0:
                            wait_at(dve, zg_landed[t // 2], 16 * n + 16, ready)
                        tt(y[:, v], y[:, v], zg[:, t // 2, v].rearrange("p (h d) -> p h d", h=MH), ALU.mult
                           ).then_inc(y_ready, 1)
                        if more:
                            decayed(k + 1, v1)
                        wait_at(dve, out_psum, k + 1, ready)
                        if v:
                            dve.sem_inc(zg_free[t // 2], 1)
                        wait_at(dve, res_ready, k + 1, ready)
                        tt(x, x, p_m[:, 0:D], ALU.add).then_inc(out_ready, 1)

                    dve.sem_inc(y_ready, 2)
                    dve.sem_inc(out_ready, 1)
                    dve.sem_inc(zg_free[0], 1)
                    dve.sem_inc(zg_free[1], 1)
                    dve.memset(state[:], 0.0).then_inc(state_ready, 1)
                    decayed(0, 0)
                    over_chunks(dve, step)

            r.clear()
        s.clear()


def build(nc, a, out):
    def dram(name, width):
        return nc.dram_tensor(name, (TOKENS, width), F32, kind="Internal").ap()

    x1, x2, xn, gz = dram("x1", D), dram("x2", D), dram("xn", D), dram("gz", MI)
    with ExitStack() as ctx:
        const = Constants(nc, ctx)
        lasting = Space(nc, ctx, "all")
        x_all = lasting.sb("x", [P, GROUPS, GT, D])
        experts = (a["router"], a["w1"], a["b1"], a["w2"], a["b2"])
        mixer = (a["rwkv_r"], a["rwkv_k"], a["rwkv_v"], a["mu"])
        moe_stage(nc, lasting, const, "moe_a", True, x_all, a["x"], x1, xn, *experts)
        attention_stage(nc, const, x_all, x1, x2, a["wqkv"], a["wo"], a["attn_norm"], a["gamma"])
        moe_stage(nc, lasting, const, "moe_b", False, x_all, None, x2, xn, *experts)
        rwkv_stage(nc, const, "rwkv_a", True, x_all, x2, None, *mixer)
        mamba_stage(nc, const, x_all, gz, a["in_proj"], a["theta"], a["out_proj"], a["mamba_norm"], a["rows"])
        rwkv_stage(nc, const, "rwkv_b", False, x_all, None, out, *mixer)


def kernel(**inputs):
    import numpy as np
    import concourse.bacc as bacc
    from concourse.bass_utils import run_bass_kernel_spmd

    a = {k: np.asarray(v) for k, v in inputs.items()}
    L0, F0, L1, F1 = "L0_attn_", "L0_ffn_", "L1_attn_", "L1_ffn_"

    def by_chunk(w):
        return w.reshape(w.shape[0] // P, P, -1).transpose(1, 0, 2)

    def columns(*vectors):
        return np.stack(vectors).reshape(len(vectors), -1, P).transpose(2, 0, 1)

    E, S, M, K = EXPERTS, SLOTS, HID, YK
    layout = {
        "x": a[L0 + "tokens"].reshape(TOKENS, D),
        "router": by_chunk(a[F0 + "Wr"].T),
        "w1": a[F0 + "W1"].reshape(E, S, KC, P, M).transpose(0, 3, 2, 1, 4).reshape(E, P, KC, S * M),
        "b1": a[F0 + "b1"].reshape(E, HC, P).transpose(2, 0, 1),
        "w2": a[F0 + "W2"].reshape(E, HC, P, K).transpose(0, 2, 1, 3),
        "b2": a[F0 + "b2"].reshape(E, D),
        "wqkv": by_chunk(np.concatenate([a[L0 + "Wq"], a[L0 + "Wkv"]], 1)),
        "wo": by_chunk(a[L0 + "Wo"]),
        "attn_norm": columns(a[L0 + "norm_w"])[:, 0],
        "gamma": columns(a[L0 + "q_gamma"], a[L0 + "k_gamma"]),
        "rwkv_r": by_chunk(a[F1 + "W_r"].T),
        "rwkv_k": by_chunk(a[F1 + "W_k"].T),
        "rwkv_v": by_chunk(a[F1 + "W_v"].T),
        "mu": columns(a[F1 + "mu_r"], a[F1 + "mu_k"]),
        "in_proj": by_chunk(a[L1 + "in_proj_w"]),
        "theta": by_chunk(a[L1 + "theta_w"]),
        "out_proj": by_chunk(a[L1 + "out_proj_w"]),
        "mamba_norm": columns(a[L1 + "norm_scale"], a[L1 + "norm_bias"]),
        "rows": np.concatenate([a[L1 + n] for n in ("bcB_scale", "bcC_scale", "B_bias", "C_bias", "dt_bias", "A_log", "D")]),
    }
    nc = bacc.Bacc("TRN2", target_bir_lowering=False, num_devices=1)
    arrays, aps = {}, {}
    for name, value in layout.items():
        arrays["in_" + name] = np.ascontiguousarray(value)
        aps[name] = nc.dram_tensor("in_" + name, value.shape, mybir.dt.from_np(value.dtype), kind="ExternalInput").ap()
    out = nc.dram_tensor("out", (TOKENS, D), F32, kind="ExternalOutput").ap()
    build(nc, aps, out)
    result = run_bass_kernel_spmd(nc, [arrays], core_ids=[0])
    return result.results[0]["out"].reshape(BATCH, SEQ, D)
```
